# Optimizing a Trainium2 kernel written in Bass

```python
import numpy as np
import jax
import jax.numpy as jnp

def _softmax(x, axis=-1):
    return jax.nn.softmax(x, axis=axis)

def _gelu(x):
    return jax.nn.gelu(x, approximate=True)

def _silu(x):
    return jax.nn.silu(x)

def _sigmoid(x):
    return jax.nn.sigmoid(x)

def _layernorm(x, axis=-1, eps=1e-05):
    m = jnp.mean(x, axis=axis, keepdims=True)
    v = jnp.var(x, axis=axis, keepdims=True)
    return (x - m) / jnp.sqrt(v + eps)

def _scatter_add(tgt, idx, src, axis=0):
    return tgt.at[idx].add(src)

def _segment_sum(src, seg, n):
    return jax.ops.segment_sum(src, seg, n)
kernel_name = 'mk_decoder_postln_d2_seqx_r4_6b3a0f'

def setup_inputs(seed: int=0):
    np.random.seed(seed)
    _w = jnp.asarray

    def _rec_inputs():
        import jax
        import jax.numpy as jnp
        _rk = jax.random.key(seed)
        x = 0.0002417 + 0.9998 * jax.random.normal(jax.random.fold_in(_rk, 1), (16, 512, 256), jnp.float32)
        _lenS = 512 - jax.random.randint(jax.random.fold_in(_rk, 7), (16,), 0, max(1, 512 // 4) + 1, jnp.int32)
        _lenS2 = 64 - jax.random.randint(jax.random.fold_in(_rk, 8), (16,), 0, max(1, 64 // 4) + 1, jnp.int32)
        _ctx_1024P = jax.random.normal(jax.random.fold_in(_rk, 11), (16, 16, 256), jnp.float32)
        _ctx_1024c = jax.random.dirichlet(jax.random.fold_in(_rk, 511), 0.3 * jnp.ones((16,), jnp.float32), (16, 64))
        _ctx_1024t = jnp.einsum('bsk,bkd->bsd', _ctx_1024c, _ctx_1024P)
        _ctx_1024t = _ctx_1024t * jax.lax.rsqrt(jnp.mean(jnp.square(_ctx_1024t)) + 1e-12) * 0.953939
        ctx_1024 = 7.22013e-05 + 1.00017 * (_ctx_1024t + 0.3 * jax.random.normal(jax.random.fold_in(_rk, 611), (16, 64, 256), jnp.float32))
        _validS = jnp.arange(512)[None, :] < _lenS[:, None]
        _validS2 = jnp.arange(64)[None, :] < _lenS2[:, None]
        _causal = jnp.tril(jnp.ones((512, 512), dtype=bool))
        mask_1x1xSxS2_fk1 = jnp.where(jnp.broadcast_to(_validS2[0:1, None, None, :], (1, 1, 512, 64)), 1.0, 0.0).astype(jnp.float32)
        mask_BxS2_ik0 = jnp.where(jnp.broadcast_to(_validS2[:, :], (16, 64)), 0, 1).astype(jnp.int32)
        return (x, ctx_1024, mask_1x1xSxS2_fk1, mask_BxS2_ik0)
    x, ctx_1024, mask_1x1xSxS2_fk1, mask_BxS2_ik0 = _rec_inputs()

    def _L0_attn_setup():
        import jax, jax.numpy as jnp
        import numpy as np
        import math
        D_MODEL = 256
        N_HEADS = 16
        HEAD_DIM = D_MODEL // N_HEADS
        R = HEAD_DIM // 2
        ROPE_BASE = 10000.0
        B, T = (4, 512)

        def _fourier_bias(alpha, beta, t):
            omega = ROPE_BASE ** (-2.0 * jnp.arange(R, dtype=jnp.float32) / HEAD_DIM)
            disp = jnp.arange(-(t - 1), t, dtype=jnp.float32)
            angles = omega[:, None] * disp[None, :]
            vec = jnp.einsum('hr,rk->hk', alpha, jnp.cos(angles)) + jnp.einsum('hr,rk->hk', beta, jnp.sin(angles))
            i = jnp.arange(t)
            idx = i[:, None] - i[None, :] + (t - 1)
            return vec[:, idx]
        key = jax.random.key(seed)
        k1, k2, k3, k4, k5 = jax.random.split(key, 5)
        x = jax.random.normal(k1, (B, T, D_MODEL), dtype=jnp.float32)
        Wqkv = jax.random.normal(k2, (3 * D_MODEL, D_MODEL), dtype=jnp.float32) * (1.0 / math.sqrt(D_MODEL))
        Wout = jax.random.normal(k3, (D_MODEL, D_MODEL), dtype=jnp.float32) * (1.0 / math.sqrt(D_MODEL))
        alpha = jax.random.normal(k4, (N_HEADS, R), dtype=jnp.float32) * 0.01
        beta = jax.random.normal(k5, (N_HEADS, R), dtype=jnp.float32) * 0.01
        return {'x': x, 'Wqkv': Wqkv, 'Wout': Wout, 'alpha': alpha, 'beta': beta}
    _L0_attn_all = _L0_attn_setup()
    _L0_attn_in = {k: v for k, v in _L0_attn_all.items() if k in ('Wqkv', 'Wout', 'alpha', 'beta')}
    del _L0_attn_all

    def _L0_xattn_setup():
        import jax, jax.numpy as jnp
        import numpy as np
        D_MODEL = 256
        NUM_HEADS = 16
        DEPTH = D_MODEL // NUM_HEADS
        B, S = (4, 512)

        def _split_heads(x):
            b, s, _ = x.shape
            return x.reshape(b, s, NUM_HEADS, DEPTH).transpose(0, 2, 1, 3)
        key = jax.random.key(seed)
        ks = jax.random.split(key, 12)
        sd = 1.0 / np.sqrt(D_MODEL)
        inp = {'v': jax.random.normal(ks[0], (B, S, D_MODEL), jnp.float32), 'k': jax.random.normal(ks[1], (B, S, D_MODEL), jnp.float32), 'q': jax.random.normal(ks[2], (B, S, D_MODEL), jnp.float32), 'mask': jnp.triu(jnp.ones((S, S), jnp.float32), k=1)[None, None, :, :], 'wq_w': jax.random.normal(ks[3], (D_MODEL, D_MODEL), jnp.float32) * sd, 'wq_b': jnp.zeros((D_MODEL,), jnp.float32), 'wk_w': jax.random.normal(ks[4], (D_MODEL, D_MODEL), jnp.float32) * sd, 'wk_b': jnp.zeros((D_MODEL,), jnp.float32), 'wv_w': jax.random.normal(ks[5], (D_MODEL, D_MODEL), jnp.float32) * sd, 'wv_b': jnp.zeros((D_MODEL,), jnp.float32), 'wo_w': jax.random.normal(ks[6], (D_MODEL, D_MODEL), jnp.float32) * sd, 'wo_b': jnp.zeros((D_MODEL,), jnp.float32)}
        return inp
    _L0_xattn_all = _L0_xattn_setup()
    _L0_xattn_in = {k: v for k, v in _L0_xattn_all.items() if k in ('wq_w', 'wq_b', 'wk_w', 'wk_b', 'wv_w', 'wv_b', 'wo_w', 'wo_b')}
    del _L0_xattn_all

    def _L0_ffn_setup():
        import jax, jax.numpy as jnp
        import numpy as np
        BEST_K = 2

        def _expert(xf, w1, w3, w2):
            return jax.nn.silu(xf @ w1) * (xf @ w3) @ w2
        key = jax.random.key(seed)
        ks = jax.random.split(key, 9)
        E, S_sh, D, H = (8, 2, 256, 128)
        B, S = (2, 512)
        w = lambda k, shape: jax.random.normal(k, shape, dtype=jnp.float32) * 0.02
        return {'x': jax.random.normal(ks[0], (B, S, D), dtype=jnp.float32), 'router_w': w(ks[1], (D, E)), 'router_b': jnp.zeros((E,), dtype=jnp.float32), 'routed_w1': w(ks[2], (E, D, H)), 'routed_w3': w(ks[3], (E, D, H)), 'routed_w2': w(ks[4], (E, H, D)), 'shared_w1': w(ks[5], (S_sh, D, H)), 'shared_w3': w(ks[6], (S_sh, D, H)), 'shared_w2': w(ks[7], (S_sh, H, D))}
    _L0_ffn_all = _L0_ffn_setup()
    _L0_ffn_in = {k: v for k, v in _L0_ffn_all.items() if k in ('router_w', 'router_b', 'routed_w1', 'routed_w3', 'routed_w2', 'shared_w1', 'shared_w3', 'shared_w2')}
    del _L0_ffn_all

    def _L1_attn_setup():
        import jax, jax.numpy as jnp
        import numpy as np
        B, T, C = (2, 512, 256)
        LAT = 64
        N_HEAD = 16
        HEAD_DIM = C // N_HEAD
        SCALE = 1.0 / np.sqrt(HEAD_DIM).astype(np.float32)
        key = jax.random.key(seed)
        ks = jax.random.split(key, 9)
        s_in = 0.02
        return {'x': jax.random.normal(ks[0], (B, T, C), dtype=jnp.float32), 'wq_lat': jax.random.normal(ks[1], (C, LAT), dtype=jnp.float32) * s_in, 'wk_lat': jax.random.normal(ks[2], (C, LAT), dtype=jnp.float32) * s_in, 'wv_lat': jax.random.normal(ks[3], (C, LAT), dtype=jnp.float32) * s_in, 'wq_heads': jax.random.normal(ks[4], (LAT, C), dtype=jnp.float32) * s_in, 'wk_heads': jax.random.normal(ks[5], (LAT, C), dtype=jnp.float32) * s_in, 'wv_heads': jax.random.normal(ks[6], (LAT, C), dtype=jnp.float32) * s_in, 'w_proj': jax.random.normal(ks[7], (C, C), dtype=jnp.float32) * s_in, 'b_proj': jnp.zeros((C,), dtype=jnp.float32)}
    _L1_attn_all = _L1_attn_setup()
    _L1_attn_in = {k: v for k, v in _L1_attn_all.items() if k in ('wq_lat', 'wk_lat', 'wv_lat', 'wq_heads', 'wk_heads', 'wv_heads', 'w_proj', 'b_proj')}
    del _L1_attn_all

    def _L1_xattn_setup():
        import jax, jax.numpy as jnp
        import numpy as np
        B, LQ, LK = (8, 512, 512)
        QD = KD = VD = HD = 256
        key = jax.random.key(seed)
        ks = jax.random.split(key, 12)
        s = lambda d: 1.0 / np.sqrt(d)
        return {'q': jax.random.normal(ks[0], (B, LQ, QD), jnp.float32), 'k': jax.random.normal(ks[1], (B, LK, KD), jnp.float32), 'mask': jax.random.randint(ks[2], (B, LK), 0, 2, jnp.int32), 'Wq': jax.random.normal(ks[3], (QD, HD), jnp.float32) * s(QD), 'bq': jax.random.normal(ks[4], (HD,), jnp.float32) * 0.02, 'Wk': jax.random.normal(ks[5], (KD, HD), jnp.float32) * s(KD), 'bk': jax.random.normal(ks[6], (HD,), jnp.float32) * 0.02, 'Wv': jax.random.normal(ks[7], (VD, HD), jnp.float32) * s(VD), 'bv': jax.random.normal(ks[8], (HD,), jnp.float32) * 0.02, 'Wo': jax.random.normal(ks[9], (HD, VD), jnp.float32) * s(HD), 'bo': jax.random.normal(ks[10], (VD,), jnp.float32) * 0.02}
    _L1_xattn_all = _L1_xattn_setup()
    _L1_xattn_in = {k: v for k, v in _L1_xattn_all.items() if k in ('Wq', 'bq', 'Wk', 'bk', 'Wv', 'bv', 'Wo', 'bo')}
    del _L1_xattn_all

    def _L1_ffn_setup():
        import jax, jax.numpy as jnp
        import numpy as np
        B, S, D_MODEL, D_FF = (4, 512, 256, 1024)

        def _quantum_transform(hidden, theta, w_real, w_imag):
            imag = w_imag * jnp.sin(theta + hidden * 0.1)
            quantum_phase = jnp.cos(theta) * w_real + jnp.sin(theta) * w_imag
            return hidden + quantum_phase * imag * 0.1
        key = jax.random.key(seed)
        ks = jax.random.split(key, 8)
        return {'x': jax.random.normal(ks[0], (B, S, D_MODEL), dtype=jnp.float32), 'W1': jax.random.normal(ks[1], (D_MODEL, D_FF), dtype=jnp.float32) * (1.0 / np.sqrt(D_MODEL)), 'b1': jnp.zeros((D_FF,), dtype=jnp.float32), 'quantum_phases': jax.random.normal(ks[2], (D_FF,), dtype=jnp.float32) * (2.0 * np.pi), 'quantum_weights_real': jax.random.normal(ks[3], (D_FF,), dtype=jnp.float32) * 0.1, 'quantum_weights_imag': jax.random.normal(ks[4], (D_FF,), dtype=jnp.float32) * 0.1, 'W2': jax.random.normal(ks[5], (D_FF, D_MODEL), dtype=jnp.float32) * (1.0 / np.sqrt(D_FF)), 'b2': jnp.zeros((D_MODEL,), dtype=jnp.float32)}
    _L1_ffn_all = _L1_ffn_setup()
    _L1_ffn_in = {k: v for k, v in _L1_ffn_all.items() if k in ('W1', 'b1', 'quantum_phases', 'quantum_weights_real', 'quantum_weights_imag', 'W2', 'b2')}
    del _L1_ffn_all
    return {'x': x, 'ctx_1024': ctx_1024, 'mask_1x1xSxS2_fk1': mask_1x1xSxS2_fk1, 'mask_BxS2_ik0': mask_BxS2_ik0, 'L0_attn_Wqkv': _L0_attn_in['Wqkv'], 'L0_attn_Wout': _L0_attn_in['Wout'], 'L0_attn_alpha': _L0_attn_in['alpha'], 'L0_attn_beta': _L0_attn_in['beta'], 'L0_xattn_wq_w': _L0_xattn_in['wq_w'], 'L0_xattn_wq_b': _L0_xattn_in['wq_b'], 'L0_xattn_wk_w': _L0_xattn_in['wk_w'], 'L0_xattn_wk_b': _L0_xattn_in['wk_b'], 'L0_xattn_wv_w': _L0_xattn_in['wv_w'], 'L0_xattn_wv_b': _L0_xattn_in['wv_b'], 'L0_xattn_wo_w': _L0_xattn_in['wo_w'], 'L0_xattn_wo_b': _L0_xattn_in['wo_b'], 'L0_ffn_router_w': _L0_ffn_in['router_w'], 'L0_ffn_router_b': _L0_ffn_in['router_b'], 'L0_ffn_routed_w1': _L0_ffn_in['routed_w1'], 'L0_ffn_routed_w3': _L0_ffn_in['routed_w3'], 'L0_ffn_routed_w2': _L0_ffn_in['routed_w2'], 'L0_ffn_shared_w1': _L0_ffn_in['shared_w1'], 'L0_ffn_shared_w3': _L0_ffn_in['shared_w3'], 'L0_ffn_shared_w2': _L0_ffn_in['shared_w2'], 'L1_attn_wq_lat': _L1_attn_in['wq_lat'], 'L1_attn_wk_lat': _L1_attn_in['wk_lat'], 'L1_attn_wv_lat': _L1_attn_in['wv_lat'], 'L1_attn_wq_heads': _L1_attn_in['wq_heads'], 'L1_attn_wk_heads': _L1_attn_in['wk_heads'], 'L1_attn_wv_heads': _L1_attn_in['wv_heads'], 'L1_attn_w_proj': _L1_attn_in['w_proj'], 'L1_attn_b_proj': _L1_attn_in['b_proj'], 'L1_xattn_Wq': _L1_xattn_in['Wq'], 'L1_xattn_bq': _L1_xattn_in['bq'], 'L1_xattn_Wk': _L1_xattn_in['Wk'], 'L1_xattn_bk': _L1_xattn_in['bk'], 'L1_xattn_Wv': _L1_xattn_in['Wv'], 'L1_xattn_bv': _L1_xattn_in['bv'], 'L1_xattn_Wo': _L1_xattn_in['Wo'], 'L1_xattn_bo': _L1_xattn_in['bo'], 'L1_ffn_W1': _L1_ffn_in['W1'], 'L1_ffn_b1': _L1_ffn_in['b1'], 'L1_ffn_quantum_phases': _L1_ffn_in['quantum_phases'], 'L1_ffn_quantum_weights_real': _L1_ffn_in['quantum_weights_real'], 'L1_ffn_quantum_weights_imag': _L1_ffn_in['quantum_weights_imag'], 'L1_ffn_W2': _L1_ffn_in['W2'], 'L1_ffn_b2': _L1_ffn_in['b2']}

def reference(x, ctx_1024, mask_1x1xSxS2_fk1, mask_BxS2_ik0, L0_attn_Wqkv, L0_attn_Wout, L0_attn_alpha, L0_attn_beta, L0_xattn_wq_w, L0_xattn_wq_b, L0_xattn_wk_w, L0_xattn_wk_b, L0_xattn_wv_w, L0_xattn_wv_b, L0_xattn_wo_w, L0_xattn_wo_b, L0_ffn_router_w, L0_ffn_router_b, L0_ffn_routed_w1, L0_ffn_routed_w3, L0_ffn_routed_w2, L0_ffn_shared_w1, L0_ffn_shared_w3, L0_ffn_shared_w2, L1_attn_wq_lat, L1_attn_wk_lat, L1_attn_wv_lat, L1_attn_wq_heads, L1_attn_wk_heads, L1_attn_wv_heads, L1_attn_w_proj, L1_attn_b_proj, L1_xattn_Wq, L1_xattn_bq, L1_xattn_Wk, L1_xattn_bk, L1_xattn_Wv, L1_xattn_bv, L1_xattn_Wo, L1_xattn_bo, L1_ffn_W1, L1_ffn_b1, L1_ffn_quantum_phases, L1_ffn_quantum_weights_real, L1_ffn_quantum_weights_imag, L1_ffn_W2, L1_ffn_b2):
    import jax
    import jax.numpy as jnp

    def _L0_attn_ref(x, Wqkv, Wout, alpha, beta):
        import jax, jax.numpy as jnp
        import numpy as np
        import math
        D_MODEL = 256
        N_HEADS = 16
        HEAD_DIM = D_MODEL // N_HEADS
        R = HEAD_DIM // 2
        ROPE_BASE = 10000.0
        B, T = (4, 512)

        def _fourier_bias(alpha, beta, t):
            omega = ROPE_BASE ** (-2.0 * jnp.arange(R, dtype=jnp.float32) / HEAD_DIM)
            disp = jnp.arange(-(t - 1), t, dtype=jnp.float32)
            angles = omega[:, None] * disp[None, :]
            vec = jnp.einsum('hr,rk->hk', alpha, jnp.cos(angles)) + jnp.einsum('hr,rk->hk', beta, jnp.sin(angles))
            i = jnp.arange(t)
            idx = i[:, None] - i[None, :] + (t - 1)
            return vec[:, idx]
        b, t, d = x.shape
        qkv = x @ Wqkv.T
        q, k, v = jnp.split(qkv, 3, axis=-1)

        def heads(a):
            return a.reshape(b, t, N_HEADS, HEAD_DIM).transpose(0, 2, 1, 3)
        q, k, v = (heads(q), heads(k), heads(v))
        scale = 1.0 / math.sqrt(HEAD_DIM)
        logits = jnp.einsum('bhqd,bhkd->bhqk', q, k) * scale
        logits = logits + _fourier_bias(alpha, beta, t)[None]
        causal = jnp.tril(jnp.ones((t, t), dtype=bool))
        logits = jnp.where(causal[None, None], logits, -jnp.inf)
        attn = jax.nn.softmax(logits, axis=-1)
        out = jnp.einsum('bhqk,bhkd->bhqd', attn, v)
        out = out.transpose(0, 2, 1, 3).reshape(b, t, d)
        return out @ Wout.T

    def _L0_xattn_ref(v, k, q, mask, wq_w, wq_b, wk_w, wk_b, wv_w, wv_b, wo_w, wo_b):
        import jax, jax.numpy as jnp
        import numpy as np
        D_MODEL = 256
        NUM_HEADS = 16
        DEPTH = D_MODEL // NUM_HEADS
        B, S = (4, 512)

        def _split_heads(x):
            b, s, _ = x.shape
            return x.reshape(b, s, NUM_HEADS, DEPTH).transpose(0, 2, 1, 3)
        qh = _split_heads(q @ wq_w + wq_b)
        kh = _split_heads(k @ wk_w + wk_b)
        vh = _split_heads(v @ wv_w + wv_b)
        scale = 1.0 / jnp.sqrt(jnp.asarray(DEPTH, jnp.float32))
        logits = jnp.einsum('bhqd,bhkd->bhqk', qh, kh) * scale
        logits = logits + mask * -1000000000.0
        attn = jax.nn.softmax(logits, axis=-1)
        out = jnp.einsum('bhqk,bhkd->bhqd', attn, vh)
        out = out.transpose(0, 2, 1, 3).reshape(out.shape[0], -1, D_MODEL)
        return out @ wo_w + wo_b

    def _L0_ffn_ref(x, router_w, router_b, routed_w1, routed_w3, routed_w2, shared_w1, shared_w3, shared_w2):
        import jax, jax.numpy as jnp
        import numpy as np
        BEST_K = 2

        def _expert(xf, w1, w3, w2):
            return jax.nn.silu(xf @ w1) * (xf @ w3) @ w2
        B, S, D = x.shape
        T = B * S
        xf = x.reshape(T, D)
        logits = xf @ router_w + router_b
        topk_vals, topk_idx = jax.lax.top_k(logits, BEST_K)
        sparse = jnp.full_like(logits, -jnp.inf)
        sparse = sparse.at[jnp.arange(T)[:, None], topk_idx].set(topk_vals)
        gates = jax.nn.softmax(sparse, axis=-1)
        routed = jax.vmap(_expert, in_axes=(None, 0, 0, 0))(xf, routed_w1, routed_w3, routed_w2)
        routed_out = jnp.einsum('etd,te->td', routed, gates)
        shared_out = jax.vmap(_expert, in_axes=(None, 0, 0, 0))(xf, shared_w1, shared_w3, shared_w2).sum(axis=0)
        return (routed_out + shared_out).reshape(B, S, D)

    def _L1_attn_ref(x, wq_lat, wk_lat, wv_lat, wq_heads, wk_heads, wv_heads, w_proj, b_proj):
        import jax, jax.numpy as jnp
        import numpy as np
        B, T, C = (2, 512, 256)
        LAT = 64
        N_HEAD = 16
        HEAD_DIM = C // N_HEAD
        SCALE = 1.0 / np.sqrt(HEAD_DIM).astype(np.float32)
        Bx, Tx, Cx = x.shape
        q = x @ wq_lat @ wq_heads
        k = x @ wk_lat @ wk_heads
        v = x @ wv_lat @ wv_heads
        q = q.reshape(Bx, Tx, N_HEAD, HEAD_DIM).transpose(0, 2, 1, 3)
        k = k.reshape(Bx, Tx, N_HEAD, HEAD_DIM).transpose(0, 2, 1, 3)
        v = v.reshape(Bx, Tx, N_HEAD, HEAD_DIM).transpose(0, 2, 1, 3)
        att = jnp.einsum('bhqd,bhkd->bhqk', q, k) * SCALE
        causal = jnp.tril(jnp.ones((Tx, Tx), dtype=bool))
        att = jnp.where(causal[None, None], att, -jnp.inf)
        att = jax.nn.softmax(att, axis=-1)
        y = jnp.einsum('bhqk,bhkd->bhqd', att, v)
        y = y.transpose(0, 2, 1, 3).reshape(Bx, Tx, Cx)
        return y @ w_proj + b_proj

    def _L1_xattn_ref(q, k, mask, Wq, bq, Wk, bk, Wv, bv, Wo, bo):
        import jax, jax.numpy as jnp
        import numpy as np
        B, LQ, LK = (8, 512, 512)
        QD = KD = VD = HD = 256
        qh = jnp.einsum('bld,dh->blh', q, Wq) + bq
        kh = jnp.einsum('bld,dh->blh', k, Wk) + bk
        vh = jnp.einsum('blh,hv->blv', kh, Wv) + bv
        scores = jnp.einsum('bqh,bkh->bqk', qh, kh)
        scores = jnp.where(mask[:, None, :] == 0, jnp.float32(-10000.0), scores)
        probs = jax.nn.softmax(scores, axis=-1)
        out = jnp.einsum('bqk,bkh->bqh', probs, vh)
        return jnp.einsum('bqh,hv->bqv', out, Wo) + bo

    def _L1_ffn_ref(x, W1, b1, quantum_phases, quantum_weights_real, quantum_weights_imag, W2, b2):
        import jax, jax.numpy as jnp
        import numpy as np
        B, S, D_MODEL, D_FF = (4, 512, 256, 1024)

        def _quantum_transform(hidden, theta, w_real, w_imag):
            imag = w_imag * jnp.sin(theta + hidden * 0.1)
            quantum_phase = jnp.cos(theta) * w_real + jnp.sin(theta) * w_imag
            return hidden + quantum_phase * imag * 0.1
        hidden = jnp.einsum('bsd,df->bsf', x, W1) + b1
        q = _quantum_transform(hidden, quantum_phases, quantum_weights_real, quantum_weights_imag)
        act = jax.nn.relu(q)
        return jnp.einsum('bsf,fd->bsd', act, W2) + b2
    x = _layernorm(x + _L0_attn_ref(x, L0_attn_Wqkv, L0_attn_Wout, L0_attn_alpha, L0_attn_beta), axis=-1)
    x = _layernorm(x + _L0_xattn_ref(ctx_1024, ctx_1024, x, mask_1x1xSxS2_fk1, L0_xattn_wq_w, L0_xattn_wq_b, L0_xattn_wk_w, L0_xattn_wk_b, L0_xattn_wv_w, L0_xattn_wv_b, L0_xattn_wo_w, L0_xattn_wo_b), axis=-1)
    x = _layernorm(x + _L0_ffn_ref(x, L0_ffn_router_w, L0_ffn_router_b, L0_ffn_routed_w1, L0_ffn_routed_w3, L0_ffn_routed_w2, L0_ffn_shared_w1, L0_ffn_shared_w3, L0_ffn_shared_w2), axis=-1)
    x = _layernorm(x + _L1_attn_ref(x, L1_attn_wq_lat, L1_attn_wk_lat, L1_attn_wv_lat, L1_attn_wq_heads, L1_attn_wk_heads, L1_attn_wv_heads, L1_attn_w_proj, L1_attn_b_proj), axis=-1)
    x = _layernorm(x + _L1_xattn_ref(x, ctx_1024, mask_BxS2_ik0, L1_xattn_Wq, L1_xattn_bq, L1_xattn_Wk, L1_xattn_bk, L1_xattn_Wv, L1_xattn_bv, L1_xattn_Wo, L1_xattn_bo), axis=-1)
    x = _layernorm(x + _L1_ffn_ref(x, L1_ffn_W1, L1_ffn_b1, L1_ffn_quantum_phases, L1_ffn_quantum_weights_real, L1_ffn_quantum_weights_imag, L1_ffn_W2, L1_ffn_b2), axis=-1)
    return x

_drawn_inputs = setup_inputs


def setup_inputs(seed=0):
    import zlib

    import numpy as np

    out = dict(_drawn_inputs(seed))
    spreads = {'L0_xattn_wq_b': (0.0, 0.1),
     'L0_xattn_wk_b': (0.0, 2.0),
     'L0_xattn_wv_b': (0.0, 0.1),
     'L0_xattn_wo_b': (0.0, 0.1),
     'L0_ffn_router_b': (0.0, 0.8),
     'L1_attn_b_proj': (0.0, 0.1),
     'L1_ffn_b1': (0.0, 0.1),
     'L1_ffn_b2': (0.0, 0.1)}
    factors = {'L0_attn_alpha': 8.0,
     'L0_attn_beta': 8.0,
     'L0_ffn_router_w': 4.585,
     'L0_ffn_routed_w1': 4.022,
     'L0_ffn_routed_w3': 3.946,
     'L0_ffn_routed_w2': 3.828,
     'L1_attn_wq_lat': 8.0,
     'L1_attn_wk_lat': 8.0,
     'L1_attn_wv_lat': 4.005,
     'L1_attn_wq_heads': 8.0,
     'L1_attn_wk_heads': 8.0,
     'L1_attn_wv_heads': 3.753,
     'L1_attn_w_proj': 3.626,
     'L1_xattn_bk': 3.702,
     'L1_xattn_bv': 4.263,
     'L1_xattn_bo': 3.733,
     'L1_ffn_quantum_phases': 8.0,
     'L1_ffn_quantum_weights_real': 35.714,
     'L1_ffn_quantum_weights_imag': 8.0}
    for name, (base, spread) in spreads.items():
        noise = np.random.default_rng([zlib.crc32(name.encode()), seed]).standard_normal(out[name].shape)
        drawn = base * np.exp(spread * noise) if base else spread * noise
        out[name] = jnp.asarray(drawn.astype(out[name].dtype))
    for name, factor in factors.items():
        out[name] = (out[name] * factor).astype(out[name].dtype)
    return out
```

```python
from contextlib import ExitStack

import numpy as np

import concourse.bass as bass
from concourse import mybir

ALU = mybir.AluOpType
ACT = mybir.ActivationFunctionType
AX = mybir.AxisListType
F32 = mybir.dt.float32
F32R = mybir.dt.float32r
BF16 = mybir.dt.bfloat16
I32 = mybir.dt.int32

P = 128
BATCH, SEQ, DIM = 16, 512, 256
CTX = 64
HEADS, HDIM = 16, 16
HALF = HEADS // 2
TT = SEQ // P
CT = DIM // P
EXPERTS, SHARED = 8, 2
HID = 128
LAT = 64
FF = 1024
FT = FF // P
SCALE = 0.25
EPS = 1e-5
NEG = -1e9
MASKED = -1e30
TWO_PI = float(np.nextafter(np.float32(2 * np.pi), np.float32(0)))
INV_2PI = float(np.float32(1 / (2 * np.pi)))
ROUND = float(1.5 * 2 ** 23)
PI_A = 6.28125
PI_B = round((2 * np.pi - PI_A) * 2 ** 20) / 2 ** 20
PI_C = 2 * np.pi - PI_A - PI_B

PT_AT = [0, 512, 1024, 896]
PT_COLS = 1280

W_PHASE = [
    dict(qk=CT * 512, v=CT * 256, o=CT * 256, xq=CT * 256, xk=CT * 256, xv=CT * 256, xo=CT * 256),
    dict(w1=CT * 10 * HID, w3=CT * 10 * HID, w2=10 * DIM, router=CT * P, lat=CT * 256,
         hq=DIM, hk=DIM, hv=DIM, o=CT * 256),
    dict(xqT=CT * 256, xk=CT * 256, xv=CT * 256, xo=CT * 256, w1=CT * FF, w2=FT * DIM),
]


def column_starts(names):
    at, out = 0, {}
    for name, n in names.items():
        out[name] = (at, n)
        at += n
    return out, at


class Queue:

    def __init__(self):
        self.steps = []
        self.seen = {}

    def wait(self, *marks):
        for mark in marks:
            if mark is None:
                continue
            sem, value = mark
            if self.seen.get(sem.name, 0) < value:
                self.seen[sem.name] = value
                self.steps.append(lambda e, s=sem, v=value: e.wait_ge(s, v))

    def add(self, make):
        self.steps.append(make)


class Lane:

    def __init__(self, queue, sem, step=1):
        self.queue, self.sem, self.step, self.count = queue, sem, step, 0

    def __call__(self, make, *after):
        self.queue.wait(*after)
        self.count += self.step
        self.queue.add(lambda e: make(e).then_inc(self.sem, self.step))
        return (self.sem, self.count)

    def silent(self, make, *after):
        self.queue.wait(*after)
        self.queue.add(make)

    @property
    def now(self):
        return (self.sem, self.count) if self.count else None


def decoder(nc, dram, out, batches=BATCH, phases=(1, 2, 3)):
    ctx = ExitStack()
    with ctx:
        def sem(name):
            return ctx.enter_context(nc.semaphore(name))

        queues = {n: Queue() for n in ("pe", "dve", "act", "pool", "sp")}

        def scratch(name, shape, dt=F32):
            return nc.dram_tensor(name, shape, dt, kind="Internal").ap()

        x_mid = [scratch(f"x_mid{n}", (BATCH, P, TT, DIM)) for n in range(2)]
        kt_scratch = scratch("kt_scratch", (P, 2, CT, BATCH * CTX))
        ctx_scratch = scratch("ctx_scratch", (P, 2, CT, BATCH * CTX))
        qk_scratch = scratch("qk_scratch", (2, 2, P, 2, 2, SEQ))

        ps = ctx.enter_context(nc.psum_tensor("ps", [P, 8, 512], F32))

        def sb(stack, name, shape, dt=F32):
            return stack.enter_context(nc.sbuf_tensor(name, shape, dt))

        ident = sb(ctx, "ident", [P, P])
        ident_b = sb(ctx, "ident_b", [P, P], BF16)
        future = sb(ctx, "future", [P, P], BF16)
        mhalf = sb(ctx, "mhalf", [P, TT])
        x_ring = sb(ctx, "x_ring", [P, 3, TT, DIM])

        s_const = sem("s_const")
        const = Lane(queues["pool"], s_const)

        class Stream:

            def __init__(self, phase, name, bank0):
                self.bank0 = bank0
                self.pe = Lane(queues["pe"], sem(f"s{phase}{name}_pe"))
                self.dve = Lane(queues["dve"], sem(f"s{phase}{name}_dve"))
                self.act = Lane(queues["act"], sem(f"s{phase}{name}_act"))
                self.pool = Lane(queues["pool"], sem(f"s{phase}{name}_pool"))
                self.free = {}

            def bank(self, i, n=1):
                b = self.bank0 + i
                return ps[:, b, :] if n == 1 else ps[:, b:b + n, :].rearrange("p a b -> p (a b)")

        lanes_seen = []

        def dma_lane(name, queue="sp"):
            lane = Lane(queues[queue], sem(name), 16)
            lanes_seen.append(lane)
            return lane

        def barrier():
            marks = [lane.now for lane in lanes_seen]
            for q in queues.values():
                q.wait(*marks)

        zero_b = const(lambda e: e.memset(ident_b[:, :], 0.0))
        zero = const(lambda e: e.memset(ident[:, :], 0.0))
        zero_u = const(lambda e: e.memset(future[:, :], 0.0))
        const(lambda e: e.memset(mhalf[:, :], -0.5))
        for t, mark in ((ident_b, zero_b), (ident, zero)):
            const(lambda e, t=t: e.affine_select(out=t[:, :], in_=t[:, :], compare_op=ALU.not_equal, fill=1.0,
                                                 base=0, pattern=[[-1, P]], channel_multiplier=1), mark)
        const(lambda e: e.affine_select(out=future[:, :], in_=future[:, :], compare_op=ALU.is_ge, fill=MASKED,
                                        base=0, pattern=[[-1, P]], channel_multiplier=1), zero_u)
        lanes_seen.append(const)

        def passes(pe, out_ap, operands, *after, start=True, stop=True, check=True):
            pe.queue.wait(*after)
            for i, (lhs, rhs) in enumerate(operands):
                first, last = start and i == 0, stop and i == len(operands) - 1

                def make(e, lhs=lhs, rhs=rhs, first=first, last=last):
                    return e.matmul(out_ap, lhs, rhs, start=first, stop=last, skip_group_check=not check)
                if i == len(operands) - 1:
                    return pe(make)
                pe.silent(make)

        def three(lh, ll, rh, rl):
            return [(lh, rh), (ll, rh), (lh, rl)]

        def split_psum(s, src, hi, lo, *after, scale=1.0, bias=None):
            if bias is None:
                m = s.act(lambda e: e.activation(hi, src, ACT.Copy, scale=scale), *after)
                return m, s.dve(lambda e: e.scalar_tensor_tensor(
                    out=lo, in0=src, scalar=scale, in1=hi.bitcast(F32), op0=ALU.mult, op1=ALU.subtract), m)
            m = s.act(lambda e: e.activation(hi, src, ACT.Identity, bias=bias), *after)
            return m, s.dve(lambda e: e.scalar_tensor_tensor(
                out=lo, in0=src, scalar=bias, in1=hi.bitcast(F32), op0=ALU.add, op1=ALU.subtract), m)

        def to_channels(s, tok, hi, lo, ready, buf_free):
            marks = []
            for c in range(CT):
                s.pe.queue.wait(ready, s.free.get(c), s.free.get(c, None))
                for t in range(TT):
                    def make(e, c=c, t=t):
                        return e.transpose(s.bank(c)[:, t * P:(t + 1) * P], tok[:, t, c * P:(c + 1) * P], ident[:, :])
                    if t == TT - 1:
                        m = s.pe(make)
                    else:
                        s.pe.silent(make)
                a, d = split_psum(s, s.bank(c), hi[:, c, :], lo[:, c, :], m, buf_free)
                s.free[c] = d
                marks += [a, d]
            return marks

        def layernorm(s, x, stats, after, last_use=None):
            bn, ag, rs = stats
            add = s.dve(lambda e: e.tensor_tensor(x.rearrange("p t d -> p (t d)"), x.rearrange("p t d -> p (t d)"),
                                                  s.bank(0, 2), ALU.add), after, last_use)
            s.free[0] = s.free[1] = add
            for t in range(TT):
                m = s.dve(lambda e, t=t: e.bn_stats(bn[:, t, :], x[:, t, :]), add)
            for t in range(TT):
                m2 = s.dve(lambda e, t=t: e.bn_aggr(ag[:, t, :], bn[:, t, :]), m)
            m = s.dve(lambda e: e.tensor_scalar(rs[:, 0, :], ag[:, :, 1], EPS, None, ALU.add), m2)
            m = s.pool(lambda e: e.tensor_tensor(rs[:, 1, :], rs[:, 0, :], mhalf[:, :], ALU.pow), m, const.now)
            for t in range(TT):
                end = s.dve(lambda e, t=t: e.tensor_scalar(x[:, t, :], x[:, t, :], ag[:, t, 0:1], rs[:, 1, t:t + 1],
                                                           ALU.subtract, ALU.mult), m)
            return end

        def merge(first, second):
            clocks = [0.0, 0.0]
            streams = [first, second]
            alive = [True, True]
            while any(alive):
                k = 0 if alive[0] and (not alive[1] or clocks[0] <= clocks[1]) else 1
                try:
                    clocks[k] += next(streams[k])
                except StopIteration:
                    alive[k] = False

        def chain(*generators):
            for g in generators:
                yield from g

        def load_weights(stack, phase):
            starts, cols = column_starts(W_PHASE[phase - 1])
            hi = sb(stack, f"w{phase}_hi", [P, cols], F32R)
            lo = sb(stack, f"w{phase}_lo", [P, cols], F32R)
            step = 1024
            stage_ctx = ExitStack()
            stage = stage_ctx.enter_context(nc.sbuf_tensor(f"w{phase}_stage", [P, 2, step], F32))
            load = [dma_lane(f"s_w{phase}_{n}") for n in range(2)]
            dve = Lane(queues["dve"], sem(f"s_ws{phase}"))
            act = Lane(queues["act"], sem(f"s_wa{phase}"))
            lanes_seen.extend([dve, act])
            free = [None, None]
            for i, at in enumerate(range(0, cols, step)):
                n, b = min(step, cols - at), i % 2
                m = load[b](lambda e, at=at, n=n, b=b: e.dma_start(stage[:, b, 0:n], dram[f"w{phase}"][:, at:at + n]),
                            free[b])
                a = act(lambda e, at=at, n=n, b=b: e.activation(hi[:, at:at + n], stage[:, b, 0:n], ACT.Copy), m)
                free[b] = dve(lambda e, at=at, n=n, b=b: e.tensor_tensor(
                    lo[:, at:at + n], stage[:, b, 0:n], hi[:, at:at + n].bitcast(F32), ALU.subtract), a)

            def get(name, *dims):
                at, n = starts[name]
                views = [t[:, at:at + n] for t in (hi, lo)]
                if len(dims) == 1:
                    return [v.rearrange("p (a b) -> p a b", a=dims[0]) for v in views]
                if len(dims) == 2:
                    return [v.rearrange("p (a b c) -> p a b c", a=dims[0], b=dims[1]) for v in views]
                return views
            return get, stage_ctx, free

        class Attention:
            def __init__(self, stack, s, phase, slots):
                self.s, self.slots, self.phase = s, slots, phase
                self.q = sb(stack, f"q_stack{phase}", [P, slots, SEQ], F32R)
                self.k = sb(stack, f"k_stack{phase}", [P, slots, SEQ], F32R)
                self.out_dma = dma_lane(f"s_qk_out{phase}")
                self.in_dma = [dma_lane(f"s_qk_in{phase}_{n}") for n in range(2)]
                self.max_dma = dma_lane(f"s_max{phase}")
                self.use = [None, None]
                self.mark = {}

            def buffers(self, stack):
                phase = self.phase
                self.v = sb(stack, f"v_wide{phase}", [P, TT, HEADS, 32])
                self.pt = sb(stack, f"pt{phase}", [P, 4, PT_COLS])
                self.xh = sb(stack, f"xh{phase}", [P, CT, SEQ], F32R)
                self.xl = sb(stack, f"xl{phase}", [P, CT, SEQ], F32R)
                self.parts = sb(stack, f"parts{phase}", [P, 2, 2, SEQ], F32R)
                self.nmax = sb(stack, f"nmax{phase}", [P, HALF, TT])
                self.nmaxT = sb(stack, f"nmaxT{phase}", [HALF * TT, P], F32R)
                self.oT = self.pt[:, 0, 0:SEQ]
                self.o = sb(stack, f"o{phase}", [P, TT, DIM])
                self.rec = sb(stack, f"rec{phase}", [P, TT, 4, 1])
                self.stats = (sb(stack, f"bn{phase}", [P, TT, 6]), sb(stack, f"ag{phase}", [P, TT, 2]),
                              sb(stack, f"rs{phase}", [P, 2, TT]))
                m = self.s.pool(lambda e: e.memset(self.v[:, :, :, HDIM:32], 0.0))
                self.v_ones = self.s.pool(lambda e: e.memset(self.v[:, :, :, HDIM:HDIM + 1], 1.0), m)

            def setup(self):
                s = self.s
                m = s.pool(lambda e: e.memset(self.k[:, :, :].bitcast(F32), 0.0))
                m = s.pool(lambda e: e.memset(self.k[96:97, :, :].bitcast(F32), 1.0), m)
                s.pool(lambda e: e.memset(self.q[:, :, :].bitcast(F32), 0.0), m)
                return s.pool.now

            def send(self, b, half, split):
                home = qk_scratch[b % 2, half]
                out_m = self.out_dma(lambda e: e.dma_start(home, self.parts[:, :, :, :].bitcast(F32)), *split, *self.rows_free(half))
                self.mark["parts_free"] = out_m
                base = (half * HALF) % self.slots
                lane = self.in_dma[half]
                first = True
                for block, qpart, kpart in ((0, 0, 0), (1, 0, 1), (2, 1, 0)):
                    for stack_t, which, part in ((self.q, 0, qpart), (self.k, 1, kpart)):
                        src = home[:, which, part, :].rearrange("(h d) t -> d h t", d=HDIM)
                        dst = stack_t[32 * block:32 * block + HDIM, base:base + HALF, :].bitcast(F32)
                        m = lane(lambda e, dst=dst, src=src: e.dma_start(dst, src), out_m)
                self.mark["rows", half] = m
                return m

            def rows_free(self, half):
                return self.use if self.slots == HALF else [self.use[half]]

            def scores_max(self, half):
                s = self.s
                ready = self.mark["rows", half]
                for hh in range(HALF):
                    slot = (half * HALF) % self.slots + hh
                    s.pe.queue.wait(ready, s.free.get(0), s.free.get(1), s.free.get(2), const.now)
                    where = {3: s.bank(0)[:, 0:512], 2: s.bank(1)[:, 0:384], 0: s.bank(1)[:, 384:512],
                             1: s.bank(2)[:, 0:256]}
                    for t in (3, 2, 0, 1):
                        n = (t + 1) * P
                        dst = where[t]
                        s.pe.silent(lambda e, dst=dst, t=t, n=n, slot=slot: e.matmul(
                            dst, self.q[0:96, slot, t * P:(t + 1) * P], self.k[0:96, slot, 0:n],
                            start=True, stop=False))
                        mk = lambda e, dst=dst, n=n: e.matmul(dst[:, n - P:n], ident_b[:, :], future[:, :],
                                                              start=False, stop=True)
                        if t == 1:
                            m = s.pe(mk)
                        else:
                            s.pe.silent(mk)
                    for t in (3, 2, 0, 1):
                        d = s.dve(lambda e, t=t, hh=hh, src=where[t]: e.tensor_reduce(
                            self.nmax[:, hh, t:t + 1], src, AX.X, ALU.max, negate=True), m, self.mark.get("nmax"))
                    s.free[0] = s.free[1] = s.free[2] = d
                    yield 1500.0
                rows = HALF * TT
                m = s.pe(lambda e: e.transpose(s.bank(3)[0:rows, 0:P], self.nmax[:, :, :].rearrange("p h t -> p (h t)"),
                                               ident[:, :]), d, s.free.get(3))
                self.mark["nmax"] = m
                a = s.act(lambda e: e.activation(self.nmaxT[:, :], s.bank(3)[0:rows, 0:P], ACT.Copy), m,
                          self.mark.get("max_row"))
                s.free[3] = a
                base = (half * HALF) % self.slots
                dst = self.q[96:97, base:base + HALF, :].bitcast(F32).rearrange("p h (t q) -> p (h t) q", q=P)
                self.mark["max_row"] = self.max_dma(lambda e: e.dma_start(dst, self.nmaxT[:, :].bitcast(F32)), a)

            def attend(self, half, v_ready):
                s = self.s
                for group in range(2):
                    pt_ready = []
                    for g in range(4):
                        h = half * HALF + group * 4 + g
                        slot = (half * HALF) % self.slots + group * 4 + g
                        s.pe.queue.wait(self.mark["max_row"], s.free.get(0), s.free.get(1), s.free.get(2))
                        banks = s.bank(0, 3)
                        for j in (0, 1, 3, 2):
                            dst = banks[:, PT_AT[j]:PT_AT[j] + SEQ - j * P]
                            mk = lambda e, dst=dst, j=j, slot=slot: e.matmul(
                                dst, self.k[:, slot, j * P:(j + 1) * P], self.q[:, slot, j * P:SEQ],
                                start=True, stop=True)
                            if j == 2:
                                m = s.pe(mk)
                            else:
                                s.pe.silent(mk)
                        self.use[half] = m
                        a = s.act(lambda e, g=g: e.activation(self.pt[:, g, :], banks[:, 0:PT_COLS], ACT.Exp),
                                  m, self.mark.get("pt"))
                        s.free[0] = s.free[1] = s.free[2] = a
                        for at in (0, 512, 1024, 896):
                            blk = self.pt[:, g, at:at + P]
                            m = s.pool(lambda e, blk=blk: e.affine_select(
                                out=blk, in_=blk, compare_op=ALU.is_ge, fill=0.0, base=0,
                                pattern=[[1, P]], channel_multiplier=-1), a)
                        pt_ready.append(m)
                        yield 1300.0
                    s.pe.queue.wait(v_ready, s.free.get(3), *pt_ready)
                    for j in range(TT):
                        for g in range(4):
                            h = half * HALF + group * 4 + g
                            mk = lambda e, j=j, g=g, h=h: e.matmul(
                                s.bank(3)[32 * g:32 * g + 32, j * P:SEQ], self.v[:, j, h, :],
                                self.pt[:, g, PT_AT[j]:PT_AT[j] + SEQ - j * P], start=(j == 0), stop=(j == TT - 1))
                            if j == TT - 1 and g == 3:
                                m = s.pe(mk)
                            else:
                                s.pe.silent(mk)
                    self.mark["v_use"] = m
                    a = s.act(lambda e: e.activation(self.oT, s.bank(3), ACT.Copy), m)
                    s.pe.queue.wait(a)
                    for t in range(TT):
                        mk = lambda e, t=t: e.transpose(s.bank(3)[:, t * P:(t + 1) * P],
                                                        self.oT[:, t * P:(t + 1) * P], ident[:, :])
                        m = s.pe(mk) if t == TT - 1 else s.pe.silent(mk)
                    self.mark["pt"] = m
                    ov = s.bank(3).rearrange("p (t g d) -> p t g d", t=TT, g=4)
                    d = s.dve(lambda e: e.reciprocal(self.rec[:, :, :, :], ov[:, :, :, HDIM:HDIM + 1]), m)
                    h0 = half * HALF + group * 4
                    for t in range(TT):
                        d2 = s.dve(lambda e, t=t, h0=h0: e.tensor_tensor(
                            self.o[:, t, h0 * HDIM:(h0 + 4) * HDIM].rearrange("p (g d) -> p g d", g=4),
                            ov[:, t, :, 0:HDIM], self.rec[:, t, :, :].broadcast_to([P, 4, HDIM]), ALU.mult),
                            d, self.mark.get("o"))
                    s.free[3] = d2
                    yield 3000.0
                self.mark["o_ready"] = d2

            def project(self, w, x, bias):
                s = self.s
                marks = to_channels(s, self.o[:, :, :], self.xh, self.xl, self.mark["o_ready"], self.mark.get("x_use"))
                self.mark["o"] = s.pe.now
                m = token_major(s, self.xh, self.xl, w, marks)
                self.mark["x_use"] = m
                return layernorm(s, x, self.stats, m, bias)

        def token_major(s, ah, al, w, ready, also=()):
            s.pe.queue.wait(*ready, s.free.get(0), s.free.get(1))
            for t in range(TT):
                dst = s.bank(t // 2)[:, (t % 2) * DIM:(t % 2 + 1) * DIM]
                ops = []
                for c in range(CT):
                    ops += three(ah[:, c, t * P:(t + 1) * P], al[:, c, t * P:(t + 1) * P], w[0][:, c, :], w[1][:, c, :])
                m = passes(s.pe, dst, ops)
            return m

        def back_to_tokens(s, tiles, m, free):
            for c in range(CT):
                a = s.act(lambda e, c=c: e.activation(tiles[c], s.bank(2 + c), ACT.Copy), m, *free)
                s.free[2 + c] = a
            s.pe.queue.wait(a, s.free.get(0), s.free.get(1))
            for t in range(TT):
                for c in range(CT):
                    at = (t % 2) * DIM + c * P
                    mk = lambda e, t=t, c=c, at=at: e.transpose(s.bank(t // 2)[:, at:at + P],
                                                                tiles[c][:, t * P:(t + 1) * P], ident[:, :])
                    m = s.pe(mk) if (t, c) == (TT - 1, CT - 1) else s.pe.silent(mk)
            return m

        def bias_rows(stack, name):
            t = sb(stack, name + "_rows", [P, DIM])
            lane = dma_lane("s_" + name)
            m = lane(lambda e: e.dma_start(t[:, :], dram[name].partition_broadcast(P)))
            return t, m

        def columns(stack, name, n):
            t = sb(stack, name + "_cols", [P, n])
            lane = dma_lane("s_" + name)
            m = lane(lambda e: e.dma_start(t[:, :], dram[name]))
            return t, m

        x_load = [dma_lane(f"s_x{n}") for n in range(3)]
        x_store = [dma_lane(f"s_xs{n}") for n in range(3)]
        x_of = lambda b: x_ring[:, b % 3, :, :]

        def phase1():
            with ExitStack() as st:
                X, Y = Stream(1, "x", 0), Stream(1, "y", 4)
                for s in (X, Y):
                    lanes_seen.extend([s.pe, s.dve, s.act, s.pool])
                att = Attention(st, X, 1, HEADS)
                xq_b, m_qb = columns(st, "xq_b", CT)
                xk_b, m_kb = columns(st, "xk_b", CT)
                xv_b, m_vb = bias_rows(st, "xv_b")
                xo_b, m_ob = bias_rows(st, "xo_b")
                nmask = sb(st, "nmask", [P, TT, CTX])
                head_of = sb(st, "head_of", [P, HALF])
                get, stage_ctx, wm = load_weights(st, 1)
                trig = stage_ctx.enter_context(nc.sbuf_tensor("trig", [P, 3, SEQ], F32))
                four = stage_ctx.enter_context(nc.sbuf_tensor("four", [P, 2, 2, SEQ], F32))
                fhi = stage_ctx.enter_context(nc.sbuf_tensor("fhi", [P, 2, SEQ], F32R))
                ab = stage_ctx.enter_context(nc.sbuf_tensor("ab", [P, 2, HEADS], F32))
                ctx_st = stage_ctx.enter_context(nc.sbuf_tensor("ctx_st", [P, CT, BATCH * CTX], F32))
                ctx_h = stage_ctx.enter_context(nc.sbuf_tensor("ctx_h", [P, CT, BATCH * CTX], F32R))
                ctx_l = stage_ctx.enter_context(nc.sbuf_tensor("ctx_l", [P, CT, BATCH * CTX], F32R))
                kt32 = stage_ctx.enter_context(nc.sbuf_tensor("kt32", [P, 512], F32))
                kt_st = stage_ctx.enter_context(nc.sbuf_tensor("kt_st", [P, 2, 512], F32R))
                small = dma_lane("s_small1")
                small(lambda e: e.dma_start(trig[:, :, :], dram["trig"]))
                small(lambda e: e.dma_start(ab[:, :, :], dram["alpha_beta"]))
                m_nm = small(lambda e: e.dma_start(nmask[:, :, :], dram["mask_f"]))
                m_small = small(lambda e: e.dma_start(head_of[:, :], dram["head_of"]))
                m_ctx = small(lambda e: e.dma_start(ctx_st[:, :, :], dram["ctxT"]))
                zeroed = att.setup()
                m_nm = Y.dve(lambda e: e.tensor_scalar(nmask[:, :, :], nmask[:, :, :], NEG, None, ALU.mult), m_ctx)
                m = X.act(lambda e: e.activation(fhi[:, 0, :], trig[:, 2, :], ACT.Copy), m_ctx)
                m = X.dve(lambda e: e.tensor_tensor(four[:, 0, 0, :], trig[:, 2, :], fhi[:, 0, :].bitcast(F32),
                                                    ALU.subtract), m)
                for h in range(HEADS):
                    for blk, src in ((0, fhi[:, 0, :]), (1, four[:, 0, 0, :]), (2, fhi[:, 0, :])):
                        lane = X.act if blk == 1 else X.pool
                        r = slice(32 * blk, 32 * blk + 32)
                        if blk == 1:
                            kq = X.act(lambda e, h=h, r=r, src=src: e.activation(att.k[r, h, :], src[r], ACT.Copy),
                                       m, zeroed)
                        else:
                            kq = X.act(lambda e, h=h, r=r, src=src: e.activation(
                                att.k[r, h, :], src[r].bitcast(F32), ACT.Copy), m, zeroed)
                last = [kq, kq]
                for h in range(HEADS):
                    i = h % 2
                    m = X.dve(lambda e, h=h, i=i: e.tensor_scalar(four[:, i, 0, :], trig[:, 0, :], ab[:, 0, h:h + 1],
                                                                  None, ALU.mult), last[i])
                    m = X.dve(lambda e, h=h, i=i: e.scalar_tensor_tensor(
                        out=four[:, i, 1, :], in0=trig[:, 1, :], scalar=ab[:, 1, h:h + 1], in1=four[:, i, 0, :],
                        op0=ALU.mult, op1=ALU.add), m)
                    a = X.act(lambda e, h=h, i=i: e.activation(fhi[:, i, :], four[:, i, 1, :], ACT.Copy), m)
                    X.act(lambda e, h=h, i=i: e.activation(att.q[0:64, h, :], fhi[0:64, i, :].bitcast(F32), ACT.Copy), a, zeroed)
                    last[i] = X.dve(lambda e, h=h, i=i: e.tensor_tensor(
                        att.q[64:96, h, :], four[64:96, i, 1, :], fhi[64:96, i, :].bitcast(F32), ALU.subtract), a)
                a = Y.act(lambda e: e.activation(ctx_h[:, :, :], ctx_st[:, :, :], ACT.Copy), m_ctx)
                m_ctx2 = Y.dve(lambda e: e.tensor_tensor(ctx_l[:, :, :], ctx_st[:, :, :], ctx_h[:, :, :].bitcast(F32),
                                                         ALU.subtract), a)
                Y.pe.queue.wait(wm[0], wm[1])
                wxk = get("xk", CT)
                m_bias = Y.dve(lambda e: e.tensor_scalar(xk_b[:, :], xk_b[:, :], SCALE, None, ALU.mult), m_kb)
                kt_out = dma_lane("s_kt_out")
                for mt in range(CT):
                    for n in range(2):
                        ops = []
                        cols = slice(n * 512, n * 512 + 512)
                        for c in range(CT):
                            ops += three(wxk[0][:, c, mt * P:(mt + 1) * P], wxk[1][:, c, mt * P:(mt + 1) * P],
                                         ctx_h[:, c, cols], ctx_l[:, c, cols])
                        m = passes(Y.pe, Y.bank(0), ops, Y.free.get(0), m_ctx2)
                        m = Y.act(lambda e, mt=mt: e.activation(kt32[:, :], Y.bank(0), ACT.Identity,
                                                                bias=xk_b[:, mt:mt + 1], scale=SCALE),
                                  m, m_bias, Y.free.get("kt32"))
                        Y.free[0] = m
                        a = Y.act(lambda e: e.activation(kt_st[:, 0, :], kt32[:, :], ACT.Copy), m, kt_out.now)
                        Y.free["kt32"] = Y.dve(lambda e: e.tensor_tensor(
                            kt_st[:, 1, :], kt32[:, :], kt_st[:, 0, :].bitcast(F32), ALU.subtract), a, kt_out.now)
                        for part in range(2):
                            kt_out(lambda e, mt=mt, cols=cols, part=part: e.dma_start(
                                kt_scratch[:, part, mt, cols], kt_st[:, part, :].bitcast(F32)), a, Y.free["kt32"])
                for part, t in ((0, ctx_h), (1, ctx_l)):
                    kt_out(lambda e, part=part, t=t: e.dma_start(ctx_scratch[:, part, :, :], t[:, :, :].bitcast(F32)), m_ctx2)
                barrier()
                stage_ctx.close()
                att.buffers(st)

                yh = sb(st, "yh", [P, CT, SEQ], F32R)
                yl = sb(st, "yl", [P, CT, SEQ], F32R)
                qx_h = sb(st, "qx_h", [P, CT, SEQ], F32R)
                qx_l = sb(st, "qx_l", [P, CT, SEQ], F32R)
                kc = sb(st, "kc", [P, 2, CT, CTX], F32R)
                cc = sb(st, "cc", [P, 2, CT, 2, CTX], F32R)
                kc_load = dma_lane("s_kc")
                km_h = sb(st, "km_h", [P, CT, HALF, CTX], F32R)
                km_l = sb(st, "km_l", [P, CT, HALF, CTX], F32R)
                vx = sb(st, "vx", [P, HALF, 32])
                sc = sb(st, "sc", [P, 2, HALF, CTX])
                pr = sb(st, "pr", [P, 2, HALF, CTX])
                mx = sb(st, "mx", [P, 2, 3, HALF, 1])
                ptx = sb(st, "ptx", [P, 4, SEQ])
                ystats = (sb(st, "ybn", [P, TT, 6]), sb(st, "yag", [P, TT, 2]), sb(st, "yrs", [P, 2, TT]))
                m_vz = Y.pool(lambda e: e.memset(vx[:, :, :], 0.0))

                wqk, wv, wo = get("qk", CT), get("v", CT), get("o", CT)
                loaded, x_done, x_final = {}, {}, {}

                def load_x(b):
                    if b < batches:
                        loaded[b] = x_load[b % 3](lambda e: e.dma_start(
                            x_of(b), dram["x"][b].rearrange("(t p) d -> p t d", p=P)),
                            x_final.get(b - 3), x_done.get(b - 3))

                def attn0(b):
                    s = X
                    x = x_of(b)
                    ready = to_channels(s, x, att.xh, att.xl, loaded[b], att.mark.get("x_use"))
                    yield 2500.0
                    for half in range(2):
                        split = []
                        for which in range(2):
                            mcol = which * 256 + half * P
                            ops = []
                            for c in range(CT):
                                ops += three(wqk[0][:, c, mcol:mcol + P], wqk[1][:, c, mcol:mcol + P],
                                             att.xh[:, c, :], att.xl[:, c, :])
                            m = passes(s.pe, s.bank(which), ops, *ready, s.free.get(which))
                            a, d = split_psum(s, s.bank(which), att.parts[:, which, 0, :], att.parts[:, which, 1, :],
                                              m, att.mark.get("parts_free"), scale=SCALE if which == 0 else 1.0)
                            s.free[which] = d
                            split += [a, d]
                            yield 1500.0
                        att.send(b, half, split)
                    m = token_major(s, att.xh, att.xl, wv, ready)
                    att.mark["x_use"] = m
                    for i in range(2):
                        v_ready = s.act(lambda e, i=i: e.activation(
                            att.v[:, 2 * i:2 * i + 2, :, 0:HDIM],
                            s.bank(i).rearrange("p (t h d) -> p t h d", t=2, d=HDIM), ACT.Copy),
                            m, att.mark.get("v_use"), att.v_ones)
                    s.free[0] = s.free[1] = v_ready
                    yield 4500.0
                    for half in range(2):
                        yield from att.scores_max(half)
                        yield from att.attend(half, v_ready)
                    x_done[b] = att.project(wo, x, None)
                    yield 9000.0

                wxq, wxv, wxo = get("xq", CT), get("xv", CT), get("xo", CT)
                use = {}

                def cross0(b):
                    s = Y
                    x = x_of(b)
                    keys = slice(b * CTX, (b + 1) * CTX)
                    kc_load(lambda e: e.dma_start(kc[:, :, :, :].bitcast(F32), kt_scratch[:, :, :, keys]), use.get("kc"),
                            use.get("kc_pe"))
                    for part in range(2):
                        for twice in range(2):
                            kc_ready = kc_load(lambda e, part=part, twice=twice: e.dma_start(
                                cc[:, part, :, twice, :].bitcast(F32), ctx_scratch[:, part, :, keys]))
                    for part, src in ((km_h, kc[:, 0, :, :]), (km_l, kc[:, 1, :, :])):
                        for c in range(CT):
                            km = s.pool(lambda e, part=part, src=src, c=c: e.tensor_tensor(
                                part[:, c, :, :], src[:, c, :].bitcast(F32).unsqueeze(1).broadcast_to([P, HALF, CTX]),
                                head_of[:, :].unsqueeze(2).broadcast_to([P, HALF, CTX]), ALU.mult),
                                kc_ready, m_small, use.get("km"))
                    use["kc"] = km
                    ops = []
                    for c in range(CT):
                        ch = cc[:, 0, c, :, :].rearrange("p a k -> p (a k)")
                        cl = cc[:, 1, c, :, :].rearrange("p a k -> p (a k)")
                        ops += three(ch, cl, wxv[0][:, c, :], wxv[1][:, c, :])
                    m = use["kc_pe"] = passes(s.pe, s.bank(2)[:, 0:DIM], ops, s.free.get(2), kc_ready)
                    for odd in range(2):
                        r = slice(64 * odd, 64 * odd + 64)
                        vm = s.dve(lambda e, r=r, odd=odd: e.tensor_tensor(
                            vx[r, :, 16 * odd:16 * odd + 16],
                            s.bank(2)[r, 0:DIM].rearrange("p (a o d) -> p a o d", o=2, d=HDIM)[:, :, odd, :],
                            xv_b[r, :].rearrange("p (a o d) -> p a o d", o=2, d=HDIM)[:, :, odd, :], ALU.add),
                            m, m_vb, m_vz, use.get("vx"))
                    s.free[2] = vm
                    yield 1500.0
                    ready = to_channels(s, x, yh, yl, x_done[b], use.get("yh"))
                    yield 2500.0
                    qm = []
                    for mt in range(CT):
                        ops = []
                        for c in range(CT):
                            ops += three(wxq[0][:, c, mt * P:(mt + 1) * P], wxq[1][:, c, mt * P:(mt + 1) * P],
                                         yh[:, c, :], yl[:, c, :])
                        m = passes(s.pe, s.bank(mt), ops, *ready, s.free.get(mt))
                        a, d = split_psum(s, s.bank(mt), qx_h[:, mt, :], qx_l[:, mt, :], m, use.get("qx"),
                                          m_qb, bias=xq_b[:, mt:mt + 1])
                        s.free[mt] = d
                        qm += [a, d]
                    use["yh"] = m
                    yield 3000.0
                    xb = s.pool(lambda e: e.tensor_tensor(x, x, xo_b[:, :].unsqueeze(1).broadcast_to([P, TT, DIM]),
                                                          ALU.add), *ready, m_ob, s.pe.now)
                    om = []
                    for c in range(CT):
                        for t in range(TT):
                            i = t % 2
                            rows = slice(t * P, (t + 1) * P)
                            kmv = [part[:, c, :, :].rearrange("p h k -> p (h k)") for part in (km_h, km_l)]
                            m = passes(s.pe, s.bank(2 + i), three(qx_h[:, c, rows], qx_l[:, c, rows], kmv[0], kmv[1]),
                                       *qm, km, s.free.get(2 + i))
                            use["qx"] = use["km"] = m
                            d = s.dve(lambda e, i=i, t=t: e.tensor_tensor(
                                sc[:, i, :, :], s.bank(2 + i).rearrange("p (h k) -> p h k", h=HALF),
                                nmask[:, t, :].unsqueeze(1).broadcast_to([P, HALF, CTX]), ALU.add),
                                m, m_nm, use.get(("sc", i)))
                            s.free[2 + i] = d
                            d = s.dve(lambda e, i=i: e.tensor_reduce(mx[:, i, 0, :, :], sc[:, i, :, :], AX.X, ALU.max), d,
                                      use.get(("sc", i)))
                            d = s.pool(lambda e, i=i: e.tensor_tensor(
                                sc[:, i, :, :], sc[:, i, :, :], mx[:, i, 0, :, :].broadcast_to([P, HALF, CTX]),
                                ALU.subtract), d)
                            a = s.act(lambda e, i=i: e.activation(pr[:, i, :, :], sc[:, i, :, :], ACT.Exp), d,
                                      use.get(("pr", i)))
                            use["sc", i] = a
                            d = s.dve(lambda e, i=i: e.tensor_reduce(mx[:, i, 1, :, :], pr[:, i, :, :], AX.X, ALU.add), a)
                            d = s.dve(lambda e, i=i: e.reciprocal(mx[:, i, 2, :, :], mx[:, i, 1, :, :]), d)
                            d = s.pool(lambda e, i=i: e.tensor_tensor(
                                pr[:, i, :, :], pr[:, i, :, :], mx[:, i, 2, :, :].broadcast_to([P, HALF, CTX]),
                                ALU.mult), d)
                            use["sc", i] = d
                            s.pe.queue.wait(d, s.free.get(i))
                            for p in range(4):
                                mk = lambda e, i=i, p=p: e.transpose(
                                    s.bank(i)[:, p * P:(p + 1) * P],
                                    pr[:, i, 2 * p:2 * p + 2, :].rearrange("p h k -> p (h k)"), ident[:, :])
                                m = s.pe(mk) if p == 3 else s.pe.silent(mk)
                            use["pr", i] = m
                            a = s.act(lambda e, i=i, c=c, rows=rows: e.activation(
                                ptx[:, :, rows], s.bank(i).rearrange("p (a q) -> p a q", a=4), ACT.Copy),
                                m, use.get("ptx"))
                            s.free[i] = a
                            yield 3500.0
                        s.pe.queue.wait(a, vm, s.free.get(2))
                        for p in range(4):
                            mk = lambda e, p=p, c=c: e.matmul(s.bank(2)[32 * p:32 * p + 32, :], vx[:, 4 * c + p, :],
                                                              ptx[:, p, :], start=True, stop=True)
                            m = s.pe(mk) if p == 3 else s.pe.silent(mk)
                        use["ptx"] = use["vx"] = m
                        a, d = split_psum(s, s.bank(2), yh[:, c, :], yl[:, c, :], m)
                        s.free[2] = d
                        om += [a, d]
                        yield 2000.0
                    m = token_major(s, yh, yl, wxo, om)
                    use["yh"] = m
                    end = layernorm(s, x, ystats, m, xb)
                    x_final[b] = x_store[b % 3](lambda e: e.dma_start(x_mid[0][b], x), end)
                    yield 9000.0

                for b in range(2):
                    load_x(b)
                for b in range(batches + 1):
                    merge(attn0(b) if b < batches else iter(()), cross0(b - 1) if b > 0 else iter(()))
                    load_x(b + 2)
                barrier()

        def phase2():
            with ExitStack() as st:
                X, Y = Stream(2, "x", 0), Stream(2, "y", 4)
                for s in (X, Y):
                    lanes_seen.extend([s.pe, s.dve, s.act, s.pool])
                proj_b, m_pb = bias_rows(st, "proj_b")
                router_b, m_rb = columns(st, "router_b", 1)
                att = Attention(st, X, 2, HALF)
                get, stage_ctx, wm = load_weights(st, 2)
                zeroed = att.setup()
                barrier()
                stage_ctx.close()
                att.buffers(st)

                yh = sb(st, "yh2", [P, CT, SEQ], F32R)
                yl = sb(st, "yl2", [P, CT, SEQ], F32R)
                gate_of = sb(st, "gate_of", [P, 2, 2, SEQ])
                gate_row = sb(st, "gate_row", [1, 2, SEQ])
                gate = sb(st, "gate", [P, TT, EXPERTS])
                gs = sb(st, "gs", [P, 6, TT, EXPERTS])
                gs1 = sb(st, "gs1", [P, 4, TT, 1])
                gT = sb(st, "gT", [TT * EXPERTS, P])
                th = sb(st, "th", [P, SEQ])
                hid = sb(st, "hid", [P, SEQ])
                lgT = th[0:EXPERTS, :]
                hid_h = sb(st, "hid_h", [P, SEQ], F32R)
                hid_l = sb(st, "hid_l", [P, SEQ], F32R)
                ystats = (sb(st, "ybn2", [P, TT, 6]), sb(st, "yag2", [P, TT, 2]), sb(st, "yrs2", [P, 2, TT]))
                row_dma = dma_lane("s_gate_row")

                w1, w3, w2, wr = get("w1", CT, 10), get("w3", CT, 10), get("w2", 10), get("router", CT)
                wlat, whq, whk, whv, wo = get("lat", CT), get("hq"), get("hk"), get("hv"), get("o", CT)
                loaded, x_done, x_final, use = {}, {}, {}, {}

                def load_x(b):
                    if b < batches:
                        loaded[b] = x_load[b % 3](lambda e: e.dma_start(x_of(b), x_mid[0][b]), x_final.get(b - 3))

                def gates(s, b, ready):
                    ops = []
                    for c in range(CT):
                        ops += three(wr[0][:, c, :], wr[1][:, c, :], yh[:, c, :], yl[:, c, :])
                    m = passes(s.pe, s.bank(0), ops, *ready, s.free.get(0))
                    m = s.act(lambda e: e.activation(lgT, s.bank(0)[0:EXPERTS, :], ACT.Identity,
                                                     bias=router_b[0:EXPERTS, 0:1]), m, m_rb, use.get("th"))
                    s.free[0] = m
                    s.pe.queue.wait(m, s.free.get(1))
                    for t in range(TT):
                        mk = lambda e, t=t: e.transpose(s.bank(1)[:, t * EXPERTS:(t + 1) * EXPERTS],
                                                        lgT[:, t * P:(t + 1) * P], ident[0:EXPERTS, 0:EXPERTS])
                        m = s.pe(mk) if t == TT - 1 else s.pe.silent(mk)
                    n = TT * EXPERTS
                    flat = lambda i: gs[:, i, :, :]
                    wide = lambda v: v.broadcast_to([P, TT, EXPERTS])
                    lg, top, above, equal, count, tmp = (flat(i) for i in range(6))
                    use["th"] = m
                    m = s.dve(lambda e: e.tensor_copy(lg, s.bank(1)[:, 0:n].rearrange("p (t e) -> p t e", t=TT)), m)
                    s.free[1] = m
                    for t in range(TT):
                        m2 = s.dve(lambda e, t=t: e.max(top[:, t, :], lg[:, t, :]), m)
                    second = top[:, :, 1:2]
                    m = s.dve(lambda e: e.tensor_tensor(above, lg, wide(second), ALU.is_gt), m2)
                    m = s.dve(lambda e: e.tensor_tensor(equal, lg, wide(second), ALU.is_equal), m)
                    m = s.dve(lambda e: e.tensor_reduce(gs1[:, 0, :, :], above, AX.X, ALU.add), m)
                    src = equal
                    bufs = [count, tmp]
                    for i, step in enumerate((1, 2, 4)):
                        dst = bufs[i % 2]
                        m = s.dve(lambda e, dst=dst, src=src, step=step: e.tensor_copy(dst[:, :, 0:step], src[:, :, 0:step]), m)
                        m = s.dve(lambda e, dst=dst, src=src, step=step: e.tensor_tensor(
                            dst[:, :, step:EXPERTS], src[:, :, step:EXPERTS], src[:, :, 0:EXPERTS - step], ALU.add), m)
                        src = dst
                    m = s.dve(lambda e, src=src: e.tensor_tensor(tmp, src, wide(gs1[:, 0, :, :]), ALU.add), m)
                    m = s.dve(lambda e: e.tensor_scalar(tmp, tmp, 2.5, None, ALU.is_lt), m)
                    m = s.dve(lambda e: e.tensor_tensor(tmp, tmp, equal, ALU.mult), m)
                    m = s.dve(lambda e: e.tensor_tensor(tmp, tmp, above, ALU.add), m)
                    m = s.dve(lambda e: e.tensor_tensor(lg, lg, wide(top[:, :, 0:1]), ALU.subtract), m)
                    a = s.act(lambda e: e.activation(gate[:, :, :], lg, ACT.Exp), m, use.get("gate"))
                    m = s.dve(lambda e: e.tensor_tensor(gate[:, :, :], gate[:, :, :], tmp, ALU.mult), a)
                    m = s.dve(lambda e: e.tensor_reduce(gs1[:, 1, :, :], gate[:, :, :], AX.X, ALU.add), m)
                    m = s.dve(lambda e: e.reciprocal(gs1[:, 2, :, :], gs1[:, 1, :, :]), m)
                    m = s.dve(lambda e: e.tensor_tensor(gate[:, :, :], gate[:, :, :], wide(gs1[:, 2, :, :]), ALU.mult), m)
                    m = s.pe(lambda e: e.transpose(s.bank(0)[0:n, 0:P], gate[:, :, :].rearrange("p t e -> p (t e)"),
                                                   ident[:, :]), m, s.free.get(0))
                    use["gate"] = m
                    a = s.act(lambda e: e.activation(gT[:, :], s.bank(0)[0:n, 0:P], ACT.Copy, scale=0.5), m, use.get("gT"))
                    s.free[0] = a
                    return a

                def spread_gates(s, pair, ready):
                    for t in range(TT):
                        at = t * EXPERTS + 2 * pair
                        m = row_dma(lambda e, t=t, at=at: e.dma_start(gate_row[0:1, :, t * P:(t + 1) * P],
                                                                      gT[at:at + 2, :]), ready, use.get("gate_row"))
                    use["gT"] = m
                    use["gate_row"] = s.pool(lambda e: e.partition_broadcast(
                        gate_of[:, pair % 2, :, :].rearrange("p e t -> p (e t)"),
                        gate_row[:, :, :].rearrange("p e t -> p (e t)")), m, use.get(("gate_of", pair % 2)))
                    return use["gate_row"]

                def experts(b):
                    s = Y
                    x = x_of(b)
                    ready = to_channels(s, x, yh, yl, loaded[b], use.get("yh"))
                    yield 2500.0
                    gate_rows = gates(s, b, ready)
                    gated = {pair: spread_gates(s, pair, gate_rows) for pair in range(2)}
                    yield 8000.0
                    for i in range(SHARED + EXPERTS):
                        for w, bank in ((w1, 0), (w3, 1)):
                            ops = []
                            for c in range(CT):
                                ops += three(w[0][:, c, i, :], w[1][:, c, i, :], yh[:, c, :], yl[:, c, :])
                            m = passes(s.pe, s.bank(bank), ops, *ready, s.free.get(bank))
                            if bank == 0:
                                a = s.act(lambda e: e.activation(th[:, :], s.bank(0), ACT.Tanh, scale=0.5), m, use.get("th"))
                                d = s.dve(lambda e: e.scalar_tensor_tensor(out=hid[:, :], in0=th[:, :], scalar=1.0,
                                                                           in1=s.bank(0), op0=ALU.add, op1=ALU.mult),
                                          a, use.get("hid"))
                                use["th"] = s.free[0] = d
                                yield 1500.0
                        use["yh"] = m
                        d = s.dve(lambda e: e.tensor_tensor(hid[:, :], hid[:, :], s.bank(1), ALU.mult), m, d)
                        s.free[1] = d
                        half = 0.5
                        if i >= SHARED:
                            pair, odd = divmod(i - SHARED, 2)
                            d = s.pool(lambda e, pair=pair, odd=odd: e.tensor_tensor(
                                hid[:, :], hid[:, :], gate_of[:, pair % 2, odd, :], ALU.mult), d, gated[pair])
                            use["gate_of", pair % 2] = d
                            if odd and pair < 2:
                                gated[pair + 2] = spread_gates(s, pair + 2, gate_rows)
                            half = 1.0
                        a = s.act(lambda e, half=half: e.activation(hid_h[:, :], hid[:, :], ACT.Copy, scale=half), d,
                                  use.get("hid_pe"))
                        if i < SHARED:
                            d = s.dve(lambda e: e.scalar_tensor_tensor(
                                out=hid_l[:, :], in0=hid[:, :], scalar=0.5, in1=hid_h[:, :].bitcast(F32),
                                op0=ALU.mult, op1=ALU.subtract), a)
                        else:
                            d = s.dve(lambda e: e.tensor_tensor(hid_l[:, :], hid[:, :], hid_h[:, :].bitcast(F32),
                                                                 ALU.subtract), a)
                        use["hid"] = d
                        for c in range(CT):
                            cols = slice(c * P, (c + 1) * P)
                            m = passes(s.pe, s.bank(2 + c), three(w2[0][:, i, cols], w2[1][:, i, cols],
                                                                  hid_h[:, :], hid_l[:, :]),
                                       a, d, s.free.get(2 + c) if i == 0 else None, start=(i == 0),
                                       stop=(i == SHARED + EXPERTS - 1))
                        use["hid_pe"] = m
                        yield 2600.0
                    end = back_to_tokens(s, (th[:, :], hid[:, :]), m, (use["th"], use["hid"]))
                    x_done[b] = layernorm(s, x, ystats, end)
                    yield 6000.0

                def attn1(b):
                    s = X
                    x = x_of(b)
                    ready = to_channels(s, x, att.xh, att.xl, x_done[b], att.mark.get("x_use"))
                    yield 2500.0
                    m1 = s.pool(lambda e: e.tensor_tensor(x, x, proj_b[:, :].unsqueeze(1).broadcast_to([P, TT, DIM]),
                                                          ALU.add), *ready, m_pb, s.pe.now)
                    for half in range(1):
                        lat = []
                        for which in range(2 if half == 0 else 1):
                            ops = []
                            for c in range(CT):
                                cols = slice(which * P, which * P + P)
                                ops += three(wlat[0][:, c, cols], wlat[1][:, c, cols], att.xh[:, c, :], att.xl[:, c, :])
                            m = passes(s.pe, s.bank(which), ops, *ready, s.free.get(which))
                            a, d = split_psum(s, s.bank(which), lats[which][:, 0, :], lats[which][:, 1, :], m,
                                              use.get(("lat", which)), att.mark.get("parts_free"))
                            s.free[which] = d
                            lat += [a, d]
                            if which == 1:
                                att.mark["x_use"] = m
                            yield 1500.0
                        if True:
                            s.pe.queue.wait(*lat, s.free.get(0), s.free.get(1))
                            for t in range(TT):
                                dst = s.bank(t // 2)[:, (t % 2) * DIM:(t % 2 + 1) * DIM]
                                rows = slice(t * P, (t + 1) * P)
                                m = passes(s.pe, dst, three(lats[1][:, 0, rows], lats[1][:, 1, rows], whv[0], whv[1]))
                            use["lat", 1] = m
                            for i in range(2):
                                v_ready = s.act(lambda e, i=i: e.activation(
                                    att.v[:, 2 * i:2 * i + 2, :, 0:HDIM],
                                    s.bank(i).rearrange("p (t h d) -> p t h d", t=2, d=HDIM), ACT.Copy),
                                    m, att.mark.get("v_use"), att.v_ones)
                            s.free[0] = s.free[1] = v_ready
                            yield 2500.0
                    v_read = use["lat", 1]
                    for half in range(2):
                        split = []
                        for which, wh in ((0, whq), (1, whk)):
                            cols = slice(half * P, half * P + P)
                            m = passes(s.pe, s.bank(which), three(wh[0][:, cols], wh[1][:, cols], lats[0][:, 0, :],
                                                                  lats[0][:, 1, :]), *lat, s.free.get(which))
                            a, d = split_psum(s, s.bank(which), att.parts[:, which, 0, :], att.parts[:, which, 1, :],
                                              m, att.mark.get("parts_free"), v_read, scale=SCALE if which == 0 else 1.0)
                            s.free[which] = d
                            split += [a, d]
                            use["lat", 0] = m
                        att.send(b, half, split)
                        yield 1500.0
                        yield from att.scores_max(half)
                        yield from att.attend(half, v_ready)
                    end = att.project(wo, x, m1)
                    x_final[b] = x_store[b % 3](lambda e: e.dma_start(x_mid[1][b], x), end)
                    yield 9000.0

                lats = [sb(st, "lat", [P, 2, SEQ], F32R), att.parts[:, 1, :, :]]
                for b in range(2):
                    load_x(b)
                for b in range(batches + 1):
                    merge(attn1(b - 1) if b > 0 else iter(()), experts(b) if b < batches else iter(()))
                    load_x(b + 2)
                barrier()

        def phase3():
            with ExitStack() as st:
                X, Y = Stream(3, "x", 0), Stream(3, "y", 4)
                for s in (X, Y):
                    lanes_seen.extend([s.pe, s.dve, s.act, s.pool])
                cq_b, m_qb = columns(st, "cq_b", CT)
                ck_b, m_kb = columns(st, "ck_b", CT)
                cv_b, m_vb = columns(st, "cv_b", CT)
                co_b, m_ob = bias_rows(st, "co_b")
                f2_b, m_fb = bias_rows(st, "f2_b")
                ff_c, m_fc = columns(st, "ff_c", 4 * FT)
                fc = sb(st, "fc", [P, 12, FT])
                keys_all = BATCH * CTX
                a_h = sb(st, "a_h", [P, CT, keys_all], F32R)
                a_l = sb(st, "a_l", [P, CT, keys_all], F32R)
                v_h = sb(st, "v_h", [P, CT, BATCH, 2, CTX], F32R)
                v_l = sb(st, "v_l", [P, CT, BATCH, 2, CTX], F32R)
                q_bias = sb(st, "q_bias", [P, keys_all])
                seen = sb(st, "seen", [P, keys_all])
                unseen = sb(st, "unseen", [P, keys_all])
                get, stage_ctx, wm = load_weights(st, 3)
                stage = lambda name, shape, dt=F32: stage_ctx.enter_context(nc.sbuf_tensor(name, shape, dt))
                ctx_st = stage("ctx_st3", [P, CT, keys_all])
                ctx_h = stage("ctx_h3", [P, CT, keys_all], F32R)
                ctx_l = stage("ctx_l3", [P, CT, keys_all], F32R)
                k_h = stage("k_h3", [P, CT, keys_all], F32R)
                k_l = stage("k_l3", [P, CT, keys_all], F32R)
                tile32 = stage("tile32", [P, 512])
                bq = stage("bq", [P, CT, P])
                bq_h = stage("bq_h", [P, CT, P], F32R)
                bq_l = stage("bq_l", [P, CT, P], F32R)
                mask_i = stage("mask_i", [P, keys_all], I32)
                small = dma_lane("s_small3")
                small(lambda e: e.dma_start(mask_i[:, :], dram["mask_i"].partition_broadcast(P)))
                m_ctx = small(lambda e: e.dma_start(ctx_st[:, :, :], dram["ctxT"]))
                a = Y.act(lambda e: e.activation(ctx_h[:, :, :], ctx_st[:, :, :], ACT.Copy), m_ctx)
                m_ctx = Y.dve(lambda e: e.tensor_tensor(ctx_l[:, :, :], ctx_st[:, :, :], ctx_h[:, :, :].bitcast(F32),
                                                        ALU.subtract), a)
                m = Y.dve(lambda e: e.tensor_scalar(seen[:, :], mask_i[:, :], 0.0, None, ALU.not_equal), small.now)
                Y.dve(lambda e: e.tensor_scalar(unseen[:, :], seen[:, :], 10000.0, -10000.0, ALU.mult, ALU.add), m)
                m = Y.dve(lambda e: e.tensor_copy(bq[:, :, :], cq_b[:, :].unsqueeze(2).broadcast_to([P, CT, P])), m_qb)
                a = Y.act(lambda e: e.activation(bq_h[:, :, :], bq[:, :, :], ACT.Copy), m)
                m_bq = Y.dve(lambda e: e.tensor_tensor(bq_l[:, :, :], bq[:, :, :], bq_h[:, :, :].bitcast(F32),
                                                       ALU.subtract), a)
                Y.pe.queue.wait(wm[0], wm[1])

                def all_keys(w, hi_in, lo_in, store, bias, *after):
                    for mt in range(CT):
                        for n in range(2):
                            cols = slice(n * 512, n * 512 + 512)
                            ops = []
                            for c in range(CT):
                                ops += three(w[0][:, c, mt * P:(mt + 1) * P], w[1][:, c, mt * P:(mt + 1) * P],
                                             hi_in[:, c, cols], lo_in[:, c, cols])
                            m = passes(Y.pe, Y.bank(0), ops, Y.free.get(0), *after)
                            m = Y.act(lambda e, mt=mt: e.activation(
                                tile32[:, :], Y.bank(0), ACT.Identity,
                                bias=0.0 if bias is None else bias[:, mt:mt + 1]), m, Y.free.get("tile"))
                            Y.free[0] = m
                            done = store(mt, n, cols, m)
                            Y.free["tile"] = done
                    return done

                def store_split(hi, lo):
                    def store(mt, n, cols, m):
                        a = Y.act(lambda e: e.activation(hi[:, mt, cols], tile32[:, :], ACT.Copy), m)
                        return Y.dve(lambda e: e.tensor_tensor(lo[:, mt, cols], tile32[:, :],
                                                               hi[:, mt, cols].bitcast(F32), ALU.subtract), a)
                    return store

                def store_twice(mt, n, cols, m):
                    rows = slice(n * 8, n * 8 + 8)
                    t3 = tile32[:, :].rearrange("p (b k) -> p b k", k=CTX)
                    for i in range(2):
                        a = Y.act(lambda e, i=i: e.activation(v_h[:, mt, rows, i, :], t3, ACT.Copy), m)
                        d = Y.dve(lambda e, i=i: e.tensor_tensor(v_l[:, mt, rows, i, :], t3,
                                                                 v_h[:, mt, rows, i, :].bitcast(F32), ALU.subtract), a)
                    return d

                k_ready = all_keys(get("xk", CT), ctx_h, ctx_l, store_split(k_h, k_l), ck_b, m_ctx, m_kb)
                all_keys(get("xv", CT), k_h, k_l, store_twice, cv_b, k_ready, m_vb)
                all_keys(get("xqT", CT), k_h, k_l, store_split(a_h, a_l), None, k_ready)
                for n in range(2):
                    cols = slice(n * 512, n * 512 + 512)
                    ops = []
                    for c in range(CT):
                        ops += three(bq_h[:, c, :], bq_l[:, c, :], k_h[:, c, cols], k_l[:, c, cols])
                    m = passes(Y.pe, Y.bank(0), ops, Y.free.get(0), m_bq)
                    Y.free[0] = Y.act(lambda e, cols=cols: e.activation(q_bias[:, cols], Y.bank(0), ACT.Copy), m)

                phase_c, real_c, imag_c, b1_c = (ff_c[:, i * FT:(i + 1) * FT] for i in range(4))
                col = lambda i: fc[:, i, :]
                turns, angle, frac, sin_c, cos_c, amp, shift = (col(i) for i in range(7))

                def ts(out_ap, in_ap, s1, s2, op0, op1, *after):
                    return Y.dve(lambda e: e.tensor_scalar(out_ap, in_ap, s1, s2, op0, op1), *after)

                def tt(out_ap, a_ap, b_ap, op, *after):
                    return Y.dve(lambda e: e.tensor_tensor(out_ap, a_ap, b_ap, op), *after)

                m = ts(turns, phase_c, INV_2PI, ROUND, ALU.mult, ALU.add, m_fc)
                m = ts(turns, turns, -ROUND, None, ALU.add, ALU.bypass, m)
                src = phase_c
                for part in (PI_A, PI_B, PI_C):
                    m = ts(col(8), turns, -part, None, ALU.mult, ALU.bypass, m)
                    m = tt(angle, src, col(8), ALU.add, m)
                    src = angle
                m = ts(frac, angle, INV_2PI, None, ALU.mult, ALU.bypass, m)
                for quarter, res in ((0.0, sin_c), (0.25, cos_c)):
                    m = ts(col(8), frac, quarter, None, ALU.add, ALU.bypass, m)
                    m = ts(col(9), col(8), ROUND, None, ALU.add, ALU.bypass, m)
                    m = ts(col(9), col(9), -ROUND, None, ALU.add, ALU.bypass, m)
                    m = tt(col(8), col(8), col(9), ALU.subtract, m)
                    m = Y.act(lambda e, res=res: e.activation(res, col(8), ACT.Sin, scale=TWO_PI), m)
                m = tt(cos_c, cos_c, real_c, ALU.mult, m)
                m = tt(sin_c, sin_c, imag_c, ALU.mult, m)
                m = tt(amp, cos_c, sin_c, ALU.add, m)
                m = tt(amp, amp, imag_c, ALU.mult, m)
                m = ts(amp, amp, 0.1, None, ALU.mult, ALU.bypass, m)
                m = ts(col(8), b1_c, 0.1, None, ALU.mult, ALU.bypass, m)
                m = tt(shift, angle, col(8), ALU.add, m)
                m = ts(shift, shift, INV_2PI, None, ALU.mult, ALU.bypass, m)
                barrier()
                stage_ctx.close()

                xh = sb(st, "xh3", [P, CT, SEQ], F32R)
                xl = sb(st, "xl3", [P, CT, SEQ], F32R)
                sc = sb(st, "sc3", [P, TT, CTX])
                st1 = sb(st, "st3", [P, 3, TT, 1])
                p2 = sb(st, "p2", [P, TT, 2, CTX])
                pT = sb(st, "pT", [P, SEQ], F32R)
                vw_h = sb(st, "vw_h", [P, DIM], F32R)
                vw_l = sb(st, "vw_l", [P, DIM], F32R)
                xstats = (sb(st, "xbn3", [P, TT, 6]), sb(st, "xag3", [P, TT, 2]), sb(st, "xrs3", [P, 2, TT]))
                ystats = (sb(st, "ybn3", [P, TT, 6]), sb(st, "yag3", [P, TT, 2]), sb(st, "yrs3", [P, 2, TT]))
                yh = sb(st, "yh3", [P, CT, SEQ], F32R)
                yl = sb(st, "yl3", [P, CT, SEQ], F32R)
                tr = sb(st, "tr", [P, 2, SEQ])
                ang = sb(st, "ang", [P, 2, SEQ])
                act_h = sb(st, "act_h", [P, 2, SEQ], F32R)
                act_l = sb(st, "act_l", [P, 2, SEQ], F32R)
                wo, w1, w2 = get("xo", CT), get("w1", CT), get("w2", FT)
                loaded, x_done, x_final, use = {}, {}, {}, {}

                def load_x(b):
                    if b < batches:
                        loaded[b] = x_load[b % 3](lambda e: e.dma_start(x_of(b), x_mid[1][b]), x_final.get(b - 3))

                def cross1(b):
                    s = X
                    x = x_of(b)
                    keys = slice(b * CTX, (b + 1) * CTX)
                    ops = []
                    for c in range(CT):
                        ops += three(v_h[:, c, b, :, :].rearrange("p a k -> p (a k)"),
                                     v_l[:, c, b, :, :].rearrange("p a k -> p (a k)"), wo[0][:, c, :], wo[1][:, c, :])
                    m = passes(s.pe, s.bank(3)[:, 0:DIM], ops, s.free.get(3))
                    a, vw = split_psum(s, s.bank(3)[:, 0:DIM], vw_h[:, :], vw_l[:, :], m, use.get("vw"))
                    s.free[3] = vw
                    yield 1500.0
                    ready = to_channels(s, x, xh, xl, loaded[b], use.get("xh"))
                    yield 2500.0
                    xb = s.pool(lambda e: e.tensor_tensor(x, x, co_b[:, :].unsqueeze(1).broadcast_to([P, TT, DIM]),
                                                          ALU.add), *ready, m_ob, s.pe.now)
                    s.pe.queue.wait(*ready, s.free.get(2))
                    for t in range(TT):
                        rows = slice(t * P, (t + 1) * P)
                        ops = []
                        for c in range(CT):
                            ops += three(xh[:, c, rows], xl[:, c, rows], a_h[:, c, keys], a_l[:, c, keys])
                        m = passes(s.pe, s.bank(2)[:, t * CTX:(t + 1) * CTX], ops)
                    use["xh"] = m
                    key = lambda t: t[:, keys].unsqueeze(1).broadcast_to([P, TT, CTX])
                    wide = lambda i: st1[:, i, :, :].broadcast_to([P, TT, CTX])
                    m = s.dve(lambda e: e.tensor_tensor(sc[:, :, :], s.bank(2)[:, 0:TT * CTX].rearrange(
                        "p (t k) -> p t k", t=TT), key(q_bias), ALU.add), m, use.get("sc"))
                    s.free[2] = m
                    m = s.dve(lambda e: e.tensor_tensor(sc[:, :, :], sc[:, :, :], key(seen), ALU.mult), m)
                    m = s.dve(lambda e: e.tensor_tensor(sc[:, :, :], sc[:, :, :], key(unseen), ALU.add), m)
                    m = s.dve(lambda e: e.tensor_reduce(st1[:, 0, :, :], sc[:, :, :], AX.X, ALU.max), m)
                    m = s.dve(lambda e: e.tensor_tensor(sc[:, :, :], sc[:, :, :], wide(0), ALU.subtract), m)
                    m = s.act(lambda e: e.activation(sc[:, :, :], sc[:, :, :], ACT.Exp), m)
                    m = s.dve(lambda e: e.tensor_reduce(st1[:, 1, :, :], sc[:, :, :], AX.X, ALU.add), m)
                    m = s.dve(lambda e: e.reciprocal(st1[:, 2, :, :], st1[:, 1, :, :]), m)
                    m = s.dve(lambda e: e.tensor_tensor(sc[:, :, :], sc[:, :, :], wide(2), ALU.mult), m)
                    m = s.dve(lambda e: e.tensor_copy(p2[:, :, 0, :].bitcast(F32R), sc[:, :, :]), m, use.get("p2"))
                    m = s.dve(lambda e: e.tensor_tensor(p2[:, :, 1, :].bitcast(F32R), sc[:, :, :], p2[:, :, 0, :],
                                                        ALU.subtract), m)
                    yield 4000.0
                    s.pe.queue.wait(m, s.free.get(3))
                    for t in range(TT):
                        mk = lambda e, t=t: e.transpose(s.bank(3)[:, t * P:(t + 1) * P],
                                                        p2[:, t, :, :].rearrange("p a k -> p (a k)"), ident[:, :])
                        m = s.pe(mk) if t == TT - 1 else s.pe.silent(mk)
                    use["p2"] = m
                    a = s.act(lambda e: e.activation(pT[:, :], s.bank(3), ACT.Copy), m, use.get("pT"))
                    s.free[3] = a
                    s.pe.queue.wait(a, vw, s.free.get(0), s.free.get(1))
                    for t in range(TT):
                        rows = slice(t * P, (t + 1) * P)
                        m = passes(s.pe, s.bank(t // 2)[:, (t % 2) * DIM:(t % 2 + 1) * DIM],
                                   [(pT[:, rows], vw_h[:, :]), (pT[:, rows], vw_l[:, :])])
                    use["pT"] = use["vw"] = m
                    yield 3000.0
                    x_done[b] = layernorm(s, x, xstats, m, xb)
                    yield 6000.0

                def feed_forward(b):
                    s = Y
                    x = x_of(b)
                    ready = to_channels(s, x, yh, yl, x_done[b], use.get("yh"))
                    yield 2500.0
                    xb = s.pool(lambda e: e.tensor_tensor(x, x, f2_b[:, :].unsqueeze(1).broadcast_to([P, TT, DIM]),
                                                          ALU.add), *ready, m_fb, s.pe.now)

                    def up(i):
                        k = i % 2
                        ops = []
                        for c in range(CT):
                            cols = slice(i * P, (i + 1) * P)
                            ops += three(w1[0][:, c, cols], w1[1][:, c, cols], yh[:, c, :], yl[:, c, :])
                        m = passes(s.pe, s.bank(k), ops, *ready, s.free.get(k))
                        use["yh"] = m
                        c1 = 0.1 * INV_2PI
                        a = s.act(lambda e: e.activation(ang[:, k, :], s.bank(k), ACT.Identity, scale=c1,
                                                         bias=shift[:, i:i + 1]), m, use.get(("ang", k)))
                        d = s.dve(lambda e: e.tensor_scalar(tr[:, k, :], ang[:, k, :], ROUND, None, ALU.add), a,
                                  use.get(("tr", k)))
                        d = s.dve(lambda e: e.scalar_tensor_tensor(out=ang[:, k, :], in0=tr[:, k, :], scalar=ROUND,
                                                                   in1=ang[:, k, :], op0=ALU.subtract,
                                                                   op1=ALU.subtract), d)
                        a = s.act(lambda e: e.activation(tr[:, k, :], ang[:, k, :], ACT.Sin, scale=-TWO_PI), d)
                        d = s.dve(lambda e: e.scalar_tensor_tensor(out=ang[:, k, :], in0=tr[:, k, :],
                                                                   scalar=amp[:, i:i + 1], in1=s.bank(k),
                                                                   op0=ALU.mult, op1=ALU.add), a)
                        use["tr", k] = s.free[k] = d
                        d = s.dve(lambda e: e.tensor_scalar(ang[:, k, :], ang[:, k, :], b1_c[:, i:i + 1], 0.0, ALU.add,
                                                            ALU.max), d)
                        a = s.act(lambda e: e.activation(act_h[:, k, :], ang[:, k, :], ACT.Copy), d, use.get(("act", k)))
                        d = s.pool(lambda e: e.tensor_tensor(act_l[:, k, :], ang[:, k, :], act_h[:, k, :].bitcast(F32),
                                                             ALU.subtract), a)
                        use["ang", k] = d
                        return a, d

                    def down(i, parts):
                        k = i % 2
                        for c in range(CT):
                            cols = slice(c * P, (c + 1) * P)
                            m = passes(s.pe, s.bank(2 + c), three(w2[0][:, i, cols], w2[1][:, i, cols],
                                                                  act_h[:, k, :], act_l[:, k, :]),
                                       *parts, s.free.get(2 + c) if i == 0 else None, start=(i == 0), stop=(i == FT - 1))
                        use["act", k] = m
                        return m

                    parts = {0: up(0)}
                    for i in range(FT):
                        if i + 1 < FT:
                            parts[i + 1] = up(i + 1)
                        yield 2000.0
                        m = down(i, parts[i])
                        yield 2000.0
                    tiles = (tr[:, 0, :], tr[:, 1, :])
                    m = back_to_tokens(s, tiles, m, (use["tr", 0], use["tr", 1]))
                    use["tr", 0] = use["tr", 1] = m
                    end = layernorm(s, x, ystats, m, xb)
                    x_final[b] = x_store[b % 3](lambda e: e.dma_start(out[b].rearrange("(t p) d -> p t d", p=P), x), end)
                    yield 6000.0

                for b in range(2):
                    load_x(b)
                for b in range(batches + 1):
                    merge(cross1(b) if b < batches else iter(()), feed_forward(b - 1) if b > 0 else iter(()))
                    load_x(b + 2)
                barrier()

        for n, phase in ((1, phase1), (2, phase2), (3, phase3)):
            if n in phases:
                phase()

        block = ctx.enter_context(nc.Block())
        for engine, name in ((block.sync, "sp"), (block.tensor, "pe"), (block.vector, "dve"),
                             (block.scalar, "act"), (block.gpsimd, "pool")):
            def play(e, steps=queues[name].steps):
                for step in steps:
                    step(e)
            engine(play)


def rows_of(w):
    k, n = w.shape
    return np.ascontiguousarray(w.reshape(k // P, P, n).transpose(1, 0, 2).reshape(P, -1))


def cols_of(v):
    return np.ascontiguousarray(v.reshape(-1, P).T)


def trig_tables():
    r = HDIM // 2
    omega = 10000.0 ** (-2.0 * np.arange(r) / HDIM)
    ang = omega[:, None] * np.arange(SEQ)[None, :]
    cos, sin = np.cos(ang), np.sin(ang)
    t = np.zeros((P, 3, SEQ), np.float32)
    for block in range(3):
        at = 32 * block + HDIM
        t[at:at + r, 0], t[at:at + r, 1], t[at:at + r, 2] = cos, sin, cos
        t[at + r:at + 2 * r, 0], t[at + r:at + 2 * r, 1], t[at + r:at + 2 * r, 2] = sin, -cos, sin
    return t


def lay_out(inp):
    a = {k: np.asarray(v) for k, v in inp.items()}
    r = HDIM // 2
    qkv = a["L0_attn_Wqkv"].T
    out = {"x": a["x"], "trig": trig_tables()}
    ctx = a["ctx_1024"].reshape(BATCH * CTX, DIM).T
    out["ctxT"] = rows_of(ctx).reshape(P, CT, BATCH * CTX)
    ab = np.zeros((P, 2, HEADS), np.float32)
    for block in range(3):
        for part in range(2):
            at = 32 * block + HDIM + part * r
            ab[at:at + r, 0], ab[at:at + r, 1] = a["L0_attn_alpha"].T, a["L0_attn_beta"].T
    out["alpha_beta"] = ab
    out["head_of"] = (np.arange(P)[:, None] // HDIM == np.arange(HALF)[None, :]).astype(np.float32)
    out["mask_f"] = np.ascontiguousarray(a["mask_1x1xSxS2_fk1"].reshape(TT, P, CTX).transpose(1, 0, 2))
    out["w1"] = np.concatenate([rows_of(np.ascontiguousarray(qkv[:, 0:512])), rows_of(np.ascontiguousarray(qkv[:, 512:768])),
                                rows_of(np.ascontiguousarray(a["L0_attn_Wout"].T)), rows_of(a["L0_xattn_wq_w"]),
                                rows_of(a["L0_xattn_wk_w"]), rows_of(a["L0_xattn_wv_w"]), rows_of(a["L0_xattn_wo_w"])], 1)
    experts = lambda n, w: np.concatenate([a[f"L0_ffn_shared_w{n}"], a[f"L0_ffn_routed_w{n}"]], 0)
    wide = lambda w: rows_of(np.ascontiguousarray(w.transpose(1, 0, 2).reshape(DIM, -1)))
    pad = lambda w, top, rows=P: np.concatenate([np.zeros((top, w.shape[1]), w.dtype), w,
                                                 np.zeros((rows - top - w.shape[0], w.shape[1]), w.dtype)], 0)
    lat = np.concatenate([a["L1_attn_wq_lat"], a["L1_attn_wk_lat"], a["L1_attn_wv_lat"],
                          np.zeros((DIM, LAT), np.float32)], 1)
    router = np.concatenate([a["L0_ffn_router_w"], np.zeros((DIM, P - EXPERTS), np.float32)], 1)
    out["w2"] = np.concatenate([wide(experts(1, 0)), wide(experts(3, 0)),
                                experts(2, 0).transpose(1, 0, 2).reshape(HID, -1), rows_of(router), rows_of(lat),
                                pad(a["L1_attn_wq_heads"], 0), pad(a["L1_attn_wk_heads"], LAT),
                                pad(a["L1_attn_wv_heads"], 0), rows_of(a["L1_attn_w_proj"])], 1)
    ff = {n: a[f"L1_ffn_{n}"] for n in ("W1", "W2", "b1", "b2")}
    out["w3"] = np.concatenate([rows_of(np.ascontiguousarray(a["L1_xattn_Wq"].T)), rows_of(a["L1_xattn_Wk"]),
                                rows_of(a["L1_xattn_Wv"]), rows_of(a["L1_xattn_Wo"]), rows_of(ff["W1"]),
                                rows_of(ff["W2"])], 1)
    for name, key in (("cq_b", "bq"), ("ck_b", "bk"), ("cv_b", "bv")):
        out[name] = cols_of(a["L1_xattn_" + key])
    out["co_b"], out["f2_b"] = a["L1_xattn_bo"], ff["b2"]
    out["ff_c"] = np.concatenate([cols_of(a["L1_ffn_quantum_phases"]), cols_of(a["L1_ffn_quantum_weights_real"]),
                                  cols_of(a["L1_ffn_quantum_weights_imag"]), cols_of(ff["b1"])], 1)
    out["mask_i"] = a["mask_BxS2_ik0"].reshape(-1)
    out["proj_b"] = a["L1_attn_b_proj"]
    out["router_b"] = np.concatenate([a["L0_ffn_router_b"], np.zeros(P - EXPERTS, np.float32)]).reshape(P, 1)
    out["xq_b"], out["xk_b"] = cols_of(a["L0_xattn_wq_b"]), cols_of(a["L0_xattn_wk_b"])
    out["xv_b"], out["xo_b"] = a["L0_xattn_wv_b"], a["L0_xattn_wo_b"]
    return out


def kernel(**inputs):
    import concourse.bacc as bacc
    from concourse.bass_utils import run_bass_kernel_spmd

    nc = bacc.Bacc("TRN2", target_bir_lowering=False, num_devices=1)
    arrays = {"in_" + name: value for name, value in lay_out(inputs).items()}
    dram = {name[3:]: nc.dram_tensor(name, value.shape, mybir.dt.from_np(value.dtype), kind="ExternalInput").ap()
            for name, value in arrays.items()}
    out = nc.dram_tensor("out_dram", (BATCH, SEQ, DIM), F32, kind="ExternalOutput").ap()
    decoder(nc, dram, out)
    result = run_bass_kernel_spmd(nc, [arrays], core_ids=[0])
    return result.results[0]["out_dram"]
```

```python
from contextlib import ExitStack

import numpy as np

import concourse.bass as bass
from concourse import mybir

ALU = mybir.AluOpType
ACT = mybir.ActivationFunctionType
AX = mybir.AxisListType
F32 = mybir.dt.float32
F32R = mybir.dt.float32r
BF16 = mybir.dt.bfloat16
I32 = mybir.dt.int32

P = 128
BATCH, SEQ, DIM = 16, 512, 256
CTX = 64
HEADS, HDIM = 16, 16
GROUP = 4
HALF = HEADS // 2
TT = SEQ // P
CT = DIM // P
EXPERTS, SHARED = 8, 2
GATES = 2
DEEP = 3
ROUTER = 32
HID = 128
LAT = 64
FF = 1024
FT = FF // P
SCALE = 0.25
EPS = 1e-5
NEG = -1e9
MASKED = -1e30
TWO_PI = float(np.nextafter(np.float32(2 * np.pi), np.float32(0)))
INV_2PI = float(np.float32(1 / (2 * np.pi)))
ROUND = float(1.5 * 2 ** 23)
PI_A = 6.28125
PI_B = round((2 * np.pi - PI_A) * 2 ** 20) / 2 ** 20
PI_C = 2 * np.pi - PI_A - PI_B

PT_AT = [0, 512, 1024, 896]
PT_COLS = 1280

W_PHASE = [
    dict(qk=CT * 512, v=CT * 256, o=CT * 256, xq=CT * 256, xk=CT * 256, xv=CT * 256, xo=CT * 256),
    dict(w1=CT * 10 * HID, w3=CT * 10 * HID, w2=10 * DIM, router=CT * ROUTER, lat=CT * 256,
         hq=DIM, hk=DIM, hv=DIM, o=CT * 256),
    dict(xqT=CT * 256, xk=CT * 256, xv=CT * 256, xo=CT * 256, w1=CT * FF, w2=FT * DIM),
]


def column_starts(names):
    at, out = 0, {}
    for name, n in names.items():
        out[name] = (at, n)
        at += n
    return out, at


USUAL = dict(pe=216, dve=450, act=500, pool=900, sp=2200)
HANDOVER = dict(pe=150, dve=120, act=230, pool=150, sp=0)


class Queue:

    def __init__(self, name):
        self.name, self.steps, self.seen, self.lanes, self.clock = name, [], {}, [], 0.0

    def wait(self, *marks):
        for sem, value in marks:
            if self.seen.get(sem.name, 0) < value:
                self.seen[sem.name] = value
                self.steps.append(lambda e, s=sem, v=value: e.wait_ge(s, v))


class Lane:

    def __init__(self, queue, sem, step=1):
        self.queue, self.sem, self.step, self.count = queue, sem, step, 0
        self.waits, self.group, self.items, self.ends, self.done = [], [], [], {}, 0
        queue.lanes.append(self)

    def wait(self, *after):
        self.waits += [mark for mark in after if mark is not None]

    def silent(self, make, *after):
        self.wait(*after)
        self.group.append(make)

    def __call__(self, make, *after, ns=None):
        self.wait(*after)
        self.count += self.step
        self.group.append(lambda e: make(e).then_inc(self.sem, self.step))
        if ns is None:
            ns = USUAL[self.queue.name] * len(self.group)
        self.items.append((self.waits, self.group, self.count, ns))
        self.waits, self.group = [], []
        return (self.sem, self.count)

    @property
    def now(self):
        return (self.sem, self.count) if self.count else None


def take_turns(queues):
    lanes = [lane for q in queues.values() for lane in q.lanes]
    by_sem = {lane.sem.name: lane for lane in lanes}
    at = {id(lane): 0 for lane in lanes}
    while True:
        best = None
        for lane in lanes:
            if at[id(lane)] == len(lane.items):
                continue
            waits = lane.items[at[id(lane)]][0]
            if any(by_sem[sem.name].done < value for sem, value in waits):
                continue
            ready = max([by_sem[sem.name].ends[value] for sem, value in waits], default=0.0)
            start = max(ready, lane.queue.clock)
            if best is None or (start, ready) < best[:2]:
                best = (start, ready, lane)
        if best is None:
            break
        start, _, lane = best
        waits, group, lane.done, ns = lane.items[at[id(lane)]]
        at[id(lane)] += 1
        lane.queue.wait(*waits)
        lane.queue.steps += group
        lane.queue.clock = start + (60 if lane.queue.name == "sp" else ns)
        lane.ends[lane.done] = start + ns + HANDOVER[lane.queue.name]
    for lane in lanes:
        assert at[id(lane)] == len(lane.items) and not lane.waits and not lane.group
        lane.items = []


def decoder(nc, dram, out, batches=BATCH, phases=(1, 2, 3)):
    ctx = ExitStack()
    with ctx:
        def sem(name):
            return ctx.enter_context(nc.semaphore(name))

        queues = {n: Queue(n) for n in ("pe", "dve", "act", "pool", "sp")}

        def scratch(name, shape, dt=F32):
            return nc.dram_tensor(name, shape, dt, kind="Internal").ap()

        x_mid = [scratch(f"x_mid{n}", (BATCH, P, TT, DIM)) for n in range(2)]
        kt_scratch = scratch("kt_scratch", (P, 2, CT, BATCH * CTX))
        ctx_scratch = scratch("ctx_scratch", (P, 2, CT, BATCH * CTX))
        gate_scratch = scratch("gate_scratch", (2, TT * EXPERTS, P))
        qk_scratch = scratch("qk_scratch", (2, 2, P, 2, 2, SEQ))

        ps = ctx.enter_context(nc.psum_tensor("ps", [P, 8, 512], F32))

        def sb(stack, name, shape, dt=F32):
            return stack.enter_context(nc.sbuf_tensor(name, shape, dt))

        ident = sb(ctx, "ident", [P, P])
        ident_b = sb(ctx, "ident_b", [P, P], BF16)
        future = sb(ctx, "future", [P, P], BF16)
        mhalf = sb(ctx, "mhalf", [P, TT])
        x_ring = sb(ctx, "x_ring", [P, 3, TT, DIM])

        s_const = sem("s_const")
        const = Lane(queues["pool"], s_const)

        class Stream:

            def __init__(self, phase, name, bank0):
                self.bank0 = bank0
                self.pe = Lane(queues["pe"], sem(f"s{phase}{name}_pe"))
                self.dve = Lane(queues["dve"], sem(f"s{phase}{name}_dve"))
                self.act = Lane(queues["act"], sem(f"s{phase}{name}_act"))
                self.pool = Lane(queues["pool"], sem(f"s{phase}{name}_pool"))
                self.free, self.turns = {}, 0

            def turn(self):
                self.turns += 1
                return self.turns % 2

            def bank(self, i, n=1):
                b = self.bank0 + i
                return ps[:, b, :] if n == 1 else ps[:, b:b + n, :].rearrange("p a b -> p (a b)")


        def dma_lane(name, queue="sp"):
            lane = Lane(queues[queue], sem(name), 16)
            return lane

        def barrier():
            take_turns(queues)
            marks = [lane.now for q in queues.values() for lane in q.lanes if lane.count]
            for q in queues.values():
                q.wait(*marks)

        zero_b = const(lambda e: e.memset(ident_b[:, :], 0.0))
        zero = const(lambda e: e.memset(ident[:, :], 0.0))
        zero_u = const(lambda e: e.memset(future[:, :], 0.0))
        const(lambda e: e.memset(mhalf[:, :], -0.5))
        for t, mark in ((ident_b, zero_b), (ident, zero)):
            const(lambda e, t=t: e.affine_select(out=t[:, :], in_=t[:, :], compare_op=ALU.not_equal, fill=1.0,
                                                 base=0, pattern=[[-1, P]], channel_multiplier=1), mark)
        const(lambda e: e.affine_select(out=future[:, :], in_=future[:, :], compare_op=ALU.is_ge, fill=MASKED,
                                        base=0, pattern=[[-1, P]], channel_multiplier=1), zero_u)

        def passes(pe, out_ap, operands, *after, start=True, stop=True, check=True):
            pe.wait(*after)
            for i, (lhs, rhs) in enumerate(operands):
                first, last = start and i == 0, stop and i == len(operands) - 1

                def make(e, lhs=lhs, rhs=rhs, first=first, last=last):
                    return e.matmul(out_ap, lhs, rhs, start=first, stop=last, skip_group_check=not check)
                if i == len(operands) - 1:
                    return pe(make)
                pe.silent(make)

        def three(lh, ll, rh, rl):
            return [(lh, rh), (ll, rh), (lh, rl)]

        def split_psum(s, src, hi, lo, *after, scale=1.0, bias=None):
            if bias is None:
                m = s.act(lambda e: e.activation(hi, src, ACT.Copy, scale=scale), *after)
                return m, s.dve(lambda e: e.scalar_tensor_tensor(
                    out=lo, in0=src, scalar=scale, in1=hi.bitcast(F32), op0=ALU.mult, op1=ALU.subtract), m)
            m = s.act(lambda e: e.activation(hi, src, ACT.Identity, bias=bias), *after)
            return m, s.dve(lambda e: e.scalar_tensor_tensor(
                out=lo, in0=src, scalar=bias, in1=hi.bitcast(F32), op0=ALU.add, op1=ALU.subtract), m)

        def to_channels(s, tok, hi, lo, ready, buf_free):
            marks = []
            for c in range(CT):
                s.pe.wait(ready, s.free.get(c), s.free.get(c, None))
                for t in range(TT):
                    def make(e, c=c, t=t):
                        return e.transpose(s.bank(c)[:, t * P:(t + 1) * P], tok[:, t, c * P:(c + 1) * P], ident[:, :])
                    if t == TT - 1:
                        m = s.pe(make)
                    else:
                        s.pe.silent(make)
                a, d = split_psum(s, s.bank(c), hi[:, c, :], lo[:, c, :], m, buf_free)
                s.free[c] = d
                marks += [a, d]
            return marks

        def layernorm(s, x, stats, after, last_use=None):
            bn, ag, rs = stats
            add = s.dve(lambda e: e.tensor_tensor(x.rearrange("p t d -> p (t d)"), x.rearrange("p t d -> p (t d)"),
                                                  s.bank(0, 2), ALU.add), after, last_use)
            s.free[0] = s.free[1] = add
            for t in range(TT):
                m = s.dve(lambda e, t=t: e.bn_stats(bn[:, t, :], x[:, t, :]), add)
            for t in range(TT):
                m2 = s.dve(lambda e, t=t: e.bn_aggr(ag[:, t, :], bn[:, t, :]), m)
            m = s.dve(lambda e: e.tensor_scalar(rs[:, 0, :], ag[:, :, 1], EPS, None, ALU.add), m2)
            m = s.pool(lambda e: e.tensor_tensor(rs[:, 1, :], rs[:, 0, :], mhalf[:, :], ALU.pow), m, const.now)
            for t in range(TT):
                end = s.dve(lambda e, t=t: e.tensor_scalar(x[:, t, :], x[:, t, :], ag[:, t, 0:1], rs[:, 1, t:t + 1],
                                                           ALU.subtract, ALU.mult), m)
            return end

        def load_weights(stack, phase):
            starts, cols = column_starts(W_PHASE[phase - 1])
            hi = sb(stack, f"w{phase}_hi", [P, cols], F32R)
            lo = sb(stack, f"w{phase}_lo", [P, cols], F32R)
            step = 1024
            stage_ctx = ExitStack()
            stage = stage_ctx.enter_context(nc.sbuf_tensor(f"w{phase}_stage", [P, 2, step], F32))
            load = [dma_lane(f"s_w{phase}_{n}") for n in range(2)]
            dve = Lane(queues["dve"], sem(f"s_ws{phase}"))
            act = Lane(queues["act"], sem(f"s_wa{phase}"))
            free = [None, None]
            for i, at in enumerate(range(0, cols, step)):
                n, b = min(step, cols - at), i % 2
                m = load[b](lambda e, at=at, n=n, b=b: e.dma_start(stage[:, b, 0:n], dram[f"w{phase}"][:, at:at + n]),
                            free[b])
                a = act(lambda e, at=at, n=n, b=b: e.activation(hi[:, at:at + n], stage[:, b, 0:n], ACT.Copy), m)
                free[b] = dve(lambda e, at=at, n=n, b=b: e.tensor_tensor(
                    lo[:, at:at + n], stage[:, b, 0:n], hi[:, at:at + n].bitcast(F32), ALU.subtract), a)

            def get(name, *dims):
                at, n = starts[name]
                views = [t[:, at:at + n] for t in (hi, lo)]
                if len(dims) == 1:
                    return [v.rearrange("p (a b) -> p a b", a=dims[0]) for v in views]
                if len(dims) == 2:
                    return [v.rearrange("p (a b c) -> p a b c", a=dims[0], b=dims[1]) for v in views]
                return views
            return get, stage_ctx, free

        class Attention:

            def __init__(self, stack, m, a, phase, sets):
                self.m, self.a, self.sets, self.phase = m, a, sets, phase
                self.q = sb(stack, f"q_stack{phase}", [P, sets * GROUP, SEQ], F32R)
                self.k = sb(stack, f"k_stack{phase}", [P, sets * GROUP, SEQ], F32R)
                self.out_dma = dma_lane(f"s_qk_out{phase}")
                self.in_dma = [dma_lane(f"s_qk_in{phase}_{n}") for n in range(sets)]
                self.max_dma = [dma_lane(f"s_max{phase}_{n}") for n in range(2)]
                self.use = [None] * sets
                self.mark = {}

            def buffers(self, stack):
                phase = self.phase
                self.v = sb(stack, f"v_ones{phase}", [P, TT, HEADS + 1, HDIM + 1])
                self.pt = sb(stack, f"pt{phase}", [P, GROUP, PT_COLS])
                self.xh = sb(stack, f"xh{phase}", [P, CT, SEQ], F32R)
                self.xl = sb(stack, f"xl{phase}", [P, CT, SEQ], F32R)
                self.oh = sb(stack, f"oh{phase}", [P, CT, SEQ], F32R)
                self.ol = sb(stack, f"ol{phase}", [P, CT, SEQ], F32R)
                self.parts = sb(stack, f"parts{phase}", [P, 2, 2, SEQ], F32R)
                self.nmax = sb(stack, f"nmax{phase}", [P, 2, GROUP, TT])
                self.nmaxT = sb(stack, f"nmaxT{phase}", [GROUP * TT, P], F32R)
                self.oT = self.pt[:, 0, 0:SEQ]
                self.o = sb(stack, f"o{phase}", [P, TT, DIM])
                self.rec = sb(stack, f"rec{phase}", [P, TT, GROUP, 1])
                self.stats = (sb(stack, f"bn{phase}", [P, TT, 6]), sb(stack, f"ag{phase}", [P, TT, 2]),
                              sb(stack, f"rs{phase}", [P, 2, TT]))
                self.v_ones = self.m.pool(lambda e: e.memset(self.v[:, :, :, :], 1.0))

            def setup(self):
                s = self.m
                m = s.pool(lambda e: e.memset(self.k[:, :, :].bitcast(F32), 0.0))
                m = s.pool(lambda e: e.memset(self.k[96:97, :, :].bitcast(F32), 1.0), m, const.now)
                s.pool(lambda e: e.memset(self.q[:, :, :].bitcast(F32), 0.0), m)
                return s.pool.now

            def send(self, b, half, split):
                home = qk_scratch[b % 2, half]
                self.mark["parts_free"] = self.mark["home", half] = self.out_dma(
                    lambda e: e.dma_start(home, self.parts[:, :, :, :].bitcast(F32)), *split,
                    *self.mark.get(("home_use", b % 2, half), []))
                self.mark["home_use", b % 2, half] = []

            def load_rows(self, b, group):
                half, at = group // 2, (group % 2) * GROUP * HDIM
                home = qk_scratch[b % 2, half]
                base = (group % self.sets) * GROUP
                lane = self.in_dma[group % self.sets]
                for block, qpart, kpart in ((0, 0, 0), (1, 0, 1), (2, 1, 0)):
                    for stack_t, which, part in ((self.q, 0, qpart), (self.k, 1, kpart)):
                        src = home[at:at + GROUP * HDIM, which, part, :].rearrange("(h d) t -> d h t", d=HDIM)
                        dst = stack_t[32 * block:32 * block + HDIM, base:base + GROUP, :].bitcast(F32)
                        m = lane(lambda e, dst=dst, src=src: e.dma_start(dst, src), self.mark["home", half],
                                 self.use[group % self.sets])
                self.mark["rows"] = m
                self.mark["home_use", b % 2, half].append(m)

            def scores_max(self, group):
                s = self.m
                base, k = (group % self.sets) * GROUP, group % 2
                nmax = self.nmax[:, k, :, :]
                for pair in range(0, GROUP, 2):
                    for unit in (((0, 3, 0),), ((0, 2, 0), (0, 0, 384)), ((1, 3, 0),), ((1, 2, 0), (1, 0, 384)),
                                 ((0, 1, 0), (1, 1, 256))):
                        i = s.turn()
                        s.pe.wait(self.mark["rows"], s.free.get(i), const.now)
                        for n, (h, t, col) in enumerate(unit):
                            slot, width = base + pair + h, (t + 1) * P
                            dst = s.bank(i)[:, col:col + width]
                            s.pe.silent(lambda e, dst=dst, t=t, width=width, slot=slot: e.matmul(
                                dst, self.q[0:96, slot, t * P:(t + 1) * P], self.k[0:96, slot, 0:width],
                                start=True, stop=False))
                            mk = lambda e, dst=dst, width=width: e.matmul(dst[:, width - P:width], ident_b[:, :],
                                                                          future[:, :], start=False, stop=True)
                            m = s.pe(mk, ns=350 * len(unit)) if n == len(unit) - 1 else s.pe.silent(mk)
                        if len(unit) == 2 and unit[0][1] == unit[1][1]:
                            d = s.dve(lambda e, i=i, pair=pair, nmax=nmax: e.tensor_reduce(
                                nmax[:, pair:pair + 2, 1], s.bank(i).rearrange("p (h k) -> p h k", h=2), AX.X, ALU.max,
                                negate=True), m, self.mark.get(("nmax", k)), ns=600)
                        else:
                            for h, t, col in unit:
                                d = s.dve(lambda e, h=h, t=t, pair=pair, nmax=nmax, src=s.bank(i)[:, col:col + (t + 1) * P]:
                                          e.tensor_reduce(nmax[:, pair + h, t:t + 1], src, AX.X, ALU.max, negate=True),
                                          m, self.mark.get(("nmax", k)), ns=70 + 133 * (t + 1))
                        s.free[i] = d
                rows, i = GROUP * TT, s.turn()
                m = s.pe(lambda e: e.transpose(s.bank(i)[0:rows, 0:P], nmax.rearrange("p h t -> p (h t)"), ident[:, :]),
                         d, s.free.get(i))
                self.mark["nmax", k] = m
                a = s.act(lambda e: e.activation(self.nmaxT[:, :], s.bank(i)[0:rows, 0:P], ACT.Copy), m,
                          self.mark.get(("max_row", 1 - k)), ns=200)
                s.free[i] = a
                dst = self.q[96:97, base:base + GROUP, :].bitcast(F32).rearrange("p h (t q) -> p (h t) q", q=P)
                self.mark["max_row", k] = self.max_dma[k](
                    lambda e: e.dma_start(dst, self.nmaxT[:, :].bitcast(F32)), a)

            def attend(self, group, v_ready):
                s = self.a
                base = (group % self.sets) * GROUP
                selected = []
                for pair in range(0, GROUP, 2):
                    for unit, at in ((((0, 0, 0),), 0), (((0, 1, 0), (0, 3, 384)), 512), (((1, 0, 0),), 0),
                                     (((1, 1, 0), (1, 3, 384)), 512), (((0, 2, 0), (1, 2, 256)), 1024)):
                        i = s.turn()
                        s.pe.wait(self.mark["max_row", group % 2], s.free.get(i))
                        for n, (h, j, col) in enumerate(unit):
                            slot = base + pair + h
                            mk = lambda e, i=i, j=j, slot=slot, col=col: e.matmul(
                                s.bank(i)[:, col:col + SEQ - j * P], self.k[:, slot, j * P:(j + 1) * P],
                                self.q[:, slot, j * P:SEQ], start=True, stop=True)
                            m = s.pe(mk) if n == len(unit) - 1 else s.pe.silent(mk)
                        if at == 1024:
                            src = s.bank(i).rearrange("p (h k) -> p h k", h=2)
                            dst = self.pt[:, pair:pair + 2, at:at + 256]
                        else:
                            src, dst = s.bank(i), self.pt[:, pair + unit[0][0], at:at + 512]
                        a = s.act(lambda e, src=src, dst=dst: e.activation(dst, src, ACT.Exp), m, self.mark.get("pt"))
                        s.free[i] = a
                    self.use[group % self.sets] = m
                    for at in (0, 512, 896, 1024):
                        blk = self.pt[:, pair:pair + 2, at:at + P]
                        selected.append(s.pool(lambda e, blk=blk: e.affine_select(
                            out=blk, in_=blk, compare_op=ALU.is_ge, fill=0.0, base=0,
                            pattern=[[0, 2], [1, P]], channel_multiplier=-1), a, ns=300))
                i = s.turn()
                s.pe.wait(v_ready, s.free.get(i), *selected)
                for j in range(TT):
                    for g in range(GROUP):
                        h = group * GROUP + g
                        cols = slice(h * (HDIM + 1), h * (HDIM + 1) + 32)
                        mk = lambda e, i=i, j=j, g=g, cols=cols: e.matmul(
                            s.bank(i)[32 * g:32 * g + 32, j * P:SEQ],
                            self.v[:, j, :, :].rearrange("p h d -> p (h d)")[:, cols],
                            self.pt[:, g, PT_AT[j]:PT_AT[j] + SEQ - j * P], start=(j == 0), stop=(j == TT - 1))
                        m = s.pe(mk, ns=2600) if (j, g) == (TT - 1, GROUP - 1) else s.pe.silent(mk)
                self.mark["v_use"] = m
                a = s.act(lambda e, i=i: e.activation(self.oT, s.bank(i), ACT.Copy), m)
                s.free[i] = a
                i = s.turn()
                s.pe.wait(a, s.free.get(i))
                for t in range(TT):
                    mk = lambda e, i=i, t=t: e.transpose(s.bank(i)[:, t * P:(t + 1) * P],
                                                         self.oT[:, t * P:(t + 1) * P], ident[:, :])
                    m = s.pe(mk) if t == TT - 1 else s.pe.silent(mk)
                self.mark["pt"] = m
                ov = s.bank(i).rearrange("p (t g d) -> p t g d", t=TT, g=GROUP)
                d = s.dve(lambda e: e.reciprocal(self.rec[:, :, :, :], ov[:, :, :, HDIM:HDIM + 1]), m, ns=190)
                at = group * GROUP * HDIM
                for t in range(TT):
                    d2 = s.dve(lambda e, t=t: e.tensor_tensor(
                        self.o[:, t, at:at + GROUP * HDIM].rearrange("p (g d) -> p g d", g=GROUP),
                        ov[:, t, :, 0:HDIM], self.rec[:, t, :, :].broadcast_to([P, GROUP, HDIM]), ALU.mult),
                        d, self.mark.get("o"), ns=130)
                s.free[i] = d2
                self.mark["o_ready"] = d2

            def project(self, w, x, bias):
                s = self.a
                marks = to_channels(s, self.o[:, :, :], self.oh, self.ol, self.mark["o_ready"], self.mark.get("o_use"))
                self.mark["o"] = s.pe.now
                m = token_major(s, self.oh, self.ol, w, marks)
                self.mark["o_use"] = m
                return layernorm(s, x, self.stats, m, bias)

        def token_major(s, ah, al, w, ready, also=()):
            s.pe.wait(*ready, s.free.get(0), s.free.get(1))
            for t in range(TT):
                dst = s.bank(t // 2)[:, (t % 2) * DIM:(t % 2 + 1) * DIM]
                ops = []
                for c in range(CT):
                    ops += three(ah[:, c, t * P:(t + 1) * P], al[:, c, t * P:(t + 1) * P], w[0][:, c, :], w[1][:, c, :])
                m = passes(s.pe, dst, ops)
            return m

        def store_v(s, att, m):
            for i in range(2):
                v_ready = s.act(lambda e, i=i: e.activation(
                    att.v[:, 2 * i:2 * i + 2, 0:HEADS, 0:HDIM],
                    s.bank(i).rearrange("p (t h d) -> p t h d", t=2, d=HDIM), ACT.Copy),
                    m, att.mark.get("v_use"), att.v_ones)
            s.free[0] = s.free[1] = v_ready
            return v_ready

        def back_to_tokens(s, tiles, m, free):
            for c in range(CT):
                a = s.act(lambda e, c=c: e.activation(tiles[c], s.bank(c), ACT.Copy), m, *free)
            s.pe.wait(a)
            for t in range(TT):
                for c in range(CT):
                    at = (t % 2) * DIM + c * P
                    mk = lambda e, t=t, c=c, at=at: e.transpose(s.bank(t // 2)[:, at:at + P],
                                                                tiles[c][:, t * P:(t + 1) * P], ident[:, :])
                    m = s.pe(mk) if (t, c) == (TT - 1, CT - 1) else s.pe.silent(mk)
            return m

        def bias_rows(stack, name):
            t = sb(stack, name + "_rows", [P, DIM])
            lane = dma_lane("s_" + name)
            m = lane(lambda e: e.dma_start(t[:, :], dram[name].partition_broadcast(P)))
            return t, m

        def columns(stack, name, n):
            t = sb(stack, name + "_cols", [P, n])
            lane = dma_lane("s_" + name)
            m = lane(lambda e: e.dma_start(t[:, :], dram[name]))
            return t, m

        x_load = [dma_lane(f"s_x{n}") for n in range(3)]
        x_store = [dma_lane(f"s_xs{n}") for n in range(3)]
        x_of = lambda b: x_ring[:, b % 3, :, :]

        def phase1():
            with ExitStack() as st:
                X, A, Y = Stream(1, "x", 0), Stream(1, "a", 2), Stream(1, "y", 4)
                tiles = [Stream(1, f"t{n}", 4) for n in range(2)]
                for s in tiles:
                    s.free = Y.free
                att = Attention(st, X, A, 1, HEADS // GROUP)
                xq_b, m_qb = columns(st, "xq_b", CT)
                xk_b, m_kb = columns(st, "xk_b", CT)
                xv_b, m_vb = bias_rows(st, "xv_b")
                xo_b, m_ob = bias_rows(st, "xo_b")
                nmask = sb(st, "nmask", [P, TT, CTX])
                head_of = sb(st, "head_of", [P, HALF])
                get, stage_ctx, wm = load_weights(st, 1)
                trig = stage_ctx.enter_context(nc.sbuf_tensor("trig", [P, 3, SEQ], F32))
                four = stage_ctx.enter_context(nc.sbuf_tensor("four", [P, 2, 2, SEQ], F32))
                fhi = stage_ctx.enter_context(nc.sbuf_tensor("fhi", [P, 2, SEQ], F32R))
                ab = stage_ctx.enter_context(nc.sbuf_tensor("ab", [P, 2, HEADS], F32))
                ctx_st = stage_ctx.enter_context(nc.sbuf_tensor("ctx_st", [P, CT, BATCH * CTX], F32))
                ctx_h = stage_ctx.enter_context(nc.sbuf_tensor("ctx_h", [P, CT, BATCH * CTX], F32R))
                ctx_l = stage_ctx.enter_context(nc.sbuf_tensor("ctx_l", [P, CT, BATCH * CTX], F32R))
                kt32 = stage_ctx.enter_context(nc.sbuf_tensor("kt32", [P, 512], F32))
                kt_st = stage_ctx.enter_context(nc.sbuf_tensor("kt_st", [P, 2, 512], F32R))
                small = dma_lane("s_small1")
                small(lambda e: e.dma_start(trig[:, :, :], dram["trig"]))
                small(lambda e: e.dma_start(ab[:, :, :], dram["alpha_beta"]))
                m_nm = small(lambda e: e.dma_start(nmask[:, :, :], dram["mask_f"]))
                m_small = small(lambda e: e.dma_start(head_of[:, :], dram["head_of"]))
                m_ctx = small(lambda e: e.dma_start(ctx_st[:, :, :], dram["ctxT"]))
                zeroed = att.setup()
                m_nm = Y.dve(lambda e: e.tensor_scalar(nmask[:, :, :], nmask[:, :, :], NEG, None, ALU.mult), m_ctx)
                m = X.act(lambda e: e.activation(fhi[:, 0, :], trig[:, 2, :], ACT.Copy), m_ctx)
                m = X.dve(lambda e: e.tensor_tensor(four[:, 0, 0, :], trig[:, 2, :], fhi[:, 0, :].bitcast(F32),
                                                    ALU.subtract), m)
                for h in range(HEADS):
                    for blk, src in ((0, fhi[:, 0, :]), (1, four[:, 0, 0, :]), (2, fhi[:, 0, :])):
                        lane = X.act if blk == 1 else X.pool
                        r = slice(32 * blk, 32 * blk + 32)
                        if blk == 1:
                            kq = X.act(lambda e, h=h, r=r, src=src: e.activation(att.k[r, h, :], src[r], ACT.Copy),
                                       m, zeroed)
                        else:
                            kq = X.act(lambda e, h=h, r=r, src=src: e.activation(
                                att.k[r, h, :], src[r].bitcast(F32), ACT.Copy), m, zeroed)
                last = [kq, kq]
                for h in range(HEADS):
                    i = h % 2
                    m = X.dve(lambda e, h=h, i=i: e.tensor_scalar(four[:, i, 0, :], trig[:, 0, :], ab[:, 0, h:h + 1],
                                                                  None, ALU.mult), last[i])
                    m = X.dve(lambda e, h=h, i=i: e.scalar_tensor_tensor(
                        out=four[:, i, 1, :], in0=trig[:, 1, :], scalar=ab[:, 1, h:h + 1], in1=four[:, i, 0, :],
                        op0=ALU.mult, op1=ALU.add), m)
                    a = X.act(lambda e, h=h, i=i: e.activation(fhi[:, i, :], four[:, i, 1, :], ACT.Copy), m)
                    X.act(lambda e, h=h, i=i: e.activation(att.q[0:64, h, :], fhi[0:64, i, :].bitcast(F32), ACT.Copy), a, zeroed)
                    last[i] = X.dve(lambda e, h=h, i=i: e.tensor_tensor(
                        att.q[64:96, h, :], four[64:96, i, 1, :], fhi[64:96, i, :].bitcast(F32), ALU.subtract), a)
                a = Y.act(lambda e: e.activation(ctx_h[:, :, :], ctx_st[:, :, :], ACT.Copy), m_ctx)
                m_ctx2 = Y.dve(lambda e: e.tensor_tensor(ctx_l[:, :, :], ctx_st[:, :, :], ctx_h[:, :, :].bitcast(F32),
                                                         ALU.subtract), a)
                Y.pe.wait(wm[0], wm[1])
                wxk = get("xk", CT)
                m_bias = Y.dve(lambda e: e.tensor_scalar(xk_b[:, :], xk_b[:, :], SCALE, None, ALU.mult), m_kb)
                kt_out = dma_lane("s_kt_out")
                for mt in range(CT):
                    for n in range(2):
                        ops = []
                        cols = slice(n * 512, n * 512 + 512)
                        for c in range(CT):
                            ops += three(wxk[0][:, c, mt * P:(mt + 1) * P], wxk[1][:, c, mt * P:(mt + 1) * P],
                                         ctx_h[:, c, cols], ctx_l[:, c, cols])
                        m = passes(Y.pe, Y.bank(0), ops, Y.free.get(0), m_ctx2)
                        m = Y.act(lambda e, mt=mt: e.activation(kt32[:, :], Y.bank(0), ACT.Identity,
                                                                bias=xk_b[:, mt:mt + 1], scale=SCALE),
                                  m, m_bias, Y.free.get("kt32"))
                        Y.free[0] = m
                        a = Y.act(lambda e: e.activation(kt_st[:, 0, :], kt32[:, :], ACT.Copy), m, kt_out.now)
                        Y.free["kt32"] = Y.dve(lambda e: e.tensor_tensor(
                            kt_st[:, 1, :], kt32[:, :], kt_st[:, 0, :].bitcast(F32), ALU.subtract), a, kt_out.now)
                        for part in range(2):
                            kt_out(lambda e, mt=mt, cols=cols, part=part: e.dma_start(
                                kt_scratch[:, part, mt, cols], kt_st[:, part, :].bitcast(F32)), a, Y.free["kt32"])
                for part, t in ((0, ctx_h), (1, ctx_l)):
                    kt_out(lambda e, part=part, t=t: e.dma_start(ctx_scratch[:, part, :, :], t[:, :, :].bitcast(F32)), m_ctx2)
                barrier()
                stage_ctx.close()
                att.buffers(st)

                yh = sb(st, "yh", [P, CT, SEQ], F32R)
                yl = sb(st, "yl", [P, CT, SEQ], F32R)
                qx_h = sb(st, "qx_h", [P, CT, SEQ], F32R)
                qx_l = sb(st, "qx_l", [P, CT, SEQ], F32R)
                kc = sb(st, "kc", [P, 2, CT, CTX], F32R)
                cc = sb(st, "cc", [P, 2, CT, 2, CTX], F32R)
                kc_load = dma_lane("s_kc")
                km_h = sb(st, "km_h", [P, CT, HALF, CTX], F32R)
                km_l = sb(st, "km_l", [P, CT, HALF, CTX], F32R)
                vx = sb(st, "vx", [P, HALF, 32])
                sc = sb(st, "sc", [P, 2, HALF, CTX])
                mx = sb(st, "mx", [P, 2, 3, HALF, 1])
                ptx = sb(st, "ptx", [P, 4, SEQ])
                ystats = (sb(st, "ybn", [P, TT, 6]), sb(st, "yag", [P, TT, 2]), sb(st, "yrs", [P, 2, TT]))
                m_vz = Y.pool(lambda e: e.memset(vx[:, :, :], 0.0))

                wqk, wv, wo = get("qk", CT), get("v", CT), get("o", CT)
                loaded, x_done, x_final = {}, {}, {}

                def load_x(b):
                    if b < batches:
                        loaded[b] = x_load[b % 3](lambda e: e.dma_start(
                            x_of(b), dram["x"][b].rearrange("(t p) d -> p t d", p=P)),
                            x_final.get(b - 3), x_done.get(b - 3))

                def attn0(b):
                    s = X
                    x = x_of(b)
                    ready = to_channels(s, x, att.xh, att.xl, loaded[b], att.mark.get("x_use"))
                    x_read = s.pe.now
                    for half in range(2):
                        split = []
                        for which in range(2):
                            mcol = which * 256 + half * P
                            ops = []
                            for c in range(CT):
                                ops += three(wqk[0][:, c, mcol:mcol + P], wqk[1][:, c, mcol:mcol + P],
                                             att.xh[:, c, :], att.xl[:, c, :])
                            m = passes(s.pe, s.bank(which), ops, *ready, s.free.get(which))
                            a, d = split_psum(s, s.bank(which), att.parts[:, which, 0, :], att.parts[:, which, 1, :],
                                              m, att.mark.get("parts_free"), scale=SCALE if which == 0 else 1.0)
                            s.free[which] = d
                            split += [a, d]
                        att.send(b, half, split)
                    for group in range(HEADS // GROUP):
                        att.load_rows(b, group)
                        att.scores_max(group)
                        if group == 0:
                            m = token_major(s, att.xh, att.xl, wv, ready)
                            att.mark["x_use"] = m
                            v_ready = store_v(s, att, m)
                        att.attend(group, v_ready)
                    x_done[b] = att.project(wo, x, x_read)

                wxq, wxv, wxo = get("xq", CT), get("xv", CT), get("xo", CT)
                use = {}

                def cross0(b):
                    s = Y
                    x = x_of(b)
                    keys = slice(b * CTX, (b + 1) * CTX)
                    kc_load(lambda e: e.dma_start(kc[:, :, :, :].bitcast(F32), kt_scratch[:, :, :, keys]), use.get("kc"),
                            use.get("kc_pe"))
                    for part in range(2):
                        for twice in range(2):
                            kc_ready = kc_load(lambda e, part=part, twice=twice: e.dma_start(
                                cc[:, part, :, twice, :].bitcast(F32), ctx_scratch[:, part, :, keys]))
                    for part, src in ((km_h, kc[:, 0, :, :]), (km_l, kc[:, 1, :, :])):
                        for c in range(CT):
                            km = s.pool(lambda e, part=part, src=src, c=c: e.tensor_tensor(
                                part[:, c, :, :], src[:, c, :].bitcast(F32).unsqueeze(1).broadcast_to([P, HALF, CTX]),
                                head_of[:, :].unsqueeze(2).broadcast_to([P, HALF, CTX]), ALU.mult),
                                kc_ready, m_small, use.get("km"))
                    use["kc"] = km
                    ops = []
                    for c in range(CT):
                        ch = cc[:, 0, c, :, :].rearrange("p a k -> p (a k)")
                        cl = cc[:, 1, c, :, :].rearrange("p a k -> p (a k)")
                        ops += three(ch, cl, wxv[0][:, c, :], wxv[1][:, c, :])
                    m = use["kc_pe"] = passes(s.pe, s.bank(2)[:, 0:DIM], ops, s.free.get(2), kc_ready)
                    for odd in range(2):
                        r = slice(64 * odd, 64 * odd + 64)
                        vm = s.dve(lambda e, r=r, odd=odd: e.tensor_tensor(
                            vx[r, :, 16 * odd:16 * odd + 16],
                            s.bank(2)[r, 0:DIM].rearrange("p (a o d) -> p a o d", o=2, d=HDIM)[:, :, odd, :],
                            xv_b[r, :].rearrange("p (a o d) -> p a o d", o=2, d=HDIM)[:, :, odd, :], ALU.add),
                            m, m_vb, m_vz, use.get("vx"))
                    s.free[2] = vm
                    ready = to_channels(s, x, yh, yl, x_done[b], use.get("yh"))
                    qm = []
                    for mt in range(CT):
                        ops = []
                        for c in range(CT):
                            ops += three(wxq[0][:, c, mt * P:(mt + 1) * P], wxq[1][:, c, mt * P:(mt + 1) * P],
                                         yh[:, c, :], yl[:, c, :])
                        m = passes(s.pe, s.bank(mt), ops, *ready, s.free.get(mt))
                        a, d = split_psum(s, s.bank(mt), qx_h[:, mt, :], qx_l[:, mt, :], m, use.get("qx"),
                                          m_qb, bias=xq_b[:, mt:mt + 1])
                        s.free[mt] = d
                        qm += [a, d]
                    use["yh"] = m
                    xb = s.pool(lambda e: e.tensor_tensor(x, x, xo_b[:, :].unsqueeze(1).broadcast_to([P, TT, DIM]),
                                                          ALU.add), *ready, m_ob, s.pe.now)
                    om = []
                    for c in range(CT):
                        copied = [None, None]
                        for t in range(TT):
                            i = t % 2
                            s = tiles[i]
                            rows = slice(t * P, (t + 1) * P)
                            kmv = [part[:, c, :, :].rearrange("p h k -> p (h k)") for part in (km_h, km_l)]
                            m = passes(s.pe, s.bank(2 + i), three(qx_h[:, c, rows], qx_l[:, c, rows], kmv[0], kmv[1]),
                                       *qm, km, s.free.get(2 + i))
                            use["qx"] = use["km"] = m
                            d = s.dve(lambda e, i=i, t=t: e.tensor_tensor(
                                sc[:, i, :, :], s.bank(2 + i).rearrange("p (h k) -> p h k", h=HALF),
                                nmask[:, t, :].unsqueeze(1).broadcast_to([P, HALF, CTX]), ALU.add),
                                m, m_nm, use.get(("sc", i)))
                            s.free[2 + i] = d
                            d = s.dve(lambda e, i=i: e.tensor_reduce(mx[:, i, 0, :, :], sc[:, i, :, :], AX.X, ALU.max), d,
                                      use.get(("sc", i)))
                            d = s.pool(lambda e, i=i: e.tensor_tensor(
                                sc[:, i, :, :], sc[:, i, :, :], mx[:, i, 0, :, :].broadcast_to([P, HALF, CTX]),
                                ALU.subtract), d)
                            a = s.act(lambda e, i=i: e.activation(sc[:, i, :, :], sc[:, i, :, :], ACT.Exp), d)
                            d = s.dve(lambda e, i=i: e.tensor_reduce(mx[:, i, 1, :, :], sc[:, i, :, :], AX.X, ALU.add), a)
                            d = s.dve(lambda e, i=i: e.reciprocal(mx[:, i, 2, :, :], mx[:, i, 1, :, :]), d)
                            d = s.pool(lambda e, i=i: e.tensor_tensor(
                                sc[:, i, :, :], sc[:, i, :, :], mx[:, i, 2, :, :].broadcast_to([P, HALF, CTX]),
                                ALU.mult), d)
                            s.pe.wait(d, s.free.get(i))
                            for p in range(4):
                                mk = lambda e, i=i, p=p: e.transpose(
                                    s.bank(i)[:, p * P:(p + 1) * P],
                                    sc[:, i, 2 * p:2 * p + 2, :].rearrange("p h k -> p (h k)"), ident[:, :])
                                m = s.pe(mk) if p == 3 else s.pe.silent(mk)
                            use["sc", i] = m
                            a = s.act(lambda e, i=i, c=c, rows=rows: e.activation(
                                ptx[:, :, rows], s.bank(i).rearrange("p (a q) -> p a q", a=4), ACT.Copy),
                                m, use.get("ptx"))
                            s.free[i] = copied[i] = a
                        s = Y
                        s.pe.wait(*copied, vm, s.free.get(2))
                        for p in range(4):
                            mk = lambda e, p=p, c=c: e.matmul(s.bank(2)[32 * p:32 * p + 32, :], vx[:, 4 * c + p, :],
                                                              ptx[:, p, :], start=True, stop=True)
                            m = s.pe(mk) if p == 3 else s.pe.silent(mk)
                        use["ptx"] = use["vx"] = m
                        a, d = split_psum(s, s.bank(2), yh[:, c, :], yl[:, c, :], m)
                        s.free[2] = d
                        om += [a, d]
                    m = token_major(s, yh, yl, wxo, om)
                    use["yh"] = m
                    end = layernorm(s, x, ystats, m, xb)
                    x_final[b] = x_store[b % 3](lambda e: e.dma_start(x_mid[0][b], x), end)

                for b in range(3):
                    load_x(b)
                for b in range(batches):
                    attn0(b)
                    cross0(b)
                    load_x(b + 3)
                barrier()

        def phase2():
            with ExitStack() as st:
                X, A, Y = Stream(2, "x", 0), Stream(2, "a", 2), Stream(2, "y", 4)
                gating, last = Stream(2, "g", 4), Stream(2, "f", 6)
                gating.free = Y.free
                proj_b, m_pb = bias_rows(st, "proj_b")
                router_b, m_rb = columns(st, "router_b", 1)
                att = Attention(st, X, A, 2, 2)
                get, stage_ctx, wm = load_weights(st, 2)
                zeroed = att.setup()
                barrier()
                stage_ctx.close()
                att.buffers(st)

                yh = sb(st, "yh2", [P, CT, SEQ], F32R)
                yl = sb(st, "yl2", [P, CT, SEQ], F32R)
                gate_of = sb(st, "gate_of", [P, GATES, SEQ])
                gate = sb(st, "gate", [P, TT, EXPERTS])
                gs = sb(st, "gs", [P, 6, TT, EXPERTS])
                gs1 = sb(st, "gs1", [P, 4, TT, 1])
                gT = sb(st, "gT", [TT * EXPERTS, P])
                back = sb(st, "back", [P, CT, SEQ])
                th = sb(st, "th", [P, SEQ])
                hid = sb(st, "hid", [P, SEQ])
                lgT = th[0:EXPERTS, :]
                hid_h = sb(st, "hid_h", [P, SEQ], F32R)
                hid_l = sb(st, "hid_l", [P, SEQ], F32R)
                ystats = (sb(st, "ybn2", [P, TT, 6]), sb(st, "yag2", [P, TT, 2]), sb(st, "yrs2", [P, 2, TT]))
                gate_out = dma_lane("s_gate_out")
                gate_dma = [dma_lane(f"s_gate{n}") for n in range(GATES)]

                w1, w3, w2, wr = get("w1", CT, 10), get("w3", CT, 10), get("w2", 10), get("router", CT)
                wlat, whq, whk, whv, wo = get("lat", CT), get("hq"), get("hk"), get("hv"), get("o", CT)
                loaded, x_done, x_final, use = {}, {}, {}, {}

                def load_x(b):
                    if b < batches:
                        loaded[b] = x_load[b % 3](lambda e: e.dma_start(x_of(b), x_mid[0][b]), x_final.get(b - 3))

                def gates(s, b, ready):
                    ops = []
                    for c in range(CT):
                        ops += three(wr[0][:, c, :], wr[1][:, c, :], yh[:, c, :], yl[:, c, :])
                    m = passes(s.pe, s.bank(0)[0:ROUTER, :], ops, *ready, s.free.get(0))
                    m = s.act(lambda e: e.activation(lgT, s.bank(0)[0:EXPERTS, :], ACT.Identity,
                                                     bias=router_b[0:EXPERTS, 0:1]), m, m_rb, use.get("th"))
                    s.free[0] = m
                    s.pe.wait(m, s.free.get(1))
                    for t in range(TT):
                        mk = lambda e, t=t: e.transpose(s.bank(1)[:, t * EXPERTS:(t + 1) * EXPERTS],
                                                        lgT[:, t * P:(t + 1) * P], ident[0:EXPERTS, 0:EXPERTS])
                        m = s.pe(mk) if t == TT - 1 else s.pe.silent(mk)
                    n = TT * EXPERTS
                    flat = lambda i: gs[:, i, :, :]
                    wide = lambda v: v.broadcast_to([P, TT, EXPERTS])
                    lg, top, above, equal, count, tmp = (flat(i) for i in range(6))
                    use["th"] = m
                    m = s.dve(lambda e: e.tensor_copy(lg, s.bank(1)[:, 0:n].rearrange("p (t e) -> p t e", t=TT)), m)
                    s.free[1] = m
                    for t in range(TT):
                        m2 = s.dve(lambda e, t=t: e.max(top[:, t, :], lg[:, t, :]), m)
                    second = top[:, :, 1:2]
                    m = s.dve(lambda e: e.tensor_tensor(above, lg, wide(second), ALU.is_gt), m2)
                    m = s.dve(lambda e: e.tensor_tensor(equal, lg, wide(second), ALU.is_equal), m)
                    m = s.dve(lambda e: e.tensor_reduce(gs1[:, 0, :, :], above, AX.X, ALU.add), m)
                    src = equal
                    bufs = [count, tmp]
                    for i, step in enumerate((1, 2, 4)):
                        dst = bufs[i % 2]
                        m = s.dve(lambda e, dst=dst, src=src, step=step: e.tensor_copy(dst[:, :, 0:step], src[:, :, 0:step]), m)
                        m = s.dve(lambda e, dst=dst, src=src, step=step: e.tensor_tensor(
                            dst[:, :, step:EXPERTS], src[:, :, step:EXPERTS], src[:, :, 0:EXPERTS - step], ALU.add), m)
                        src = dst
                    m = s.dve(lambda e, src=src: e.tensor_tensor(tmp, src, wide(gs1[:, 0, :, :]), ALU.add), m)
                    m = s.dve(lambda e: e.tensor_scalar(tmp, tmp, 2.5, None, ALU.is_lt), m)
                    m = s.dve(lambda e: e.tensor_tensor(tmp, tmp, equal, ALU.mult), m)
                    m = s.dve(lambda e: e.tensor_tensor(tmp, tmp, above, ALU.add), m)
                    m = s.dve(lambda e: e.tensor_tensor(lg, lg, wide(top[:, :, 0:1]), ALU.subtract), m)
                    a = s.act(lambda e: e.activation(gate[:, :, :], lg, ACT.Exp), m, use.get("gate"))
                    m = s.dve(lambda e: e.tensor_tensor(gate[:, :, :], gate[:, :, :], tmp, ALU.mult), a)
                    m = s.dve(lambda e: e.tensor_reduce(gs1[:, 1, :, :], gate[:, :, :], AX.X, ALU.add), m)
                    m = s.dve(lambda e: e.reciprocal(gs1[:, 2, :, :], gs1[:, 1, :, :]), m)
                    m = s.dve(lambda e: e.tensor_tensor(gate[:, :, :], gate[:, :, :], wide(gs1[:, 2, :, :]), ALU.mult), m)

                    def to_rows():
                        end = s.pe(lambda e: e.transpose(s.bank(0)[0:n, 0:P], gate[:, :, :].rearrange("p t e -> p (t e)"),
                                                         ident[:, :]), m, s.free.get(0))
                        use["gate"] = end
                        a = s.act(lambda e: e.activation(gT[:, :], s.bank(0)[0:n, 0:P], ACT.Copy, scale=0.5), end,
                                  use.get("gT"), ns=200)
                        s.free[0] = a
                        use["gT"] = use["gate_home"] = gate_out(
                            lambda e: e.dma_start(gate_scratch[b % 2], gT[:, :]), a, *[lane.now for lane in gate_dma])
                    return to_rows

                def spread_gate(b, n):
                    row = gate_scratch[b % 2].rearrange("(t e) q -> e t q", t=TT)[n].partition_broadcast(P)
                    k = n % GATES
                    return gate_dma[k](lambda e: e.dma_start(gate_of[:, k, :].rearrange("p (t q) -> p t q", t=TT), row),
                                       use["gate_home"], use.get(("gate_of", k)))

                def experts(b):
                    s = Y
                    x = x_of(b)
                    ready = to_channels(s, x, yh, yl, loaded[b], use.get("yh"))
                    x_read = s.pe.now
                    last_gates = gates(gating, b, ready)
                    gated = {}

                    def up(i, w, bank):
                        ops = []
                        for c in range(CT):
                            ops += three(w[0][:, c, i, :], w[1][:, c, i, :], yh[:, c, :], yl[:, c, :])
                        m = use["yh"] = passes(s.pe, s.bank(bank), ops, *ready, s.free.get(bank))
                        return m

                    def hidden(i, m1, m3):
                        a = s.act(lambda e: e.activation(th[:, :], s.bank(0), ACT.Tanh, scale=0.5), m1, use.get("th"))
                        d = s.dve(lambda e: e.scalar_tensor_tensor(out=hid[:, :], in0=th[:, :], scalar=1.0,
                                                                   in1=s.bank(0), op0=ALU.add, op1=ALU.mult),
                                  a, use.get("hid"), ns=600)
                        use["th"] = s.free[0] = d
                        d = s.dve(lambda e: e.tensor_tensor(hid[:, :], hid[:, :], s.bank(1), ALU.mult), m3, d, ns=600)
                        s.free[1] = d
                        half = 0.5
                        if i >= SHARED:
                            n = i - SHARED
                            d = s.pool(lambda e, n=n: e.tensor_tensor(
                                hid[:, :], hid[:, :], gate_of[:, n % GATES, :], ALU.mult), d, gated[n], ns=1250)
                            use["gate_of", n % GATES] = d
                            if n + GATES < EXPERTS:
                                gated[n + GATES] = spread_gate(b, n + GATES)
                            half = 1.0
                        a = s.act(lambda e, half=half: e.activation(hid_h[:, :], hid[:, :], ACT.Copy, scale=half), d,
                                  use.get("hid_pe"))
                        if i < SHARED:
                            d = s.dve(lambda e: e.scalar_tensor_tensor(
                                out=hid_l[:, :], in0=hid[:, :], scalar=0.5, in1=hid_h[:, :].bitcast(F32),
                                op0=ALU.mult, op1=ALU.subtract), a)
                        else:
                            d = s.dve(lambda e: e.tensor_tensor(hid_l[:, :], hid[:, :], hid_h[:, :].bitcast(F32),
                                                                 ALU.subtract), a)
                        use["hid"] = d
                        return a, d

                    def down(i, parts):
                        for c in range(CT):
                            cols = slice(c * P, (c + 1) * P)
                            m = passes(s.pe, s.bank(2 + c), three(w2[0][:, i, cols], w2[1][:, i, cols],
                                                                  hid_h[:, :], hid_l[:, :]),
                                       *parts, last.free.get(c) if i == 0 else None, start=(i == 0),
                                       stop=(i == SHARED + EXPERTS - 1))
                        use["hid_pe"] = m
                        return m

                    n_all = SHARED + EXPERTS
                    parts = hidden(0, up(0, w1, 0), up(0, w3, 1))
                    last_gates()
                    for n in range(GATES):
                        gated[n] = spread_gate(b, n)
                    for i in range(n_all):
                        if i + 1 < n_all:
                            m1, m3 = up(i + 1, w1, 0), up(i + 1, w3, 1)
                        m = down(i, parts)
                        if i + 1 < n_all:
                            parts = hidden(i + 1, m1, m3)
                    end = back_to_tokens(last, (back[:, 0, :], back[:, 1, :]), m, (use.get("back"),))
                    use["back"] = end
                    x_done[b] = layernorm(last, x, ystats, end, x_read)

                def attn1(b):
                    s = X
                    x = x_of(b)
                    ready = to_channels(s, x, att.xh, att.xl, x_done[b], att.mark.get("x_use"))
                    m1 = s.pool(lambda e: e.tensor_tensor(x, x, proj_b[:, :].unsqueeze(1).broadcast_to([P, TT, DIM]),
                                                          ALU.add), *ready, m_pb, s.pe.now)
                    lat = []
                    for which in range(2):
                        ops = []
                        for c in range(CT):
                            cols = slice(which * P, which * P + P)
                            ops += three(wlat[0][:, c, cols], wlat[1][:, c, cols], att.xh[:, c, :], att.xl[:, c, :])
                        m = passes(s.pe, s.bank(which), ops, *ready, s.free.get(which))
                        a, d = split_psum(s, s.bank(which), lats[:, which, 0, :], lats[:, which, 1, :], m,
                                          use.get(("lat", which)))
                        s.free[which] = d
                        lat.append([a, d])
                    att.mark["x_use"] = m
                    for half in range(2):
                        split = []
                        for which, wh in ((0, whq), (1, whk)):
                            cols = slice(half * P, half * P + P)
                            m = passes(s.pe, s.bank(which), three(wh[0][:, cols], wh[1][:, cols], lats[:, 0, 0, :],
                                                                  lats[:, 0, 1, :]), *lat[0], s.free.get(which))
                            a, d = split_psum(s, s.bank(which), att.parts[:, which, 0, :], att.parts[:, which, 1, :],
                                              m, att.mark.get("parts_free"), scale=SCALE if which == 0 else 1.0)
                            s.free[which] = d
                            split += [a, d]
                        att.send(b, half, split)
                    use["lat", 0] = m
                    for group in range(HEADS // GROUP):
                        att.load_rows(b, group)
                        att.scores_max(group)
                        if group == 0:
                            s.pe.wait(*lat[1], s.free.get(0), s.free.get(1))
                            for t in range(TT):
                                dst = s.bank(t // 2)[:, (t % 2) * DIM:(t % 2 + 1) * DIM]
                                rows = slice(t * P, (t + 1) * P)
                                m = passes(s.pe, dst, three(lats[:, 1, 0, rows], lats[:, 1, 1, rows], whv[0], whv[1]))
                            use["lat", 1] = m
                            v_ready = store_v(s, att, m)
                        att.attend(group, v_ready)
                    end = att.project(wo, x, m1)
                    x_final[b] = x_store[b % 3](lambda e: e.dma_start(x_mid[1][b], x), end)

                lats = sb(st, "lats", [P, 2, 2, SEQ], F32R)
                for b in range(3):
                    load_x(b)
                for b in range(batches):
                    experts(b)
                    attn1(b)
                    load_x(b + 3)
                barrier()

        def phase3():
            with ExitStack() as st:
                X, Y, last = Stream(3, "x", 0), Stream(3, "y", 3), Stream(3, "f", 6)
                cq_b, m_qb = columns(st, "cq_b", CT)
                ck_b, m_kb = columns(st, "ck_b", CT)
                cv_b, m_vb = columns(st, "cv_b", CT)
                co_b, m_ob = bias_rows(st, "co_b")
                f2_b, m_fb = bias_rows(st, "f2_b")
                ff_c, m_fc = columns(st, "ff_c", 4 * FT)
                fc = sb(st, "fc", [P, 12, FT])
                keys_all = BATCH * CTX
                a_h = sb(st, "a_h", [P, CT, keys_all], F32R)
                a_l = sb(st, "a_l", [P, CT, keys_all], F32R)
                v_h = sb(st, "v_h", [P, CT, BATCH, 2, CTX], F32R)
                v_l = sb(st, "v_l", [P, CT, BATCH, 2, CTX], F32R)
                q_bias = sb(st, "q_bias", [P, keys_all])
                seen = sb(st, "seen", [P, keys_all])
                unseen = sb(st, "unseen", [P, keys_all])
                get, stage_ctx, wm = load_weights(st, 3)
                stage = lambda name, shape, dt=F32: stage_ctx.enter_context(nc.sbuf_tensor(name, shape, dt))
                ctx_st = stage("ctx_st3", [P, CT, keys_all])
                ctx_h = stage("ctx_h3", [P, CT, keys_all], F32R)
                ctx_l = stage("ctx_l3", [P, CT, keys_all], F32R)
                k_h = stage("k_h3", [P, CT, keys_all], F32R)
                k_l = stage("k_l3", [P, CT, keys_all], F32R)
                tile32 = stage("tile32", [P, 512])
                bq = stage("bq", [P, CT, P])
                bq_h = stage("bq_h", [P, CT, P], F32R)
                bq_l = stage("bq_l", [P, CT, P], F32R)
                mask_i = stage("mask_i", [P, keys_all], I32)
                small = dma_lane("s_small3")
                small(lambda e: e.dma_start(mask_i[:, :], dram["mask_i"].partition_broadcast(P)))
                m_ctx = small(lambda e: e.dma_start(ctx_st[:, :, :], dram["ctxT"]))
                a = Y.act(lambda e: e.activation(ctx_h[:, :, :], ctx_st[:, :, :], ACT.Copy), m_ctx)
                m_ctx = Y.dve(lambda e: e.tensor_tensor(ctx_l[:, :, :], ctx_st[:, :, :], ctx_h[:, :, :].bitcast(F32),
                                                        ALU.subtract), a)
                m = Y.dve(lambda e: e.tensor_scalar(seen[:, :], mask_i[:, :], 0.0, None, ALU.not_equal), small.now)
                Y.dve(lambda e: e.tensor_scalar(unseen[:, :], seen[:, :], 10000.0, -10000.0, ALU.mult, ALU.add), m)
                m = Y.dve(lambda e: e.tensor_copy(bq[:, :, :], cq_b[:, :].unsqueeze(2).broadcast_to([P, CT, P])), m_qb)
                a = Y.act(lambda e: e.activation(bq_h[:, :, :], bq[:, :, :], ACT.Copy), m)
                m_bq = Y.dve(lambda e: e.tensor_tensor(bq_l[:, :, :], bq[:, :, :], bq_h[:, :, :].bitcast(F32),
                                                       ALU.subtract), a)
                Y.pe.wait(wm[0], wm[1])

                def all_keys(w, hi_in, lo_in, store, bias, *after):
                    for mt in range(CT):
                        for n in range(2):
                            cols = slice(n * 512, n * 512 + 512)
                            ops = []
                            for c in range(CT):
                                ops += three(w[0][:, c, mt * P:(mt + 1) * P], w[1][:, c, mt * P:(mt + 1) * P],
                                             hi_in[:, c, cols], lo_in[:, c, cols])
                            m = passes(Y.pe, Y.bank(0), ops, Y.free.get(0), *after)
                            m = Y.act(lambda e, mt=mt: e.activation(
                                tile32[:, :], Y.bank(0), ACT.Identity,
                                bias=0.0 if bias is None else bias[:, mt:mt + 1]), m, Y.free.get("tile"))
                            Y.free[0] = m
                            done = store(mt, n, cols, m)
                            Y.free["tile"] = done
                    return done

                def store_split(hi, lo):
                    def store(mt, n, cols, m):
                        a = Y.act(lambda e: e.activation(hi[:, mt, cols], tile32[:, :], ACT.Copy), m)
                        return Y.dve(lambda e: e.tensor_tensor(lo[:, mt, cols], tile32[:, :],
                                                               hi[:, mt, cols].bitcast(F32), ALU.subtract), a)
                    return store

                def store_twice(mt, n, cols, m):
                    rows = slice(n * 8, n * 8 + 8)
                    t3 = tile32[:, :].rearrange("p (b k) -> p b k", k=CTX)
                    for i in range(2):
                        a = Y.act(lambda e, i=i: e.activation(v_h[:, mt, rows, i, :], t3, ACT.Copy), m)
                        d = Y.dve(lambda e, i=i: e.tensor_tensor(v_l[:, mt, rows, i, :], t3,
                                                                 v_h[:, mt, rows, i, :].bitcast(F32), ALU.subtract), a)
                    return d

                k_ready = all_keys(get("xk", CT), ctx_h, ctx_l, store_split(k_h, k_l), ck_b, m_ctx, m_kb)
                all_keys(get("xv", CT), k_h, k_l, store_twice, cv_b, k_ready, m_vb)
                all_keys(get("xqT", CT), k_h, k_l, store_split(a_h, a_l), None, k_ready)
                for n in range(2):
                    cols = slice(n * 512, n * 512 + 512)
                    ops = []
                    for c in range(CT):
                        ops += three(bq_h[:, c, :], bq_l[:, c, :], k_h[:, c, cols], k_l[:, c, cols])
                    m = passes(Y.pe, Y.bank(0), ops, Y.free.get(0), m_bq)
                    Y.free[0] = Y.act(lambda e, cols=cols: e.activation(q_bias[:, cols], Y.bank(0), ACT.Copy), m)

                phase_c, real_c, imag_c, b1_c = (ff_c[:, i * FT:(i + 1) * FT] for i in range(4))
                col = lambda i: fc[:, i, :]
                turns, angle, frac, sin_c, cos_c, amp, shift = (col(i) for i in range(7))

                def ts(out_ap, in_ap, s1, s2, op0, op1, *after):
                    return Y.dve(lambda e: e.tensor_scalar(out_ap, in_ap, s1, s2, op0, op1), *after)

                def tt(out_ap, a_ap, b_ap, op, *after):
                    return Y.dve(lambda e: e.tensor_tensor(out_ap, a_ap, b_ap, op), *after)

                m = ts(turns, phase_c, INV_2PI, ROUND, ALU.mult, ALU.add, m_fc)
                m = ts(turns, turns, -ROUND, None, ALU.add, ALU.bypass, m)
                src = phase_c
                for part in (PI_A, PI_B, PI_C):
                    m = ts(col(8), turns, -part, None, ALU.mult, ALU.bypass, m)
                    m = tt(angle, src, col(8), ALU.add, m)
                    src = angle
                m = ts(frac, angle, INV_2PI, None, ALU.mult, ALU.bypass, m)
                for quarter, res in ((0.0, sin_c), (0.25, cos_c)):
                    m = ts(col(8), frac, quarter, None, ALU.add, ALU.bypass, m)
                    m = ts(col(9), col(8), ROUND, None, ALU.add, ALU.bypass, m)
                    m = ts(col(9), col(9), -ROUND, None, ALU.add, ALU.bypass, m)
                    m = tt(col(8), col(8), col(9), ALU.subtract, m)
                    m = Y.act(lambda e, res=res: e.activation(res, col(8), ACT.Sin, scale=TWO_PI), m)
                m = tt(cos_c, cos_c, real_c, ALU.mult, m)
                m = tt(sin_c, sin_c, imag_c, ALU.mult, m)
                m = tt(amp, cos_c, sin_c, ALU.add, m)
                m = tt(amp, amp, imag_c, ALU.mult, m)
                m = ts(amp, amp, 0.1, None, ALU.mult, ALU.bypass, m)
                m = ts(col(8), b1_c, 0.1, None, ALU.mult, ALU.bypass, m)
                m = tt(shift, angle, col(8), ALU.add, m)
                m = ts(shift, shift, INV_2PI, None, ALU.mult, ALU.bypass, m)
                barrier()
                stage_ctx.close()

                xh = sb(st, "xh3", [P, CT, SEQ], F32R)
                xl = sb(st, "xl3", [P, CT, SEQ], F32R)
                sc = sb(st, "sc3", [P, TT, CTX])
                st1 = sb(st, "st3", [P, 3, TT, 1])
                p2 = sb(st, "p2", [P, TT, 2, CTX])
                pT = sb(st, "pT", [P, SEQ], F32R)
                vw_h = sb(st, "vw_h", [P, DIM], F32R)
                back = sb(st, "back3", [P, CT, SEQ])
                vw_l = sb(st, "vw_l", [P, DIM], F32R)
                xstats = (sb(st, "xbn3", [P, TT, 6]), sb(st, "xag3", [P, TT, 2]), sb(st, "xrs3", [P, 2, TT]))
                ystats = (sb(st, "ybn3", [P, TT, 6]), sb(st, "yag3", [P, TT, 2]), sb(st, "yrs3", [P, 2, TT]))
                yh = sb(st, "yh3", [P, CT, SEQ], F32R)
                yl = sb(st, "yl3", [P, CT, SEQ], F32R)
                tr = sb(st, "tr", [P, DEEP, SEQ])
                ang = sb(st, "ang", [P, DEEP, SEQ])
                act_h = sb(st, "act_h", [P, DEEP, SEQ], F32R)
                act_l = sb(st, "act_l", [P, DEEP, SEQ], F32R)
                wo, w1, w2 = get("xo", CT), get("w1", CT), get("w2", FT)
                loaded, x_done, x_final, use = {}, {}, {}, {}

                def load_x(b):
                    if b < batches:
                        loaded[b] = x_load[b % 3](lambda e: e.dma_start(x_of(b), x_mid[1][b]), x_final.get(b - 3))

                def cross1(b):
                    s = X
                    x = x_of(b)
                    keys = slice(b * CTX, (b + 1) * CTX)
                    ops = []
                    for c in range(CT):
                        ops += three(v_h[:, c, b, :, :].rearrange("p a k -> p (a k)"),
                                     v_l[:, c, b, :, :].rearrange("p a k -> p (a k)"), wo[0][:, c, :], wo[1][:, c, :])
                    m = passes(s.pe, s.bank(2)[:, 0:DIM], ops, s.free.get(2))
                    a, vw = split_psum(s, s.bank(2)[:, 0:DIM], vw_h[:, :], vw_l[:, :], m, use.get("vw"))
                    s.free[2] = vw
                    ready = to_channels(s, x, xh, xl, loaded[b], use.get("xh"))
                    xb = s.pool(lambda e: e.tensor_tensor(x, x, co_b[:, :].unsqueeze(1).broadcast_to([P, TT, DIM]),
                                                          ALU.add), *ready, m_ob, s.pe.now)
                    s.pe.wait(*ready, s.free.get(2))
                    for t in range(TT):
                        rows = slice(t * P, (t + 1) * P)
                        ops = []
                        for c in range(CT):
                            ops += three(xh[:, c, rows], xl[:, c, rows], a_h[:, c, keys], a_l[:, c, keys])
                        m = passes(s.pe, s.bank(2)[:, t * CTX:(t + 1) * CTX], ops)
                    use["xh"] = m
                    key = lambda t: t[:, keys].unsqueeze(1).broadcast_to([P, TT, CTX])
                    wide = lambda i: st1[:, i, :, :].broadcast_to([P, TT, CTX])
                    m = s.dve(lambda e: e.tensor_tensor(sc[:, :, :], s.bank(2)[:, 0:TT * CTX].rearrange(
                        "p (t k) -> p t k", t=TT), key(q_bias), ALU.add), m, use.get("sc"))
                    s.free[2] = m
                    m = s.dve(lambda e: e.tensor_tensor(sc[:, :, :], sc[:, :, :], key(seen), ALU.mult), m)
                    m = s.dve(lambda e: e.tensor_tensor(sc[:, :, :], sc[:, :, :], key(unseen), ALU.add), m)
                    m = s.dve(lambda e: e.tensor_reduce(st1[:, 0, :, :], sc[:, :, :], AX.X, ALU.max), m)
                    m = s.dve(lambda e: e.tensor_tensor(sc[:, :, :], sc[:, :, :], wide(0), ALU.subtract), m)
                    m = s.act(lambda e: e.activation(sc[:, :, :], sc[:, :, :], ACT.Exp), m)
                    m = s.dve(lambda e: e.tensor_reduce(st1[:, 1, :, :], sc[:, :, :], AX.X, ALU.add), m)
                    m = s.dve(lambda e: e.reciprocal(st1[:, 2, :, :], st1[:, 1, :, :]), m)
                    m = s.dve(lambda e: e.tensor_tensor(sc[:, :, :], sc[:, :, :], wide(2), ALU.mult), m)
                    m = s.dve(lambda e: e.tensor_copy(p2[:, :, 0, :].bitcast(F32R), sc[:, :, :]), m, use.get("p2"))
                    m = s.dve(lambda e: e.tensor_tensor(p2[:, :, 1, :].bitcast(F32R), sc[:, :, :], p2[:, :, 0, :],
                                                        ALU.subtract), m)
                    s.pe.wait(m, s.free.get(2))
                    for t in range(TT):
                        mk = lambda e, t=t: e.transpose(s.bank(2)[:, t * P:(t + 1) * P],
                                                        p2[:, t, :, :].rearrange("p a k -> p (a k)"), ident[:, :])
                        m = s.pe(mk) if t == TT - 1 else s.pe.silent(mk)
                    use["p2"] = m
                    a = s.act(lambda e: e.activation(pT[:, :], s.bank(2), ACT.Copy), m, use.get("pT"))
                    s.free[2] = a
                    s.pe.wait(a, vw, s.free.get(0), s.free.get(1))
                    for t in range(TT):
                        rows = slice(t * P, (t + 1) * P)
                        m = passes(s.pe, s.bank(t // 2)[:, (t % 2) * DIM:(t % 2 + 1) * DIM],
                                   [(pT[:, rows], vw_h[:, :]), (pT[:, rows], vw_l[:, :])])
                    use["pT"] = use["vw"] = m
                    x_done[b] = layernorm(s, x, xstats, m, xb)

                def feed_forward(b):
                    s = Y
                    x = x_of(b)
                    ready = to_channels(s, x, yh, yl, x_done[b], use.get("yh"))
                    xb = last.pool(lambda e: e.tensor_tensor(x, x, f2_b[:, :].unsqueeze(1).broadcast_to([P, TT, DIM]),
                                                          ALU.add), *ready, m_fb, s.pe.now)

                    def up(i):
                        k = i % DEEP
                        ops = []
                        for c in range(CT):
                            cols = slice(i * P, (i + 1) * P)
                            ops += three(w1[0][:, c, cols], w1[1][:, c, cols], yh[:, c, :], yl[:, c, :])
                        m = passes(s.pe, s.bank(k), ops, *ready, s.free.get(k))
                        use["yh"] = m
                        c1 = 0.1 * INV_2PI
                        a = s.act(lambda e: e.activation(ang[:, k, :], s.bank(k), ACT.Identity, scale=c1,
                                                         bias=shift[:, i:i + 1]), m, use.get(("ang", k)))
                        d = s.dve(lambda e: e.tensor_scalar(tr[:, k, :], ang[:, k, :], ROUND, None, ALU.add), a,
                                  use.get(("tr", k)))
                        d = s.dve(lambda e: e.scalar_tensor_tensor(out=ang[:, k, :], in0=tr[:, k, :], scalar=ROUND,
                                                                   in1=ang[:, k, :], op0=ALU.subtract,
                                                                   op1=ALU.subtract), d)
                        a = s.act(lambda e: e.activation(tr[:, k, :], ang[:, k, :], ACT.Sin, scale=-TWO_PI), d)
                        d = s.dve(lambda e: e.scalar_tensor_tensor(out=ang[:, k, :], in0=tr[:, k, :],
                                                                   scalar=amp[:, i:i + 1], in1=s.bank(k),
                                                                   op0=ALU.mult, op1=ALU.add), a)
                        use["tr", k] = s.free[k] = d
                        d = s.dve(lambda e: e.tensor_scalar(ang[:, k, :], ang[:, k, :], b1_c[:, i:i + 1], 0.0, ALU.add,
                                                            ALU.max), d)
                        a = s.act(lambda e: e.activation(act_h[:, k, :], ang[:, k, :], ACT.Copy), d, use.get(("act", k)))
                        d = s.pool(lambda e: e.tensor_tensor(act_l[:, k, :], ang[:, k, :], act_h[:, k, :].bitcast(F32),
                                                             ALU.subtract), a)
                        use["ang", k] = d
                        return a, d

                    def down(i, parts):
                        k = i % DEEP
                        for c in range(CT):
                            cols = slice(c * P, (c + 1) * P)
                            m = passes(s.pe, last.bank(c), three(w2[0][:, i, cols], w2[1][:, i, cols],
                                                                  act_h[:, k, :], act_l[:, k, :]),
                                       *parts, last.free.get(c) if i == 0 else None, start=(i == 0), stop=(i == FT - 1))
                        use["act", k] = m
                        return m

                    parts = {i: up(i) for i in range(DEEP - 1)}
                    for i in range(FT):
                        if i + DEEP - 1 < FT:
                            parts[i + DEEP - 1] = up(i + DEEP - 1)
                        m = down(i, parts[i])
                    m = use["back"] = back_to_tokens(last, (back[:, 0, :], back[:, 1, :]), m, (use.get("back"),))
                    end = layernorm(last, x, ystats, m, xb)
                    x_final[b] = x_store[b % 3](lambda e: e.dma_start(out[b].rearrange("(t p) d -> p t d", p=P), x), end)

                for b in range(3):
                    load_x(b)
                for b in range(batches):
                    cross1(b)
                    feed_forward(b)
                    load_x(b + 3)
                barrier()

        for n, phase in ((1, phase1), (2, phase2), (3, phase3)):
            if n in phases:
                phase()

        block = ctx.enter_context(nc.Block())
        for engine, name in ((block.sync, "sp"), (block.tensor, "pe"), (block.vector, "dve"),
                             (block.scalar, "act"), (block.gpsimd, "pool")):
            def play(e, steps=queues[name].steps):
                for step in steps:
                    step(e)
            engine(play)


def rows_of(w):
    k, n = w.shape
    return np.ascontiguousarray(w.reshape(k // P, P, n).transpose(1, 0, 2).reshape(P, -1))


def cols_of(v):
    return np.ascontiguousarray(v.reshape(-1, P).T)


def trig_tables():
    r = HDIM // 2
    omega = 10000.0 ** (-2.0 * np.arange(r) / HDIM)
    ang = omega[:, None] * np.arange(SEQ)[None, :]
    cos, sin = np.cos(ang), np.sin(ang)
    t = np.zeros((P, 3, SEQ), np.float32)
    for block in range(3):
        at = 32 * block + HDIM
        t[at:at + r, 0], t[at:at + r, 1], t[at:at + r, 2] = cos, sin, cos
        t[at + r:at + 2 * r, 0], t[at + r:at + 2 * r, 1], t[at + r:at + 2 * r, 2] = sin, -cos, sin
    return t


def lay_out(inp):
    a = {k: np.asarray(v) for k, v in inp.items()}
    r = HDIM // 2
    qkv = a["L0_attn_Wqkv"].T
    out = {"x": a["x"], "trig": trig_tables()}
    ctx = a["ctx_1024"].reshape(BATCH * CTX, DIM).T
    out["ctxT"] = rows_of(ctx).reshape(P, CT, BATCH * CTX)
    ab = np.zeros((P, 2, HEADS), np.float32)
    for block in range(3):
        for part in range(2):
            at = 32 * block + HDIM + part * r
            ab[at:at + r, 0], ab[at:at + r, 1] = a["L0_attn_alpha"].T, a["L0_attn_beta"].T
    out["alpha_beta"] = ab
    out["head_of"] = (np.arange(P)[:, None] // HDIM == np.arange(HALF)[None, :]).astype(np.float32)
    out["mask_f"] = np.ascontiguousarray(a["mask_1x1xSxS2_fk1"].reshape(TT, P, CTX).transpose(1, 0, 2))
    out["w1"] = np.concatenate([rows_of(np.ascontiguousarray(qkv[:, 0:512])), rows_of(np.ascontiguousarray(qkv[:, 512:768])),
                                rows_of(np.ascontiguousarray(a["L0_attn_Wout"].T)), rows_of(a["L0_xattn_wq_w"]),
                                rows_of(a["L0_xattn_wk_w"]), rows_of(a["L0_xattn_wv_w"]), rows_of(a["L0_xattn_wo_w"])], 1)
    experts = lambda n, w: np.concatenate([a[f"L0_ffn_shared_w{n}"], a[f"L0_ffn_routed_w{n}"]], 0)
    wide = lambda w: rows_of(np.ascontiguousarray(w.transpose(1, 0, 2).reshape(DIM, -1)))
    pad = lambda w, top, rows=P: np.concatenate([np.zeros((top, w.shape[1]), w.dtype), w,
                                                 np.zeros((rows - top - w.shape[0], w.shape[1]), w.dtype)], 0)
    lat = np.concatenate([a["L1_attn_wq_lat"], a["L1_attn_wk_lat"], a["L1_attn_wv_lat"],
                          np.zeros((DIM, LAT), np.float32)], 1)
    router = np.concatenate([a["L0_ffn_router_w"], np.zeros((DIM, ROUTER - EXPERTS), np.float32)], 1)
    out["w2"] = np.concatenate([wide(experts(1, 0)), wide(experts(3, 0)),
                                experts(2, 0).transpose(1, 0, 2).reshape(HID, -1), rows_of(router), rows_of(lat),
                                pad(a["L1_attn_wq_heads"], 0), pad(a["L1_attn_wk_heads"], LAT),
                                pad(a["L1_attn_wv_heads"], 0), rows_of(a["L1_attn_w_proj"])], 1)
    ff = {n: a[f"L1_ffn_{n}"] for n in ("W1", "W2", "b1", "b2")}
    out["w3"] = np.concatenate([rows_of(np.ascontiguousarray(a["L1_xattn_Wq"].T)), rows_of(a["L1_xattn_Wk"]),
                                rows_of(a["L1_xattn_Wv"]), rows_of(a["L1_xattn_Wo"]), rows_of(ff["W1"]),
                                rows_of(ff["W2"])], 1)
    for name, key in (("cq_b", "bq"), ("ck_b", "bk"), ("cv_b", "bv")):
        out[name] = cols_of(a["L1_xattn_" + key])
    out["co_b"], out["f2_b"] = a["L1_xattn_bo"], ff["b2"]
    out["ff_c"] = np.concatenate([cols_of(a["L1_ffn_quantum_phases"]), cols_of(a["L1_ffn_quantum_weights_real"]),
                                  cols_of(a["L1_ffn_quantum_weights_imag"]), cols_of(ff["b1"])], 1)
    out["mask_i"] = a["mask_BxS2_ik0"].reshape(-1)
    out["proj_b"] = a["L1_attn_b_proj"]
    out["router_b"] = np.concatenate([a["L0_ffn_router_b"], np.zeros(P - EXPERTS, np.float32)]).reshape(P, 1)
    out["xq_b"], out["xk_b"] = cols_of(a["L0_xattn_wq_b"]), cols_of(a["L0_xattn_wk_b"])
    out["xv_b"], out["xo_b"] = a["L0_xattn_wv_b"], a["L0_xattn_wo_b"]
    return out


def kernel(**inputs):
    import concourse.bacc as bacc
    from concourse.bass_utils import run_bass_kernel_spmd

    nc = bacc.Bacc("TRN2", target_bir_lowering=False, num_devices=1)
    arrays = {"in_" + name: value for name, value in lay_out(inputs).items()}
    dram = {name[3:]: nc.dram_tensor(name, value.shape, mybir.dt.from_np(value.dtype), kind="ExternalInput").ap()
            for name, value in arrays.items()}
    out = nc.dram_tensor("out_dram", (BATCH, SEQ, DIM), F32, kind="ExternalOutput").ap()
    decoder(nc, dram, out)
    result = run_bass_kernel_spmd(nc, [arrays], core_ids=[0])
    return result.results[0]["out_dram"]
```

```python
from contextlib import ExitStack

import numpy as np

import concourse.bass as bass
from concourse import mybir

ALU = mybir.AluOpType
ACT = mybir.ActivationFunctionType
AX = mybir.AxisListType
F32 = mybir.dt.float32
F32R = mybir.dt.float32r
BF16 = mybir.dt.bfloat16
I32 = mybir.dt.int32

P = 128
BATCH, SEQ, DIM = 16, 512, 256
CTX = 64
HEADS, HDIM = 16, 16
GROUP = 4
HALF = HEADS // 2
TT = SEQ // P
CT = DIM // P
EXPERTS, SHARED = 8, 2
STAGES = 4
RING = 4
GATES = 2
DEEP = 3
ROUTER = 16
HID = 128
LAT = 64
FF = 1024
FT = FF // P
SCALE = 0.25
EPS = 1e-5
NEG = -1e9
MASKED = -1e30
TWO_PI = float(np.nextafter(np.float32(2 * np.pi), np.float32(0)))
INV_2PI = float(np.float32(1 / (2 * np.pi)))
ROUND = float(1.5 * 2 ** 23)
PI_A = 6.28125
PI_B = round((2 * np.pi - PI_A) * 2 ** 20) / 2 ** 20
PI_C = 2 * np.pi - PI_A - PI_B

PT_AT = [0, 512, 1024, 896]
PT_COLS = 1280

W_PHASE = [
    dict(qk=CT * 512, v=CT * 256, o=CT * 256, xq=CT * 256, xv=CT * 256, xo=CT * 256),
    dict(w1=CT * 10 * HID, w3=CT * 10 * HID, w2=10 * DIM, router=CT * ROUTER,
         o=CT * 256),
    dict(xqT=CT * 256, xk=CT * 256, xv=CT * 256, xo=CT * 256, w1=CT * FF, w2=FT * DIM),
    dict(xk=CT * 256),
]


def column_starts(names):
    at, out = 0, {}
    for name, n in names.items():
        out[name] = (at, n)
        at += n
    return out, at


USUAL = dict(pe=100, dve=600, act=480, pool=1225, sp=2800)
HANDOVER = dict(pe=250, dve=200, act=300, pool=250, sp=0)


def product_ns(columns):
    return max(100, 42 + 0.34 * columns)


class Queue:

    def __init__(self, name, record):
        self.name, self.record = name, record
        self.steps, self.seen, self.lanes, self.clock = [], {}, [], 0.0

    def wait(self, *marks):
        for sem, value in marks:
            if self.seen.get(sem.name, 0) < value:
                self.seen[sem.name] = value
                self.steps.append(lambda e, s=sem, v=value: e.wait_ge(s, v))


class Step:

    def __init__(self, lane, waits, group, value, ns):
        self.lane, self.waits, self.group, self.value = lane, waits, group, value
        self.hold = 60 if lane.queue.name == "sp" else ns
        self.ns = ns + HANDOVER[lane.queue.name]
        self.rest = 0.0


class Lane:

    def __init__(self, queue, sem, step=1):
        self.queue, self.sem, self.step, self.count = queue, sem, step, 0
        self.waits, self.group, self.steps, self.at, self.ends, self.done = [], [], [], 0, {}, 0
        queue.lanes.append(self)

    def wait(self, *after):
        self.waits += [mark for mark in after if mark is not None]

    def silent(self, make, *after):
        self.wait(*after)
        self.group.append(make)

    def __call__(self, make, *after, ns=None):
        self.wait(*after)
        self.count += self.step
        self.group.append(lambda e: make(e).then_inc(self.sem, self.step))
        if ns is None:
            ns = USUAL[self.queue.name] * len(self.group)
        step = Step(self, self.waits, self.group, self.count, ns)
        self.steps.append(step)
        self.queue.record.append(step)
        self.waits, self.group = [], []
        return (self.sem, self.count)

    @property
    def now(self):
        return (self.sem, self.count) if self.count else None


def take_turns(queues, record):
    lanes = [lane for q in queues.values() for lane in q.lanes]
    by_sem = {lane.sem.name: lane for lane in lanes}
    by_mark = {(step.lane.sem.name, step.value): step for step in record}
    before = {}
    for lane in lanes:
        for first, second in zip(lane.steps, lane.steps[1:]):
            before[id(second)] = first
    for step in reversed(record):
        for sem, value in step.waits:
            maker = by_mark.get((sem.name, value))
            if maker is not None:
                maker.rest = max(maker.rest, maker.ns + step.rest)
        maker = before.get(id(step))
        if maker is not None:
            maker.rest = max(maker.rest, maker.hold + step.rest)
    for _ in range(len(record)):
        best = None
        for lane in lanes:
            if lane.at == len(lane.steps):
                continue
            step = lane.steps[lane.at]
            if any(by_sem[sem.name].done < value for sem, value in step.waits):
                continue
            ready = max([by_sem[sem.name].ends[value] for sem, value in step.waits], default=0.0)
            start = max(ready, lane.queue.clock)
            key = (start, -step.rest)
            if best is None or key < best[0]:
                best = (key, start, step)
        _, start, step = best
        lane = step.lane
        lane.at += 1
        lane.done = step.value
        lane.ends[step.value] = start + step.ns
        lane.queue.clock = start + step.hold
        lane.queue.wait(*step.waits)
        lane.queue.steps += step.group
    for lane in lanes:
        assert lane.at == len(lane.steps) and not lane.waits and not lane.group
        lane.steps, lane.at = [], 0
    record.clear()


def decoder(nc, dram, out, batches=BATCH, phases=(1, 2, 3)):
    ctx = ExitStack()
    with ctx:
        def sem(name):
            return ctx.enter_context(nc.semaphore(name))

        record = []
        queues = {n: Queue(n, record) for n in ("pe", "dve", "act", "pool", "sp")}

        def scratch(name, shape, dt=F32):
            return nc.dram_tensor(name, shape, dt, kind="Internal").ap()

        x_mid = [scratch(f"x_mid{n}", (BATCH, P, TT, DIM)) for n in range(2)]
        kt_scratch = scratch("kt_scratch", (P, 2, CT, BATCH * CTX))
        ctx_scratch = scratch("ctx_scratch", (P, 2, CT, BATCH * CTX))
        gate_scratch = scratch("gate_scratch", (2, TT * EXPERTS, P))
        qk_scratch = scratch("qk_scratch", (2, 2, P, 2, 2, SEQ))

        ps = ctx.enter_context(nc.psum_tensor("ps", [P, 8, 512], F32))

        def sb(stack, name, shape, dt=F32):
            return stack.enter_context(nc.sbuf_tensor(name, shape, dt))

        ident = sb(ctx, "ident", [P, P])
        future = sb(ctx, "future", [P, SEQ], BF16)
        mhalf = sb(ctx, "mhalf", [P, TT])
        x_ring = sb(ctx, "x_ring", [P, RING, TT, DIM])

        s_const = sem("s_const")
        const = Lane(queues["pool"], s_const)

        class Stream:

            def __init__(self, phase, name, bank0, banks=2):
                self.bank0, self.banks = bank0, banks
                self.pe = Lane(queues["pe"], sem(f"s{phase}{name}_pe"))
                self.dve = Lane(queues["dve"], sem(f"s{phase}{name}_dve"))
                self.act = Lane(queues["act"], sem(f"s{phase}{name}_act"))
                self.pool = Lane(queues["pool"], sem(f"s{phase}{name}_pool"))
                self.free, self.turns = {}, 0

            def turn(self):
                self.turns += 1
                return self.turns % self.banks

            def bank(self, i, n=1):
                b = self.bank0 + i
                return ps[:, b, :] if n == 1 else ps[:, b:b + n, :].rearrange("p a b -> p (a b)")


        def dma_lane(name, queue="sp"):
            lane = Lane(queues[queue], sem(name), 16)
            return lane

        def barrier():
            take_turns(queues, record)
            marks = [lane.now for q in queues.values() for lane in q.lanes if lane.count]
            for q in queues.values():
                q.wait(*marks)

        zero = const(lambda e: e.memset(ident[:, :], 0.0))
        zero_u = const(lambda e: e.memset(future[:, :], 0.0))
        const(lambda e: e.memset(mhalf[:, :], -0.5))
        const(lambda e: e.affine_select(out=ident[:, :], in_=ident[:, :], compare_op=ALU.not_equal, fill=1.0,
                                        base=0, pattern=[[-1, P]], channel_multiplier=1), zero)
        diagonal = future[:, SEQ - P:SEQ]
        const(lambda e: e.affine_select(out=diagonal, in_=diagonal, compare_op=ALU.is_ge, fill=MASKED,
                                        base=0, pattern=[[-1, P]], channel_multiplier=1), zero_u)

        def passes(pe, out_ap, operands, *after, start=True, stop=True, check=True):
            pe.wait(*after)
            for i, (lhs, rhs) in enumerate(operands):
                first, last = start and i == 0, stop and i == len(operands) - 1

                def make(e, lhs=lhs, rhs=rhs, first=first, last=last):
                    return e.matmul(out_ap, lhs, rhs, start=first, stop=last, skip_group_check=not check)
                if i == len(operands) - 1:
                    return pe(make, ns=len(operands) * product_ns(out_ap.shape[-1]))
                pe.silent(make)

        def three(lh, ll, rh, rl):
            return [(lh, rh), (ll, rh), (lh, rl)]

        def split_psum(s, src, hi, lo, *after, scale=1.0, bias=None):
            if bias is None:
                m = s.act(lambda e: e.activation(hi, src, ACT.Copy, scale=scale), *after)
                return m, s.dve(lambda e: e.scalar_tensor_tensor(
                    out=lo, in0=src, scalar=scale, in1=hi.bitcast(F32), op0=ALU.mult, op1=ALU.subtract), m)
            m = s.act(lambda e: e.activation(hi, src, ACT.Identity, bias=bias), *after)
            return m, s.dve(lambda e: e.scalar_tensor_tensor(
                out=lo, in0=src, scalar=bias, in1=hi.bitcast(F32), op0=ALU.add, op1=ALU.subtract), m)

        def to_channels(s, tok, hi, lo, ready, buf_free):
            marks = []
            for c in range(CT):
                s.pe.wait(ready, s.free.get(c))
                for t in range(TT):
                    def make(e, c=c, t=t):
                        return e.transpose(s.bank(c)[:, t * P:(t + 1) * P], tok[:, t, c * P:(c + 1) * P], ident[:, :])
                    if t == TT - 1:
                        m = s.pe(make)
                    else:
                        s.pe.silent(make)
                a, d = split_psum(s, s.bank(c), hi[:, c, :], lo[:, c, :], m, buf_free)
                s.free[c] = d
                marks += [a, d]
            return marks

        def layernorm(s, x, stats, after, last_use=None):
            bn, ag, rs = stats
            add = s.dve(lambda e: e.tensor_tensor(x.rearrange("p t d -> p (t d)"), x.rearrange("p t d -> p (t d)"),
                                                  s.bank(0, 2), ALU.add), after, last_use, ns=1130)
            s.free[0] = s.free[1] = add
            for t in range(TT):
                m = s.dve(lambda e, t=t: e.bn_stats(bn[:, t, :], x[:, t, :]), add, ns=335)
            for t in range(TT):
                m2 = s.dve(lambda e, t=t: e.bn_aggr(ag[:, t, :], bn[:, t, :]), m, ns=75)
            m = s.dve(lambda e: e.tensor_scalar(rs[:, 0, :], ag[:, :, 1], EPS, None, ALU.add), m2, ns=75)
            m = s.pool(lambda e: e.tensor_tensor(rs[:, 1, :], rs[:, 0, :], mhalf[:, :], ALU.pow), m, const.now, ns=960)
            m = s.dve(lambda e: e.scalar_tensor_tensor(out=rs[:, 2, :], in0=ag[:, :, 0], scalar=-1.0, in1=rs[:, 1, :],
                                                       op0=ALU.mult, op1=ALU.mult), m, ns=75)
            for t in range(TT):
                end = s.act(lambda e, t=t: e.activation(x[:, t, :], x[:, t, :], ACT.Identity, bias=rs[:, 2, t:t + 1],
                                                        scale=rs[:, 1, t:t + 1]), m, ns=350)
            return end

        def load_weights(stack, phase):
            starts, cols = column_starts(W_PHASE[phase - 1])
            hi = sb(stack, f"w{phase}_hi", [P, cols], F32R)
            lo = sb(stack, f"w{phase}_lo", [P, cols], F32R)
            step = 1024
            stage_ctx = ExitStack()
            stage = stage_ctx.enter_context(nc.sbuf_tensor(f"w{phase}_stage", [P, STAGES, step], F32))
            load = [dma_lane(f"s_w{phase}_{n}") for n in range(STAGES)]
            dve = Lane(queues["dve"], sem(f"s_ws{phase}"))
            act = Lane(queues["act"], sem(f"s_wa{phase}"))
            free = [None] * STAGES
            for i, at in enumerate(range(0, cols, step)):
                n, b = min(step, cols - at), i % STAGES
                m = load[b](lambda e, at=at, n=n, b=b: e.dma_start(stage[:, b, 0:n], dram[f"w{phase}"][:, at:at + n]),
                            free[b])
                a = act(lambda e, at=at, n=n, b=b: e.activation(hi[:, at:at + n], stage[:, b, 0:n], ACT.Copy), m)
                free[b] = dve(lambda e, at=at, n=n, b=b: e.tensor_tensor(
                    lo[:, at:at + n], stage[:, b, 0:n], hi[:, at:at + n].bitcast(F32), ALU.subtract), a)

            def get(name, *dims):
                at, n = starts[name]
                views = [t[:, at:at + n] for t in (hi, lo)]
                if len(dims) == 1:
                    return [v.rearrange("p (a b) -> p a b", a=dims[0]) for v in views]
                if len(dims) == 2:
                    return [v.rearrange("p (a b c) -> p a b c", a=dims[0], b=dims[1]) for v in views]
                return views
            return get, stage_ctx, free

        class Attention:

            def __init__(self, stack, m, a, o, phase, sets):
                o.free, o.turn = a.free, a.turn
                self.m, self.a, self.o_lanes, self.sets, self.phase = m, a, o, sets, phase
                self.q = sb(stack, f"q_stack{phase}", [P, sets * GROUP, SEQ], F32R)
                self.k = sb(stack, f"k_stack{phase}", [P, sets * GROUP, SEQ], F32R)
                self.out_dma = dma_lane(f"s_qk_out{phase}")
                self.in_dma = [dma_lane(f"s_qk_in{phase}_{n}") for n in range(sets)]
                self.max_dma = [dma_lane(f"s_max{phase}_{n}") for n in range(2)]
                self.use = [None] * sets
                self.mark = {}

            def buffers(self, stack):
                phase = self.phase
                self.v = sb(stack, f"v_ones{phase}", [P, TT, HEADS + 1, HDIM + 1])
                self.pt = sb(stack, f"pt{phase}", [P, GROUP, PT_COLS])
                self.xh = sb(stack, f"xh{phase}", [P, CT, SEQ], F32R)
                self.xl = sb(stack, f"xl{phase}", [P, CT, SEQ], F32R)
                self.oh = sb(stack, f"oh{phase}", [P, CT, SEQ], F32R)
                self.ol = sb(stack, f"ol{phase}", [P, CT, SEQ], F32R)
                self.parts = sb(stack, f"parts{phase}", [P, 2, 2, SEQ], F32R)
                self.nmax = sb(stack, f"nmax{phase}", [P, 2, GROUP, TT])
                self.nmaxT = sb(stack, f"nmaxT{phase}", [GROUP * TT, P], F32R)
                self.oT = sb(stack, f"oT{phase}", [P, SEQ])
                self.o = sb(stack, f"o{phase}", [P, TT, DIM])
                self.rec = sb(stack, f"rec{phase}", [P, TT, GROUP, 1])
                self.stats = (sb(stack, f"bn{phase}", [P, TT, 6]), sb(stack, f"ag{phase}", [P, TT, 2]),
                              sb(stack, f"rs{phase}", [P, 3, TT]))
                self.v_ones = self.m.pool(lambda e: e.memset(self.v[:, :, :, :], 1.0))

            def ones_row(self):
                self.m.pool(lambda e: e.memset(self.k[96:97, :, :].bitcast(F32), 1.0), const.now, self.m.pool.now)

            def no_bias_rows(self):
                s = self.m
                s.pool(lambda e: e.memset(self.k[0:96, :, :].bitcast(F32), 0.0))
                s.dve(lambda e: e.memset(self.q[0:96, :, :].bitcast(F32), 0.0))

            def send(self, b, half, split):
                home = qk_scratch[b % 2, half]
                self.mark["parts_free"] = self.mark["home", half] = self.out_dma(
                    lambda e: e.dma_start(home, self.parts[:, :, :, :].bitcast(F32)), *split,
                    *self.mark.get(("home_use", b % 2, half), []))
                self.mark["home_use", b % 2, half] = []

            def load_rows(self, b, group):
                half, at = group // 2, (group % 2) * GROUP * HDIM
                home = qk_scratch[b % 2, half]
                base = (group % self.sets) * GROUP
                lane = self.in_dma[group % self.sets]
                for block, qpart, kpart in ((0, 0, 0), (1, 0, 1), (2, 1, 0)):
                    for stack_t, which, part in ((self.q, 0, qpart), (self.k, 1, kpart)):
                        src = home[at:at + GROUP * HDIM, which, part, :].rearrange("(h d) t -> d h t", d=HDIM)
                        dst = stack_t[32 * block:32 * block + HDIM, base:base + GROUP, :].bitcast(F32)
                        m = lane(lambda e, dst=dst, src=src: e.dma_start(dst, src), self.mark["home", half],
                                 self.use[group % self.sets])
                self.mark["rows"] = m
                self.mark["home_use", b % 2, half].append(m)

            def scores_max(self, group):
                s = self.m
                base, k = (group % self.sets) * GROUP, group % 2
                nmax = self.nmax[:, k, :, :]
                for pair in range(0, GROUP, 2):
                    for unit in (((0, 3, 0),), ((0, 2, 0), (0, 0, 384)), ((1, 3, 0),), ((1, 2, 0), (1, 0, 384)),
                                 ((0, 1, 0), (1, 1, 256))):
                        i = s.turn()
                        s.pe.wait(self.mark["rows"], s.free.get(i), const.now)
                        unit_ns = sum(product_ns((t + 1) * P) for _, t, _ in unit)
                        for n, (h, t, col) in enumerate(unit):
                            slot, width = base + pair + h, (t + 1) * P
                            mk = lambda e, dst=s.bank(i)[:, col:col + width], t=t, width=width, slot=slot: e.matmul(
                                dst, self.q[0:96, slot, t * P:(t + 1) * P], self.k[0:96, slot, 0:width],
                                start=True, stop=True)
                            m = s.pe(mk, ns=unit_ns) if n == len(unit) - 1 else s.pe.silent(mk)
                        for h, t, col in unit:
                            width = (t + 1) * P
                            d = s.dve(lambda e, h=h, t=t, pair=pair, width=width, src=s.bank(i)[:, col:col + width]:
                                      e.tensor_tensor_reduce(src, src, future[:, SEQ - width:SEQ], -1.0, 3e38, ALU.add,
                                                             ALU.min, nmax[:, pair + h, t:t + 1]),
                                      m, self.mark.get(("nmax", k)), ns=70 + 133 * (t + 1))
                        s.free[i] = d
                rows, i = GROUP * TT, s.turn()
                m = s.pe(lambda e: e.transpose(s.bank(i)[0:rows, 0:P], nmax.rearrange("p h t -> p (h t)"), ident[:, :]),
                         d, s.free.get(i))
                self.mark["nmax", k] = m
                a = s.act(lambda e: e.activation(self.nmaxT[:, :], s.bank(i)[0:rows, 0:P], ACT.Copy), m,
                          self.mark.get(("max_row", 1 - k)), ns=200)
                s.free[i] = a
                dst = self.q[96:97, base:base + GROUP, :].bitcast(F32).rearrange("p h (t q) -> p (h t) q", q=P)
                self.mark["max_row", k] = self.max_dma[k](
                    lambda e: e.dma_start(dst, self.nmaxT[:, :].bitcast(F32)), a)

            def attend(self, group, v_ready):
                s = self.a
                base = (group % self.sets) * GROUP
                selected = []
                for pair in range(0, GROUP, 2):
                    for unit, at in ((((0, 0, 0),), 0), (((0, 1, 0), (0, 3, 384)), 512), (((1, 0, 0),), 0),
                                     (((1, 1, 0), (1, 3, 384)), 512), (((0, 2, 0), (1, 2, 256)), 1024)):
                        i = s.turn()
                        s.pe.wait(self.mark["max_row", group % 2], s.free.get(i))
                        unit_ns = sum(product_ns(SEQ - j * P) for _, j, _ in unit)
                        for n, (h, j, col) in enumerate(unit):
                            slot = base + pair + h
                            mk = lambda e, i=i, j=j, slot=slot, col=col: e.matmul(
                                s.bank(i)[:, col:col + SEQ - j * P], self.k[0:97, slot, j * P:(j + 1) * P],
                                self.q[0:97, slot, j * P:SEQ], start=True, stop=True)
                            m = s.pe(mk, ns=unit_ns) if n == len(unit) - 1 else s.pe.silent(mk)
                        if at == 1024:
                            src = s.bank(i).rearrange("p (h k) -> p h k", h=2)
                            dst = self.pt[:, pair:pair + 2, at:at + 256]
                        else:
                            src, dst = s.bank(i), self.pt[:, pair + unit[0][0], at:at + 512]
                        a = s.act(lambda e, src=src, dst=dst: e.activation(dst, src, ACT.Exp), m, self.mark.get("pt"))
                        s.free[i] = a
                    self.use[group % self.sets] = m
                    for at in (0, 512, 896, 1024):
                        blk = self.pt[:, pair:pair + 2, at:at + P]
                        selected.append(s.pool(lambda e, blk=blk: e.affine_select(
                            out=blk, in_=blk, compare_op=ALU.is_ge, fill=0.0, base=0,
                            pattern=[[0, 2], [1, P]], channel_multiplier=-1), a, ns=300))
                i = s.turn()
                s.pe.wait(v_ready, s.free.get(i), *selected)
                for j in range(TT):
                    for g in range(GROUP):
                        h = group * GROUP + g
                        cols = slice(h * (HDIM + 1), h * (HDIM + 1) + 32)
                        mk = lambda e, i=i, j=j, g=g, cols=cols: e.matmul(
                            s.bank(i)[32 * g:32 * g + 32, j * P:SEQ],
                            self.v[:, j, :, :].rearrange("p h d -> p (h d)")[:, cols],
                            self.pt[:, g, PT_AT[j]:PT_AT[j] + SEQ - j * P], start=(j == 0), stop=(j == TT - 1))
                        m = s.pe(mk, ns=2340) if (j, g) == (TT - 1, GROUP - 1) else s.pe.silent(mk)
                self.mark["v_use"] = self.mark["pt"] = m
                s = self.o_lanes
                a = s.act(lambda e, i=i: e.activation(self.oT[:, :], s.bank(i), ACT.Copy), m, self.mark.get("oT"))
                s.free[i] = a
                i = s.turn()
                s.pe.wait(a, s.free.get(i))
                for t in range(TT):
                    mk = lambda e, i=i, t=t: e.transpose(s.bank(i)[:, t * P:(t + 1) * P],
                                                         self.oT[:, t * P:(t + 1) * P], ident[:, :])
                    m = s.pe(mk) if t == TT - 1 else s.pe.silent(mk)
                self.mark["oT"] = m
                ov = s.bank(i).rearrange("p (t g d) -> p t g d", t=TT, g=GROUP)
                d = s.dve(lambda e: e.reciprocal(self.rec[:, :, :, :], ov[:, :, :, HDIM:HDIM + 1]), m, ns=190)
                at = group * GROUP * HDIM
                for t in range(TT):
                    d2 = s.dve(lambda e, t=t: e.tensor_tensor(
                        self.o[:, t, at:at + GROUP * HDIM].rearrange("p (g d) -> p g d", g=GROUP),
                        ov[:, t, :, 0:HDIM], self.rec[:, t, :, :].broadcast_to([P, GROUP, HDIM]), ALU.mult),
                        d, self.mark.get("o"), ns=130)
                s.free[i] = d2
                self.mark["o_ready"] = d2

            def layer(self, b, x, x_ready, wqk, wv, wo, bias=None, bias_ready=None):
                s, a = self.m, self.a
                ready = to_channels(s, x, self.xh, self.xl, x_ready, self.mark.get("x_use"))
                x_read = s.pe.now
                if bias is not None:
                    x_read = s.pool(lambda e: e.tensor_tensor(
                        x, x, bias[:, :].unsqueeze(1).broadcast_to([P, TT, DIM]), ALU.add), x_read, bias_ready, ns=2450)
                for half in range(2):
                    split = []
                    for which in range(2):
                        mcol = which * 256 + half * P
                        ops = []
                        for c in range(CT):
                            ops += three(wqk[0][:, c, mcol:mcol + P], wqk[1][:, c, mcol:mcol + P],
                                         self.xh[:, c, :], self.xl[:, c, :])
                        m = passes(s.pe, s.bank(which), ops, *ready, s.free.get(which))
                        split += split_psum(s, s.bank(which), self.parts[:, which, 0, :], self.parts[:, which, 1, :],
                                            m, self.mark.get("parts_free"), scale=SCALE if which == 0 else 1.0)
                        s.free[which] = split[-1]
                    self.send(b, half, split)
                for group in range(HEADS // GROUP):
                    self.load_rows(b, group)
                    self.scores_max(group)
                    if group == 0:
                        m = self.mark["x_use"] = token_major(a, self.xh, self.xl, wv, (*ready, s.pe.now))
                        v_ready = store_v(a, self, m)
                    self.attend(group, v_ready)
                return self.project(wo, x, x_read)

            def project(self, w, x, bias):
                s = self.o_lanes
                marks = to_channels(s, self.o[:, :, :], self.oh, self.ol, self.mark["o_ready"], self.mark.get("o_use"))
                self.mark["o"] = s.pe.now
                m = token_major(s, self.oh, self.ol, w, marks)
                self.mark["o_use"] = m
                return layernorm(s, x, self.stats, m, bias)

        def token_major(s, ah, al, w, ready, also=()):
            s.pe.wait(*ready, s.free.get(0), s.free.get(1))
            for t in range(TT):
                dst = s.bank(t // 2)[:, (t % 2) * DIM:(t % 2 + 1) * DIM]
                ops = []
                for c in range(CT):
                    ops += three(ah[:, c, t * P:(t + 1) * P], al[:, c, t * P:(t + 1) * P], w[0][:, c, :], w[1][:, c, :])
                m = passes(s.pe, dst, ops)
            return m

        def store_v(s, att, m):
            for i in range(2):
                v_ready = s.act(lambda e, i=i: e.activation(
                    att.v[:, 2 * i:2 * i + 2, 0:HEADS, 0:HDIM],
                    s.bank(i).rearrange("p (t h d) -> p t h d", t=2, d=HDIM), ACT.Copy),
                    m, att.mark.get("v_use"), att.v_ones)
            s.free[0] = s.free[1] = v_ready
            return v_ready

        def back_to_tokens(s, tiles, m, free):
            for c in range(CT):
                a = s.act(lambda e, c=c: e.activation(tiles[c], s.bank(c), ACT.Copy), m, *free)
            s.pe.wait(a)
            for t in range(TT):
                for c in range(CT):
                    at = (t % 2) * DIM + c * P
                    mk = lambda e, t=t, c=c, at=at: e.transpose(s.bank(t // 2)[:, at:at + P],
                                                                tiles[c][:, t * P:(t + 1) * P], ident[:, :])
                    m = s.pe(mk) if (t, c) == (TT - 1, CT - 1) else s.pe.silent(mk)
            return m

        def bias_rows(stack, name):
            t = sb(stack, name + "_rows", [P, DIM])
            lane = dma_lane("s_" + name)
            m = lane(lambda e: e.dma_start(t[:, :], dram[name].partition_broadcast(P)))
            return t, m

        def columns(stack, name, n):
            t = sb(stack, name + "_cols", [P, n])
            lane = dma_lane("s_" + name)
            m = lane(lambda e: e.dma_start(t[:, :], dram[name]))
            return t, m

        x_load = [dma_lane(f"s_x{n}") for n in range(RING)]
        x_store = [dma_lane(f"s_xs{n}") for n in range(RING)]
        x_of = lambda b: x_ring[:, b % RING, :, :]

        def phase1():
            with ExitStack() as st:
                X, A, O, Y = Stream(1, "x", 0), Stream(1, "a", 2, 3), Stream(1, "o", 2), Stream(1, "y", 5)
                tiles = [Stream(1, f"t{n}", 5) for n in range(2)]
                for s in tiles:
                    s.free = Y.free
                att = Attention(st, X, A, O, 1, HEADS // GROUP)
                xq_b, m_qb = columns(st, "xq_b", CT)
                xk_b, m_kb = columns(st, "xk_b", CT)
                xv_b, m_vb = bias_rows(st, "xv_b")
                xo_b, m_ob = bias_rows(st, "xo_b")
                nmask = sb(st, "nmask", [P, TT, CTX])
                get, staged, wm = load_weights(st, 1)
                stage_ctx = ExitStack()
                get_xk, staged_xk, wm_xk = load_weights(stage_ctx, 4)
                stage_ctx.push(staged_xk)
                trig = stage_ctx.enter_context(nc.sbuf_tensor("trig", [P, 3, SEQ], F32))
                four = stage_ctx.enter_context(nc.sbuf_tensor("four", [P, 2, 2, SEQ], F32))
                fhi = stage_ctx.enter_context(nc.sbuf_tensor("fhi", [P, 2, SEQ], F32R))
                ab = stage_ctx.enter_context(nc.sbuf_tensor("ab", [P, 2, HEADS], F32))
                ctx_st = stage_ctx.enter_context(nc.sbuf_tensor("ctx_st", [P, CT, BATCH * CTX], F32))
                ctx_h = stage_ctx.enter_context(nc.sbuf_tensor("ctx_h", [P, CT, BATCH * CTX], F32R))
                ctx_l = stage_ctx.enter_context(nc.sbuf_tensor("ctx_l", [P, CT, BATCH * CTX], F32R))
                kt32 = stage_ctx.enter_context(nc.sbuf_tensor("kt32", [P, 512], F32))
                kt_st = stage_ctx.enter_context(nc.sbuf_tensor("kt_st", [P, 2, 512], F32R))
                small = dma_lane("s_small1")
                small(lambda e: e.dma_start(trig[:, :, :], dram["trig"]))
                small(lambda e: e.dma_start(ab[:, :, :], dram["alpha_beta"]))
                small(lambda e: e.dma_start(nmask[:, :, :], dram["mask_f"]))
                m_ctx = small(lambda e: e.dma_start(ctx_st[:, :, :], dram["ctxT"]))
                att.ones_row()
                m_nm = Y.dve(lambda e: e.tensor_scalar(nmask[:, :, :], nmask[:, :, :], NEG, None, ALU.mult), m_ctx)
                m = X.act(lambda e: e.activation(fhi[:, 0, :], trig[:, 2, :], ACT.Copy), m_ctx)
                m = X.dve(lambda e: e.tensor_tensor(four[:, 0, 0, :], trig[:, 2, :], fhi[:, 0, :].bitcast(F32),
                                                    ALU.subtract), m)
                rows_dma = dma_lane("s_fourier")
                for block, src in ((0, fhi[:, 0, :].bitcast(F32)), (1, four[:, 0, 0, :]), (2, fhi[:, 0, :].bitcast(F32))):
                    r = slice(32 * block, 32 * block + 32)
                    rows_dma(lambda e, r=r, src=src: e.dma_start(
                        att.k[r, :, :].bitcast(F32), src[r].unsqueeze(1).broadcast_to([32, HEADS, SEQ])), m)
                last = [rows_dma.now, rows_dma.now]
                for h in range(HEADS):
                    i = h % 2
                    m = X.dve(lambda e, h=h, i=i: e.tensor_scalar(four[:, i, 0, :], trig[:, 0, :], ab[:, 0, h:h + 1],
                                                                  None, ALU.mult), last[i], ns=335)
                    m = X.dve(lambda e, h=h, i=i: e.scalar_tensor_tensor(
                        out=four[:, i, 1, :], in0=trig[:, 1, :], scalar=ab[:, 1, h:h + 1], in1=four[:, i, 0, :],
                        op0=ALU.mult, op1=ALU.add), m)
                    a = X.act(lambda e, h=h, i=i: e.activation(fhi[:, i, :], four[:, i, 1, :], ACT.Copy), m)
                    X.act(lambda e, h=h, i=i: e.activation(att.q[0:64, h, :], fhi[0:64, i, :].bitcast(F32), ACT.Copy), a)
                    last[i] = X.dve(lambda e, h=h, i=i: e.tensor_tensor(
                        att.q[64:96, h, :], four[64:96, i, 1, :], fhi[64:96, i, :].bitcast(F32), ALU.subtract), a)
                a = Y.act(lambda e: e.activation(ctx_h[:, :, :], ctx_st[:, :, :], ACT.Copy), m_ctx)
                m_ctx2 = Y.dve(lambda e: e.tensor_tensor(ctx_l[:, :, :], ctx_st[:, :, :], ctx_h[:, :, :].bitcast(F32),
                                                         ALU.subtract), a)
                Y.pe.wait(wm_xk[0])
                wxk = get_xk("xk", CT)
                m_bias = Y.dve(lambda e: e.tensor_scalar(xk_b[:, :], xk_b[:, :], SCALE, None, ALU.mult), m_kb)
                kt_out = dma_lane("s_kt_out")
                for mt in range(CT):
                    for n in range(2):
                        ops = []
                        cols = slice(n * 512, n * 512 + 512)
                        for c in range(CT):
                            ops += three(wxk[0][:, c, mt * P:(mt + 1) * P], wxk[1][:, c, mt * P:(mt + 1) * P],
                                         ctx_h[:, c, cols], ctx_l[:, c, cols])
                        m = passes(Y.pe, Y.bank(0), ops, Y.free.get(0), m_ctx2)
                        m = Y.act(lambda e, mt=mt: e.activation(kt32[:, :], Y.bank(0), ACT.Identity,
                                                                bias=xk_b[:, mt:mt + 1], scale=SCALE),
                                  m, m_bias, Y.free.get("kt32"))
                        Y.free[0] = m
                        a = Y.act(lambda e: e.activation(kt_st[:, 0, :], kt32[:, :], ACT.Copy), m, kt_out.now)
                        Y.free["kt32"] = Y.dve(lambda e: e.tensor_tensor(
                            kt_st[:, 1, :], kt32[:, :], kt_st[:, 0, :].bitcast(F32), ALU.subtract), a, kt_out.now)
                        for part in range(2):
                            kt_out(lambda e, mt=mt, cols=cols, part=part: e.dma_start(
                                kt_scratch[:, part, mt, cols], kt_st[:, part, :].bitcast(F32)), a, Y.free["kt32"])
                for part, t in ((0, ctx_h), (1, ctx_l)):
                    kt_out(lambda e, part=part, t=t: e.dma_start(ctx_scratch[:, part, :, :], t[:, :, :].bitcast(F32)), m_ctx2)
                barrier()
                stage_ctx.close()
                staged.close()
                att.buffers(st)

                yh = sb(st, "yh", [P, CT, SEQ], F32R)
                yl = sb(st, "yl", [P, CT, SEQ], F32R)
                qx_h = sb(st, "qx_h", [P, CT, SEQ], F32R)
                qx_l = sb(st, "qx_l", [P, CT, SEQ], F32R)
                cc = sb(st, "cc", [P, 2, CT, 2, CTX], F32R)
                kc_load = dma_lane("s_kc")
                km_h = sb(st, "km_h", [P, CT, HALF, CTX], F32R)
                km_l = sb(st, "km_l", [P, CT, HALF, CTX], F32R)
                vx = sb(st, "vx", [P, HALF, 32])
                sc = sb(st, "sc", [P, 2, HALF, CTX])
                mx = sb(st, "mx", [P, 2, 3, HALF, 1])
                ptx = sb(st, "ptx", [P, 4, SEQ])
                ystats = (sb(st, "ybn", [P, TT, 6]), sb(st, "yag", [P, TT, 2]), sb(st, "yrs", [P, 3, TT]))
                m_vz = Y.pool(lambda e: e.memset(vx[:, :, :], 0.0))
                km_load = dma_lane("s_km")
                Y.pool(lambda e: e.memset(km_h[:, :, :, :].bitcast(F32), 0.0))
                km_zero = Y.pool(lambda e: e.memset(km_l[:, :, :, :].bitcast(F32), 0.0))

                wqk, wv, wo = get("qk", CT), get("v", CT), get("o", CT)
                loaded, x_done, x_final = {}, {}, {}

                def load_x(b):
                    if b < batches:
                        loaded[b] = x_load[b % RING](lambda e: e.dma_start(
                            x_of(b), dram["x"][b].rearrange("(t p) d -> p t d", p=P)),
                            x_final.get(b - RING), x_done.get(b - RING))

                def attn0(b):
                    x_done[b] = att.layer(b, x_of(b), loaded[b], wqk, wv, wo)

                wxq, wxv, wxo = get("xq", CT), get("xv", CT), get("xo", CT)
                use = {}

                def cross0(b):
                    s = Y
                    x = x_of(b)
                    keys = slice(b * CTX, (b + 1) * CTX)
                    for part, km_part in enumerate((km_h, km_l)):
                        for h in range(HALF):
                            rows = slice(h * HDIM, (h + 1) * HDIM)
                            km = km_load(lambda e, part=part, km_part=km_part, h=h, rows=rows: e.dma_start(
                                km_part[rows, :, h, :].bitcast(F32), kt_scratch[rows, part, :, keys]),
                                use.get(("km", 0)), use.get(("km", 1)), km_zero)
                    for part in range(2):
                        for twice in range(2):
                            kc_ready = kc_load(lambda e, part=part, twice=twice: e.dma_start(
                                cc[:, part, :, twice, :].bitcast(F32), ctx_scratch[:, part, :, keys]), use.get("kc_pe"))
                    ops = []
                    for c in range(CT):
                        ch = cc[:, 0, c, :, :].rearrange("p a k -> p (a k)")
                        cl = cc[:, 1, c, :, :].rearrange("p a k -> p (a k)")
                        ops += three(ch, cl, wxv[0][:, c, :], wxv[1][:, c, :])
                    m = use["kc_pe"] = passes(s.pe, s.bank(2)[:, 0:DIM], ops, s.free.get(2), kc_ready)
                    for odd in range(2):
                        r = slice(64 * odd, 64 * odd + 64)
                        vm = s.dve(lambda e, r=r, odd=odd: e.tensor_tensor(
                            vx[r, :, 16 * odd:16 * odd + 16],
                            s.bank(2)[r, 0:DIM].rearrange("p (a o d) -> p a o d", o=2, d=HDIM)[:, :, odd, :],
                            xv_b[r, :].rearrange("p (a o d) -> p a o d", o=2, d=HDIM)[:, :, odd, :], ALU.add),
                            m, m_vb, m_vz, use.get("vx"))
                    s.free[2] = vm
                    ready = to_channels(s, x, yh, yl, x_done[b], use.get("yh"))
                    qm = []
                    for mt in range(CT):
                        ops = []
                        for c in range(CT):
                            ops += three(wxq[0][:, c, mt * P:(mt + 1) * P], wxq[1][:, c, mt * P:(mt + 1) * P],
                                         yh[:, c, :], yl[:, c, :])
                        m = passes(s.pe, s.bank(mt), ops, *ready, s.free.get(mt))
                        a, d = split_psum(s, s.bank(mt), qx_h[:, mt, :], qx_l[:, mt, :], m, use.get(("qx", 0)), use.get(("qx", 1)),
                                          m_qb, bias=xq_b[:, mt:mt + 1])
                        s.free[mt] = d
                        qm += [a, d]
                    use["yh"] = m
                    xb = s.pool(lambda e: e.tensor_tensor(x, x, xo_b[:, :].unsqueeze(1).broadcast_to([P, TT, DIM]),
                                                          ALU.add), *ready, m_ob, s.pe.now)
                    om = []
                    for c in range(CT):
                        copied = [None, None]
                        for t in range(TT):
                            i = t % 2
                            s = tiles[i]
                            rows = slice(t * P, (t + 1) * P)
                            kmv = [part[:, c, :, :].rearrange("p h k -> p (h k)") for part in (km_h, km_l)]
                            m = passes(s.pe, s.bank(i), three(qx_h[:, c, rows], qx_l[:, c, rows], kmv[0], kmv[1]),
                                       *qm, km, s.free.get(i))
                            use["qx", i] = use["km", i] = m
                            d = s.dve(lambda e, i=i, t=t: e.tensor_tensor(
                                sc[:, i, :, :], s.bank(i).rearrange("p (h k) -> p h k", h=HALF),
                                nmask[:, t, :].unsqueeze(1).broadcast_to([P, HALF, CTX]), ALU.add),
                                m, m_nm, use.get(("sc", i)))
                            s.free[i] = d
                            d = s.dve(lambda e, i=i: e.tensor_reduce(mx[:, i, 0, :, :], sc[:, i, :, :], AX.X, ALU.max), d,
                                      use.get(("sc", i)))
                            d = s.pool(lambda e, i=i: e.tensor_tensor(
                                sc[:, i, :, :], sc[:, i, :, :], mx[:, i, 0, :, :].broadcast_to([P, HALF, CTX]),
                                ALU.subtract), d)
                            a = s.act(lambda e, i=i: e.activation(sc[:, i, :, :], sc[:, i, :, :], ACT.Exp), d)
                            d = s.dve(lambda e, i=i: e.tensor_reduce(mx[:, i, 1, :, :], sc[:, i, :, :], AX.X, ALU.add), a)
                            d = s.dve(lambda e, i=i: e.reciprocal(mx[:, i, 2, :, :], mx[:, i, 1, :, :]), d, ns=100)
                            d = s.pool(lambda e, i=i: e.tensor_tensor(
                                sc[:, i, :, :], sc[:, i, :, :], mx[:, i, 2, :, :].broadcast_to([P, HALF, CTX]),
                                ALU.mult), d)
                            s.pe.wait(d, s.free.get(i))
                            for p in range(4):
                                mk = lambda e, i=i, p=p: e.transpose(
                                    s.bank(i)[:, p * P:(p + 1) * P],
                                    sc[:, i, 2 * p:2 * p + 2, :].rearrange("p h k -> p (h k)"), ident[:, :])
                                m = s.pe(mk) if p == 3 else s.pe.silent(mk)
                            use["sc", i] = m
                            a = s.act(lambda e, i=i, c=c, rows=rows: e.activation(
                                ptx[:, :, rows], s.bank(i).rearrange("p (a q) -> p a q", a=4), ACT.Copy),
                                m, use.get("ptx"))
                            s.free[i] = copied[i] = a
                        s = Y
                        s.pe.wait(*copied, vm, s.free.get(2))
                        for p in range(4):
                            mk = lambda e, p=p, c=c: e.matmul(s.bank(2)[32 * p:32 * p + 32, :], vx[:, 4 * c + p, :],
                                                              ptx[:, p, :], start=True, stop=True)
                            m = s.pe(mk, ns=940) if p == 3 else s.pe.silent(mk)
                        use["ptx"] = use["vx"] = m
                        a, d = split_psum(s, s.bank(2), yh[:, c, :], yl[:, c, :], m)
                        s.free[2] = d
                        om += [a, d]
                    m = token_major(s, yh, yl, wxo, om)
                    use["yh"] = m
                    end = layernorm(s, x, ystats, m, xb)
                    x_final[b] = x_store[b % RING](lambda e: e.dma_start(x_mid[0][b], x), end)

                for b in range(RING):
                    load_x(b)
                for b in range(batches):
                    attn0(b)
                    cross0(b)
                    load_x(b + RING)
                barrier()

        def phase2():
            with ExitStack() as st:
                X, A, O, Y = Stream(2, "x", 0), Stream(2, "a", 2), Stream(2, "o", 2), Stream(2, "y", 4)
                gating, last = Stream(2, "g", 4), Stream(2, "f", 6)
                gating.free = Y.free
                proj_b, m_pb = bias_rows(st, "proj_b")
                router_b, m_rb = columns(st, "router_b", 1)
                att = Attention(st, X, A, O, 2, 2)
                w_low = [sb(st, f"w_low_{part}", [P, CT, 3 * DIM], F32R) for part in ("h", "l")]
                get, stage_ctx, wm = load_weights(st, 2)
                att.no_bias_rows()
                att.ones_row()
                stage = lambda name, dt=F32: stage_ctx.enter_context(nc.sbuf_tensor(name, [LAT, 2, 3 * DIM], dt))
                low, low_h, low_l = stage("low"), stage("low_h", F32R), stage("low_l", F32R)
                low_dma = dma_lane("s_low")
                m = low_dma(lambda e: e.dma_start(low[:, :, :], dram["low"]))
                m = X.act(lambda e: e.activation(low_h[:, :, :], low[:, :, :], ACT.Copy), m)
                m = X.dve(lambda e: e.tensor_tensor(low_l[:, :, :], low[:, :, :], low_h[:, :, :].bitcast(F32),
                                                    ALU.subtract), m)
                for which in range(3):
                    for c in range(CT):
                        i = X.turn()
                        rows, cols = slice(which * DIM + c * P, which * DIM + (c + 1) * P), slice(which * DIM, (which + 1) * DIM)
                        end = passes(X.pe, X.bank(i)[:, 0:DIM], three(low_h[:, 0, rows], low_l[:, 0, rows],
                                                                      low_h[:, 1, cols], low_l[:, 1, cols]),
                                     m, X.free.get(i))
                        X.free[i] = split_psum(X, X.bank(i)[:, 0:DIM], w_low[0][:, c, cols], w_low[1][:, c, cols], end)[1]
                barrier()
                stage_ctx.close()
                att.buffers(st)

                yh = sb(st, "yh2", [P, CT, SEQ], F32R)
                yl = sb(st, "yl2", [P, CT, SEQ], F32R)
                gate_of = sb(st, "gate_of", [P, GATES, SEQ])
                gs = sb(st, "gs", [P, 6, TT, EXPERTS])
                gs1 = sb(st, "gs1", [P, 4, TT, 1])
                gT = sb(st, "gT", [TT * EXPERTS, P])
                back = sb(st, "back", [P, CT, SEQ])
                th = sb(st, "th", [P, SEQ])
                hid = sb(st, "hid", [P, SEQ])
                lgT = th[0:EXPERTS, :]
                hid_h = sb(st, "hid_h", [P, SEQ], F32R)
                hid_l = sb(st, "hid_l", [P, SEQ], F32R)
                ystats = (sb(st, "ybn2", [P, TT, 6]), sb(st, "yag2", [P, TT, 2]), sb(st, "yrs2", [P, 3, TT]))
                gate_out = dma_lane("s_gate_out")
                gate_dma = [dma_lane(f"s_gate{n}") for n in range(GATES)]

                w1, w3, w2, wr = get("w1", CT, 10), get("w3", CT, 10), get("w2", 10), get("router", CT)
                wo = get("o", CT)
                loaded, x_done, x_final, use = {}, {}, {}, {}

                def load_x(b):
                    if b < batches:
                        loaded[b] = x_load[b % RING](lambda e: e.dma_start(x_of(b), x_mid[0][b]), x_final.get(b - RING))

                def gates(s, b, ready):
                    ops = []
                    for c in range(CT):
                        ops += three(wr[0][:, c, :], wr[1][:, c, :], yh[:, c, :], yl[:, c, :])
                    m = passes(s.pe, s.bank(0)[0:ROUTER, :], ops, *ready, s.free.get(0))
                    m = s.act(lambda e: e.activation(lgT, s.bank(0)[0:EXPERTS, :], ACT.Identity,
                                                     bias=router_b[0:EXPERTS, 0:1]), m, m_rb, use.get("th"))
                    s.free[0] = m
                    s.pe.wait(m, s.free.get(1))
                    for t in range(TT):
                        mk = lambda e, t=t: e.transpose(s.bank(1)[:, t * EXPERTS:(t + 1) * EXPERTS],
                                                        lgT[:, t * P:(t + 1) * P], ident[0:EXPERTS, 0:EXPERTS])
                        m = s.pe(mk) if t == TT - 1 else s.pe.silent(mk)
                    n = TT * EXPERTS
                    flat = lambda i: gs[:, i, :, :]
                    wide = lambda v: v.broadcast_to([P, TT, EXPERTS])
                    lg, top, above, equal, count, tmp = (flat(i) for i in range(6))
                    gate = above
                    use["th"] = m
                    m = s.dve(lambda e: e.tensor_copy(lg, s.bank(1)[:, 0:n].rearrange("p (t e) -> p t e", t=TT)), m, ns=90)
                    s.free[1] = m
                    for t in range(TT):
                        m2 = s.dve(lambda e, t=t: e.max(top[:, t, :], lg[:, t, :]), m, ns=90)
                    second = top[:, :, 1:2]
                    m = s.dve(lambda e: e.tensor_tensor(above, lg, wide(second), ALU.is_gt), m2, use.get("gate"), ns=90)
                    m = s.dve(lambda e: e.tensor_tensor(equal, lg, wide(second), ALU.is_equal), m, ns=90)
                    m = s.dve(lambda e: e.tensor_reduce(gs1[:, 0, :, :], above, AX.X, ALU.add), m, ns=90)
                    src = equal
                    bufs = [count, tmp]
                    for i, step in enumerate((1, 2, 4)):
                        dst = bufs[i % 2]
                        m = s.dve(lambda e, dst=dst, src=src, step=step: e.tensor_copy(dst[:, :, 0:step], src[:, :, 0:step]), m, ns=90)
                        m = s.dve(lambda e, dst=dst, src=src, step=step: e.tensor_tensor(
                            dst[:, :, step:EXPERTS], src[:, :, step:EXPERTS], src[:, :, 0:EXPERTS - step], ALU.add), m, ns=90)
                        src = dst
                    m = s.dve(lambda e, src=src: e.tensor_tensor(tmp, src, wide(gs1[:, 0, :, :]), ALU.add), m, ns=90)
                    m = s.dve(lambda e: e.tensor_scalar(tmp, tmp, 2.5, None, ALU.is_lt), m, ns=90)
                    m = s.dve(lambda e: e.tensor_tensor(tmp, tmp, equal, ALU.mult), m, ns=90)
                    m = s.dve(lambda e: e.tensor_tensor(tmp, tmp, above, ALU.add), m, ns=90)
                    m = s.dve(lambda e: e.tensor_tensor(lg, lg, wide(top[:, :, 0:1]), ALU.subtract), m, ns=90)
                    a = s.act(lambda e: e.activation(gate, lg, ACT.Exp), m, use.get("gate"))
                    m = s.dve(lambda e: e.tensor_tensor(gate, gate, tmp, ALU.mult), a, ns=90)
                    m = s.dve(lambda e: e.tensor_reduce(gs1[:, 1, :, :], gate, AX.X, ALU.add), m, ns=90)
                    m = s.dve(lambda e: e.reciprocal(gs1[:, 2, :, :], gs1[:, 1, :, :]), m, ns=90)
                    m = s.dve(lambda e: e.tensor_tensor(gate, gate, wide(gs1[:, 2, :, :]), ALU.mult), m, ns=90)

                    def to_rows():
                        end = s.pe(lambda e: e.transpose(s.bank(0)[0:n, 0:P], gate.rearrange("p t e -> p (t e)"),
                                                         ident[:, :]), m, s.free.get(0))
                        use["gate"] = end
                        a = s.act(lambda e: e.activation(gT[:, :], s.bank(0)[0:n, 0:P], ACT.Copy, scale=0.5), end,
                                  use.get("gT"), ns=200)
                        s.free[0] = a
                        use["gT"] = use["gate_home"] = gate_out(
                            lambda e: e.dma_start(gate_scratch[b % 2], gT[:, :]), a, *[lane.now for lane in gate_dma])
                    return to_rows

                def spread_gate(b, n):
                    row = gate_scratch[b % 2].rearrange("(t e) q -> e t q", t=TT)[n].partition_broadcast(P)
                    k = n % GATES
                    return gate_dma[k](lambda e: e.dma_start(gate_of[:, k, :].rearrange("p (t q) -> p t q", t=TT), row),
                                       use["gate_home"], use.get(("gate_of", k)))

                def experts(b):
                    s = Y
                    x = x_of(b)
                    ready = to_channels(s, x, yh, yl, loaded[b], use.get("yh"))
                    x_read = s.pe.now
                    last_gates = gates(gating, b, ready)
                    gated = {}

                    def up(i, w, bank):
                        ops = []
                        for c in range(CT):
                            ops += three(w[0][:, c, i, :], w[1][:, c, i, :], yh[:, c, :], yl[:, c, :])
                        m = use["yh"] = passes(s.pe, s.bank(bank), ops, *ready, s.free.get(bank))
                        return m

                    def hidden(i, m1, m3):
                        a = s.act(lambda e: e.activation(th[:, :], s.bank(0), ACT.Tanh, scale=0.5), m1, use.get("th"))
                        d = s.dve(lambda e: e.scalar_tensor_tensor(out=hid[:, :], in0=th[:, :], scalar=1.0,
                                                                   in1=s.bank(0), op0=ALU.add, op1=ALU.mult),
                                  a, use.get("hid"), ns=600)
                        use["th"] = s.free[0] = d
                        d = s.dve(lambda e: e.tensor_tensor(hid[:, :], hid[:, :], s.bank(1), ALU.mult), m3, d, ns=600)
                        s.free[1] = d
                        half = 0.5
                        if i >= SHARED:
                            n = i - SHARED
                            d = s.pool(lambda e, n=n: e.tensor_tensor(
                                hid[:, :], hid[:, :], gate_of[:, n % GATES, :], ALU.mult), d, gated[n], ns=1250)
                            use["gate_of", n % GATES] = d
                            if n + GATES < EXPERTS:
                                gated[n + GATES] = spread_gate(b, n + GATES)
                            half = 1.0
                        a = s.act(lambda e, half=half: e.activation(hid_h[:, :], hid[:, :], ACT.Copy, scale=half), d,
                                  use.get("hid_pe"))
                        if i < SHARED:
                            d = s.dve(lambda e: e.scalar_tensor_tensor(
                                out=hid_l[:, :], in0=hid[:, :], scalar=0.5, in1=hid_h[:, :].bitcast(F32),
                                op0=ALU.mult, op1=ALU.subtract), a)
                        else:
                            d = s.dve(lambda e: e.tensor_tensor(hid_l[:, :], hid[:, :], hid_h[:, :].bitcast(F32),
                                                                 ALU.subtract), a)
                        use["hid"] = d
                        return a, d

                    def down(i, parts):
                        for c in range(CT):
                            cols = slice(c * P, (c + 1) * P)
                            m = passes(s.pe, s.bank(2 + c), three(w2[0][:, i, cols], w2[1][:, i, cols],
                                                                  hid_h[:, :], hid_l[:, :]),
                                       *parts, last.free.get(c) if i == 0 else None, start=(i == 0),
                                       stop=(i == SHARED + EXPERTS - 1))
                        use["hid_pe"] = m
                        return m

                    n_all = SHARED + EXPERTS
                    parts = hidden(0, up(0, w1, 0), up(0, w3, 1))
                    last_gates()
                    for n in range(GATES):
                        gated[n] = spread_gate(b, n)
                    for i in range(n_all):
                        if i + 1 < n_all:
                            m1, m3 = up(i + 1, w1, 0), up(i + 1, w3, 1)
                        m = down(i, parts)
                        if i + 1 < n_all:
                            parts = hidden(i + 1, m1, m3)
                    end = back_to_tokens(last, (back[:, 0, :], back[:, 1, :]), m, (use.get("back"),))
                    use["back"] = end
                    x_done[b] = layernorm(last, x, ystats, end, x_read)

                def attn1(b):
                    x = x_of(b)
                    end = att.layer(b, x, x_done[b], w_low, [w[:, :, 512:768] for w in w_low], wo, proj_b, m_pb)
                    x_final[b] = x_store[b % RING](lambda e: e.dma_start(x_mid[1][b], x), end)

                for b in range(RING):
                    load_x(b)
                for b in range(batches):
                    experts(b)
                    attn1(b)
                    load_x(b + RING)
                barrier()

        def phase3():
            with ExitStack() as st:
                X, Y, last = Stream(3, "x", 0), Stream(3, "y", 3), Stream(3, "f", 6)
                turns_of = [Stream(3, f"h{n}", 3) for n in range(DEEP)]
                for s in turns_of:
                    s.free, s.pe = Y.free, Y.pe
                cq_b, m_qb = columns(st, "cq_b", CT)
                ck_b, m_kb = columns(st, "ck_b", CT)
                cv_b, m_vb = columns(st, "cv_b", CT)
                co_b, m_ob = bias_rows(st, "co_b")
                f2_b, m_fb = bias_rows(st, "f2_b")
                ff_c, m_fc = columns(st, "ff_c", 4 * FT)
                fc = sb(st, "fc", [P, 12, FT])
                keys_all = BATCH * CTX
                a_h = sb(st, "a_h", [P, CT, keys_all], F32R)
                a_l = sb(st, "a_l", [P, CT, keys_all], F32R)
                v_h = sb(st, "v_h", [P, CT, BATCH, 2, CTX], F32R)
                v_l = sb(st, "v_l", [P, CT, BATCH, 2, CTX], F32R)
                q_bias = sb(st, "q_bias", [P, keys_all])
                seen = sb(st, "seen", [P, keys_all])
                unseen = sb(st, "unseen", [P, keys_all])
                get, stage_ctx, wm = load_weights(st, 3)
                stage = lambda name, shape, dt=F32: stage_ctx.enter_context(nc.sbuf_tensor(name, shape, dt))
                ctx_st = stage("ctx_st3", [P, CT, keys_all])
                ctx_h = stage("ctx_h3", [P, CT, keys_all], F32R)
                ctx_l = stage("ctx_l3", [P, CT, keys_all], F32R)
                k_h = stage("k_h3", [P, CT, keys_all], F32R)
                k_l = stage("k_l3", [P, CT, keys_all], F32R)
                tile32 = stage("tile32", [P, 512])
                bq = stage("bq", [P, CT, P])
                bq_h = stage("bq_h", [P, CT, P], F32R)
                bq_l = stage("bq_l", [P, CT, P], F32R)
                mask_i = stage("mask_i", [P, keys_all], I32)
                small = dma_lane("s_small3")
                small(lambda e: e.dma_start(mask_i[:, :], dram["mask_i"].partition_broadcast(P)))
                m_ctx = small(lambda e: e.dma_start(ctx_st[:, :, :], dram["ctxT"]))
                a = Y.act(lambda e: e.activation(ctx_h[:, :, :], ctx_st[:, :, :], ACT.Copy), m_ctx)
                m_ctx = Y.dve(lambda e: e.tensor_tensor(ctx_l[:, :, :], ctx_st[:, :, :], ctx_h[:, :, :].bitcast(F32),
                                                        ALU.subtract), a)
                m = Y.dve(lambda e: e.tensor_scalar(seen[:, :], mask_i[:, :], 0.0, None, ALU.not_equal), small.now)
                Y.dve(lambda e: e.tensor_scalar(unseen[:, :], seen[:, :], 10000.0, -10000.0, ALU.mult, ALU.add), m)
                m = Y.dve(lambda e: e.tensor_copy(bq[:, :, :], cq_b[:, :].unsqueeze(2).broadcast_to([P, CT, P])), m_qb)
                a = Y.act(lambda e: e.activation(bq_h[:, :, :], bq[:, :, :], ACT.Copy), m)
                m_bq = Y.dve(lambda e: e.tensor_tensor(bq_l[:, :, :], bq[:, :, :], bq_h[:, :, :].bitcast(F32),
                                                       ALU.subtract), a)
                Y.pe.wait(*wm)

                def all_keys(w, hi_in, lo_in, store, bias, *after):
                    for mt in range(CT):
                        for n in range(2):
                            cols = slice(n * 512, n * 512 + 512)
                            ops = []
                            for c in range(CT):
                                ops += three(w[0][:, c, mt * P:(mt + 1) * P], w[1][:, c, mt * P:(mt + 1) * P],
                                             hi_in[:, c, cols], lo_in[:, c, cols])
                            m = passes(Y.pe, Y.bank(0), ops, Y.free.get(0), *after)
                            m = Y.act(lambda e, mt=mt: e.activation(
                                tile32[:, :], Y.bank(0), ACT.Identity,
                                bias=0.0 if bias is None else bias[:, mt:mt + 1]), m, Y.free.get("tile"))
                            Y.free[0] = m
                            done = store(mt, n, cols, m)
                            Y.free["tile"] = done
                    return done

                def store_split(hi, lo):
                    def store(mt, n, cols, m):
                        a = Y.act(lambda e: e.activation(hi[:, mt, cols], tile32[:, :], ACT.Copy), m)
                        return Y.dve(lambda e: e.tensor_tensor(lo[:, mt, cols], tile32[:, :],
                                                               hi[:, mt, cols].bitcast(F32), ALU.subtract), a)
                    return store

                def store_twice(mt, n, cols, m):
                    rows = slice(n * 8, n * 8 + 8)
                    t3 = tile32[:, :].rearrange("p (b k) -> p b k", k=CTX)
                    for i in range(2):
                        a = Y.act(lambda e, i=i: e.activation(v_h[:, mt, rows, i, :], t3, ACT.Copy), m)
                        d = Y.dve(lambda e, i=i: e.tensor_tensor(v_l[:, mt, rows, i, :], t3,
                                                                 v_h[:, mt, rows, i, :].bitcast(F32), ALU.subtract), a)
                    return d

                k_ready = all_keys(get("xk", CT), ctx_h, ctx_l, store_split(k_h, k_l), ck_b, m_ctx, m_kb)
                all_keys(get("xv", CT), k_h, k_l, store_twice, cv_b, k_ready, m_vb)
                all_keys(get("xqT", CT), k_h, k_l, store_split(a_h, a_l), None, k_ready)
                for n in range(2):
                    cols = slice(n * 512, n * 512 + 512)
                    ops = []
                    for c in range(CT):
                        ops += three(bq_h[:, c, :], bq_l[:, c, :], k_h[:, c, cols], k_l[:, c, cols])
                    m = passes(Y.pe, Y.bank(0), ops, Y.free.get(0), m_bq)
                    Y.free[0] = Y.act(lambda e, cols=cols: e.activation(q_bias[:, cols], Y.bank(0), ACT.Copy), m)

                phase_c, real_c, imag_c, b1_c = (ff_c[:, i * FT:(i + 1) * FT] for i in range(4))
                col = lambda i: fc[:, i, :]
                turns, angle, frac, sin_c, cos_c, amp, shift = (col(i) for i in range(7))

                def ts(out_ap, in_ap, s1, s2, op0, op1, *after):
                    return Y.dve(lambda e: e.tensor_scalar(out_ap, in_ap, s1, s2, op0, op1), *after)

                def tt(out_ap, a_ap, b_ap, op, *after):
                    return Y.dve(lambda e: e.tensor_tensor(out_ap, a_ap, b_ap, op), *after)

                m = ts(turns, phase_c, INV_2PI, ROUND, ALU.mult, ALU.add, m_fc)
                m = ts(turns, turns, -ROUND, None, ALU.add, ALU.bypass, m)
                src = phase_c
                for part in (PI_A, PI_B, PI_C):
                    m = ts(col(8), turns, -part, None, ALU.mult, ALU.bypass, m)
                    m = tt(angle, src, col(8), ALU.add, m)
                    src = angle
                m = ts(frac, angle, INV_2PI, None, ALU.mult, ALU.bypass, m)
                for quarter, res in ((0.0, sin_c), (0.25, cos_c)):
                    m = ts(col(8), frac, quarter, None, ALU.add, ALU.bypass, m)
                    m = ts(col(9), col(8), ROUND, None, ALU.add, ALU.bypass, m)
                    m = ts(col(9), col(9), -ROUND, None, ALU.add, ALU.bypass, m)
                    m = tt(col(8), col(8), col(9), ALU.subtract, m)
                    m = Y.act(lambda e, res=res: e.activation(res, col(8), ACT.Sin, scale=TWO_PI), m)
                m = tt(cos_c, cos_c, real_c, ALU.mult, m)
                m = tt(sin_c, sin_c, imag_c, ALU.mult, m)
                m = tt(amp, cos_c, sin_c, ALU.add, m)
                m = tt(amp, amp, imag_c, ALU.mult, m)
                m = ts(amp, amp, 0.1, None, ALU.mult, ALU.bypass, m)
                m = ts(col(8), b1_c, 0.1, None, ALU.mult, ALU.bypass, m)
                m = tt(shift, angle, col(8), ALU.add, m)
                m = ts(shift, shift, INV_2PI, None, ALU.mult, ALU.bypass, m)
                barrier()
                stage_ctx.close()

                xh = sb(st, "xh3", [P, CT, SEQ], F32R)
                xl = sb(st, "xl3", [P, CT, SEQ], F32R)
                sc = sb(st, "sc3", [P, TT, CTX])
                st1 = sb(st, "st3", [P, 3, TT, 1])
                p2 = sb(st, "p2", [P, TT, 2, CTX])
                pT = sb(st, "pT", [P, SEQ], F32R)
                vw_h = sb(st, "vw_h", [P, DIM], F32R)
                back = sb(st, "back3", [P, CT, SEQ])
                vw_l = sb(st, "vw_l", [P, DIM], F32R)
                xstats = (sb(st, "xbn3", [P, TT, 6]), sb(st, "xag3", [P, TT, 2]), sb(st, "xrs3", [P, 3, TT]))
                ystats = (sb(st, "ybn3", [P, TT, 6]), sb(st, "yag3", [P, TT, 2]), sb(st, "yrs3", [P, 3, TT]))
                yh = sb(st, "yh3", [P, CT, SEQ], F32R)
                yl = sb(st, "yl3", [P, CT, SEQ], F32R)
                tr = sb(st, "tr", [P, DEEP, SEQ])
                ang = sb(st, "ang", [P, DEEP, SEQ])
                act_h = sb(st, "act_h", [P, DEEP, SEQ], F32R)
                act_l = sb(st, "act_l", [P, DEEP, SEQ], F32R)
                wo, w1, w2 = get("xo", CT), get("w1", CT), get("w2", FT)
                loaded, x_done, x_final, use = {}, {}, {}, {}

                def load_x(b):
                    if b < batches:
                        loaded[b] = x_load[b % RING](lambda e: e.dma_start(x_of(b), x_mid[1][b]), x_final.get(b - RING))

                def cross1(b):
                    s = X
                    x = x_of(b)
                    keys = slice(b * CTX, (b + 1) * CTX)
                    ops = []
                    for c in range(CT):
                        ops += three(v_h[:, c, b, :, :].rearrange("p a k -> p (a k)"),
                                     v_l[:, c, b, :, :].rearrange("p a k -> p (a k)"), wo[0][:, c, :], wo[1][:, c, :])
                    m = passes(s.pe, s.bank(2)[:, 0:DIM], ops, s.free.get(2))
                    a, vw = split_psum(s, s.bank(2)[:, 0:DIM], vw_h[:, :], vw_l[:, :], m, use.get("vw"))
                    s.free[2] = vw
                    ready = to_channels(s, x, xh, xl, loaded[b], use.get("xh"))
                    xb = s.pool(lambda e: e.tensor_tensor(x, x, co_b[:, :].unsqueeze(1).broadcast_to([P, TT, DIM]),
                                                          ALU.add), *ready, m_ob, s.pe.now)
                    s.pe.wait(*ready, s.free.get(2))
                    for t in range(TT):
                        rows = slice(t * P, (t + 1) * P)
                        ops = []
                        for c in range(CT):
                            ops += three(xh[:, c, rows], xl[:, c, rows], a_h[:, c, keys], a_l[:, c, keys])
                        m = passes(s.pe, s.bank(2)[:, t * CTX:(t + 1) * CTX], ops)
                    use["xh"] = m
                    key = lambda t: t[:, keys].unsqueeze(1).broadcast_to([P, TT, CTX])
                    wide = lambda i: st1[:, i, :, :].broadcast_to([P, TT, CTX])
                    m = s.dve(lambda e: e.tensor_tensor(sc[:, :, :], s.bank(2)[:, 0:TT * CTX].rearrange(
                        "p (t k) -> p t k", t=TT), key(q_bias), ALU.add), m, use.get("sc"), ns=330)
                    s.free[2] = m
                    m = s.dve(lambda e: e.tensor_tensor(sc[:, :, :], sc[:, :, :], key(seen), ALU.mult), m, ns=330)
                    m = s.dve(lambda e: e.tensor_tensor(sc[:, :, :], sc[:, :, :], key(unseen), ALU.add), m, ns=330)
                    m = s.dve(lambda e: e.tensor_reduce(st1[:, 0, :, :], sc[:, :, :], AX.X, ALU.max), m, ns=330)
                    m = s.dve(lambda e: e.tensor_tensor(sc[:, :, :], sc[:, :, :], wide(0), ALU.subtract), m, ns=330)
                    m = s.act(lambda e: e.activation(sc[:, :, :], sc[:, :, :], ACT.Exp), m)
                    m = s.dve(lambda e: e.tensor_reduce(st1[:, 1, :, :], sc[:, :, :], AX.X, ALU.add), m, ns=330)
                    m = s.dve(lambda e: e.reciprocal(st1[:, 2, :, :], st1[:, 1, :, :]), m, ns=330)
                    m = s.dve(lambda e: e.tensor_tensor(sc[:, :, :], sc[:, :, :], wide(2), ALU.mult), m, ns=330)
                    m = s.dve(lambda e: e.tensor_copy(p2[:, :, 0, :].bitcast(F32R), sc[:, :, :]), m, use.get("p2"), ns=330)
                    m = s.dve(lambda e: e.tensor_tensor(p2[:, :, 1, :].bitcast(F32R), sc[:, :, :], p2[:, :, 0, :],
                                                        ALU.subtract), m, ns=330)
                    s.pe.wait(m, s.free.get(2))
                    for t in range(TT):
                        mk = lambda e, t=t: e.transpose(s.bank(2)[:, t * P:(t + 1) * P],
                                                        p2[:, t, :, :].rearrange("p a k -> p (a k)"), ident[:, :])
                        m = s.pe(mk) if t == TT - 1 else s.pe.silent(mk)
                    use["p2"] = m
                    a = s.act(lambda e: e.activation(pT[:, :], s.bank(2), ACT.Copy), m, use.get("pT"))
                    s.free[2] = a
                    s.pe.wait(a, vw, s.free.get(0), s.free.get(1))
                    for t in range(TT):
                        rows = slice(t * P, (t + 1) * P)
                        m = passes(s.pe, s.bank(t // 2)[:, (t % 2) * DIM:(t % 2 + 1) * DIM],
                                   [(pT[:, rows], vw_h[:, :]), (pT[:, rows], vw_l[:, :])])
                    use["pT"] = use["vw"] = m
                    x_done[b] = layernorm(s, x, xstats, m, xb)

                def feed_forward(b):
                    s = Y
                    x = x_of(b)
                    ready = to_channels(s, x, yh, yl, x_done[b], use.get("yh"))
                    xb = last.pool(lambda e: e.tensor_tensor(x, x, f2_b[:, :].unsqueeze(1).broadcast_to([P, TT, DIM]),
                                                          ALU.add), *ready, m_fb, s.pe.now)

                    def up(i):
                        k = i % DEEP
                        s = turns_of[k]
                        ops = []
                        for c in range(CT):
                            cols = slice(i * P, (i + 1) * P)
                            ops += three(w1[0][:, c, cols], w1[1][:, c, cols], yh[:, c, :], yl[:, c, :])
                        m = passes(s.pe, s.bank(k), ops, *ready, s.free.get(k))
                        use["yh"] = m
                        c1 = 0.1 * INV_2PI
                        a = s.act(lambda e: e.activation(ang[:, k, :], s.bank(k), ACT.Identity, scale=c1,
                                                         bias=shift[:, i:i + 1]), m, use.get(("ang", k)))
                        d = s.dve(lambda e: e.tensor_scalar(tr[:, k, :], ang[:, k, :], ROUND, None, ALU.add), a,
                                  use.get(("tr", k)), ns=335)
                        d = s.dve(lambda e: e.scalar_tensor_tensor(out=ang[:, k, :], in0=tr[:, k, :], scalar=ROUND,
                                                                   in1=ang[:, k, :], op0=ALU.subtract,
                                                                   op1=ALU.subtract), d)
                        a = s.act(lambda e: e.activation(tr[:, k, :], ang[:, k, :], ACT.Sin, scale=-TWO_PI), d)
                        d = s.dve(lambda e: e.scalar_tensor_tensor(out=ang[:, k, :], in0=tr[:, k, :],
                                                                   scalar=amp[:, i:i + 1], in1=s.bank(k),
                                                                   op0=ALU.mult, op1=ALU.add), a)
                        use["tr", k] = s.free[k] = d
                        d = s.dve(lambda e: e.tensor_scalar(ang[:, k, :], ang[:, k, :], b1_c[:, i:i + 1], 0.0, ALU.add,
                                                            ALU.max), d)
                        a = s.act(lambda e: e.activation(act_h[:, k, :], ang[:, k, :], ACT.Copy), d, use.get(("act", k)))
                        d = s.pool(lambda e: e.tensor_tensor(act_l[:, k, :], ang[:, k, :], act_h[:, k, :].bitcast(F32),
                                                             ALU.subtract), a)
                        use["ang", k] = d
                        return a, d

                    def down(i, parts):
                        k = i % DEEP
                        for c in range(CT):
                            cols = slice(c * P, (c + 1) * P)
                            m = passes(s.pe, last.bank(c), three(w2[0][:, i, cols], w2[1][:, i, cols],
                                                                  act_h[:, k, :], act_l[:, k, :]),
                                       *parts, last.free.get(c) if i == 0 else None, start=(i == 0), stop=(i == FT - 1))
                        use["act", k] = m
                        return m

                    parts = {i: up(i) for i in range(DEEP - 1)}
                    for i in range(FT):
                        if i + DEEP - 1 < FT:
                            parts[i + DEEP - 1] = up(i + DEEP - 1)
                        m = down(i, parts[i])
                    m = use["back"] = back_to_tokens(last, (back[:, 0, :], back[:, 1, :]), m, (use.get("back"),))
                    end = layernorm(last, x, ystats, m, xb)
                    x_final[b] = x_store[b % RING](lambda e: e.dma_start(out[b].rearrange("(t p) d -> p t d", p=P), x), end)

                for b in range(RING):
                    load_x(b)
                for b in range(batches):
                    cross1(b)
                    feed_forward(b)
                    load_x(b + RING)
                barrier()

        for n, phase in ((1, phase1), (2, phase2), (3, phase3)):
            if n in phases:
                phase()

        block = ctx.enter_context(nc.Block())
        for engine, name in ((block.sync, "sp"), (block.tensor, "pe"), (block.vector, "dve"),
                             (block.scalar, "act"), (block.gpsimd, "pool")):
            def play(e, steps=queues[name].steps):
                for step in steps:
                    step(e)
            engine(play)


def rows_of(w):
    k, n = w.shape
    return np.ascontiguousarray(w.reshape(k // P, P, n).transpose(1, 0, 2).reshape(P, -1))


def cols_of(v):
    return np.ascontiguousarray(v.reshape(-1, P).T)


def trig_tables():
    r = HDIM // 2
    omega = 10000.0 ** (-2.0 * np.arange(r) / HDIM)
    ang = omega[:, None] * np.arange(SEQ)[None, :]
    cos, sin = np.cos(ang), np.sin(ang)
    t = np.zeros((P, 3, SEQ), np.float32)
    for block in range(3):
        at = 32 * block + HDIM
        t[at:at + r, 0], t[at:at + r, 1], t[at:at + r, 2] = cos, sin, cos
        t[at + r:at + 2 * r, 0], t[at + r:at + 2 * r, 1], t[at + r:at + 2 * r, 2] = sin, -cos, sin
    return t


def lay_out(inp):
    a = {k: np.asarray(v) for k, v in inp.items()}
    r = HDIM // 2
    qkv = a["L0_attn_Wqkv"].T
    out = {"x": a["x"], "trig": trig_tables(), "w4": rows_of(a["L0_xattn_wk_w"])}
    ctx = a["ctx_1024"].reshape(BATCH * CTX, DIM).T
    out["ctxT"] = rows_of(ctx).reshape(P, CT, BATCH * CTX)
    ab = np.zeros((P, 2, HEADS), np.float32)
    for block in range(3):
        for part in range(2):
            at = 32 * block + HDIM + part * r
            ab[at:at + r, 0], ab[at:at + r, 1] = a["L0_attn_alpha"].T, a["L0_attn_beta"].T
    out["alpha_beta"] = ab
    out["mask_f"] = np.ascontiguousarray(a["mask_1x1xSxS2_fk1"].reshape(TT, P, CTX).transpose(1, 0, 2))
    out["w1"] = np.concatenate([rows_of(np.ascontiguousarray(qkv[:, 0:512])), rows_of(np.ascontiguousarray(qkv[:, 512:768])),
                                rows_of(np.ascontiguousarray(a["L0_attn_Wout"].T)), rows_of(a["L0_xattn_wq_w"]),
                                rows_of(a["L0_xattn_wv_w"]), rows_of(a["L0_xattn_wo_w"])], 1)
    experts = lambda n, w: np.concatenate([a[f"L0_ffn_shared_w{n}"], a[f"L0_ffn_routed_w{n}"]], 0)
    wide = lambda w: rows_of(np.ascontiguousarray(w.transpose(1, 0, 2).reshape(DIM, -1)))
    out["low"] = np.ascontiguousarray(np.stack(
        [np.concatenate([a[f"L1_attn_w{n}_lat"].T for n in "qkv"], 1),
         np.concatenate([a[f"L1_attn_w{n}_heads"] for n in "qkv"], 1)], 1))
    router = np.concatenate([a["L0_ffn_router_w"], np.zeros((DIM, ROUTER - EXPERTS), np.float32)], 1)
    out["w2"] = np.concatenate([wide(experts(1, 0)), wide(experts(3, 0)),
                                experts(2, 0).transpose(1, 0, 2).reshape(HID, -1), rows_of(router),
                                rows_of(a["L1_attn_w_proj"])], 1)
    ff = {n: a[f"L1_ffn_{n}"] for n in ("W1", "W2", "b1", "b2")}
    out["w3"] = np.concatenate([rows_of(np.ascontiguousarray(a["L1_xattn_Wq"].T)), rows_of(a["L1_xattn_Wk"]),
                                rows_of(a["L1_xattn_Wv"]), rows_of(a["L1_xattn_Wo"]), rows_of(ff["W1"]),
                                rows_of(ff["W2"])], 1)
    for name, key in (("cq_b", "bq"), ("ck_b", "bk"), ("cv_b", "bv")):
        out[name] = cols_of(a["L1_xattn_" + key])
    out["co_b"], out["f2_b"] = a["L1_xattn_bo"], ff["b2"]
    out["ff_c"] = np.concatenate([cols_of(a["L1_ffn_quantum_phases"]), cols_of(a["L1_ffn_quantum_weights_real"]),
                                  cols_of(a["L1_ffn_quantum_weights_imag"]), cols_of(ff["b1"])], 1)
    out["mask_i"] = a["mask_BxS2_ik0"].reshape(-1)
    out["proj_b"] = a["L1_attn_b_proj"]
    out["router_b"] = np.concatenate([a["L0_ffn_router_b"], np.zeros(P - EXPERTS, np.float32)]).reshape(P, 1)
    out["xq_b"], out["xk_b"] = cols_of(a["L0_xattn_wq_b"]), cols_of(a["L0_xattn_wk_b"])
    out["xv_b"], out["xo_b"] = a["L0_xattn_wv_b"], a["L0_xattn_wo_b"]
    return out


def kernel(**inputs):
    import concourse.bacc as bacc
    from concourse.bass_utils import run_bass_kernel_spmd

    nc = bacc.Bacc("TRN2", target_bir_lowering=False, num_devices=1)
    arrays = {"in_" + name: value for name, value in lay_out(inputs).items()}
    dram = {name[3:]: nc.dram_tensor(name, value.shape, mybir.dt.from_np(value.dtype), kind="ExternalInput").ap()
            for name, value in arrays.items()}
    out = nc.dram_tensor("out_dram", (BATCH, SEQ, DIM), F32, kind="ExternalOutput").ap()
    decoder(nc, dram, out)
    result = run_bass_kernel_spmd(nc, [arrays], core_ids=[0])
    return result.results[0]["out_dram"]
```
